# Optimizing a Trainium2 kernel written in Bass

```python
import numpy as np
import jax
import jax.numpy as jnp

def _softmax(x, axis=-1):
    return jax.nn.softmax(x, axis=axis)

def _gelu(x):
    return jax.nn.gelu(x, approximate=True)

def _silu(x):
    return jax.nn.silu(x)

def _sigmoid(x):
    return jax.nn.sigmoid(x)

def _layernorm(x, axis=-1, eps=1e-05):
    m = jnp.mean(x, axis=axis, keepdims=True)
    v = jnp.var(x, axis=axis, keepdims=True)
    return (x - m) / jnp.sqrt(v + eps)

def _scatter_add(tgt, idx, src, axis=0):
    return tgt.at[idx].add(src)

def _segment_sum(src, seg, n):
    return jax.ops.segment_sum(src, seg, n)
kernel_name = 'mk_pixart_resid_d4_seqx_r8_f18e18'

def setup_inputs(seed: int=0):
    np.random.seed(seed)
    _w = jnp.asarray

    def _rec_inputs():
        import jax
        import jax.numpy as jnp
        _rk = jax.random.key(seed)
        x = 2.818e-05 + 1 * jax.random.normal(jax.random.fold_in(_rk, 1), (4, 512, 128), jnp.float32)
        _lenS = 512 - jax.random.randint(jax.random.fold_in(_rk, 7), (4,), 0, max(1, 512 // 4) + 1, jnp.int32)
        _lenS2 = 77 - jax.random.randint(jax.random.fold_in(_rk, 8), (4,), 0, max(1, 77 // 4) + 1, jnp.int32)
        _ctx_1024P = jax.random.normal(jax.random.fold_in(_rk, 11), (4, 16, 128), jnp.float32)
        _ctx_1024c = jax.random.dirichlet(jax.random.fold_in(_rk, 511), 0.3 * jnp.ones((16,), jnp.float32), (4, 77))
        _ctx_1024t = jnp.einsum('bsk,bkd->bsd', _ctx_1024c, _ctx_1024P)
        _ctx_1024t = _ctx_1024t * jax.lax.rsqrt(jnp.mean(jnp.square(_ctx_1024t)) + 1e-12) * 0.953939
        ctx_1024 = -0.000391444 + 0.999954 * (_ctx_1024t + 0.3 * jax.random.normal(jax.random.fold_in(_rk, 611), (4, 77, 128), jnp.float32))
        condB_pt = jax.random.uniform(jax.random.fold_in(_rk, 13), (4,), jnp.float32, 0.0, 226.919)
        condB_tau = jax.random.uniform(jax.random.fold_in(_rk, 14), (4,), jnp.float32, 0.0, 1.23395)
        fside_BxS2_0 = -0.00205293 + 0.99739 * jax.random.normal(jax.random.fold_in(_rk, 15), (4, 77), jnp.float32)
        return (x, ctx_1024, condB_pt, condB_tau, fside_BxS2_0, _lenS2)
    x, ctx_1024, condB_pt, condB_tau, fside_BxS2_0, _lenS2 = _rec_inputs()

    def _L0_xcond_setup():
        import jax, jax.numpy as jnp
        import numpy as np
        N, L, H, Q = (64, 258, 128, 32)
        WINDOW = 16.0
        DEV_POW = 128.0
        key = jax.random.key(seed)
        k1, k2, k3, k4, k5, k6 = jax.random.split(key, 6)
        encoder_outputs = jax.random.normal(k1, (N, L, H), dtype=jnp.float32)
        decoder_h_t = jax.random.normal(k2, (N, Q, H), dtype=jnp.float32)
        src_len = jax.random.randint(k3, (N,), 32, L + 1).astype(jnp.int32)
        p_t = jax.random.uniform(k4, (N,), dtype=jnp.float32) * (src_len.astype(jnp.float32) - 1.0)
        W_a = jax.random.normal(k5, (H, H), dtype=jnp.float32) * (1.0 / np.sqrt(H))
        W_c = jax.random.normal(k6, (H, 2 * H), dtype=jnp.float32) * (1.0 / np.sqrt(2 * H))
        return {'encoder_outputs': encoder_outputs, 'decoder_h_t': decoder_h_t, 'src_len': src_len, 'p_t': p_t, 'W_a': W_a, 'W_c': W_c}
    _L0_xcond_all = _L0_xcond_setup()
    _L0_xcond_in = {k: v for k, v in _L0_xcond_all.items() if k in ('W_a', 'W_c')}
    del _L0_xcond_all

    def _L0_ffn_setup():
        import jax, jax.numpy as jnp
        import numpy as np
        DIM = 128
        INTER = 64
        E = 32
        TOPK = 4
        GROUPS = 8
        TOPK_GROUPS = 4
        SHARED_INTER = 2 * INTER
        ROUTE_SCALE = 1.0
        B, S = (8, 512)

        def _gate(xf, gw, gb):
            T = xf.shape[0]
            scores = jax.nn.softmax((xf @ gw + gb).astype(jnp.float32), axis=-1)
            original_scores = scores
            scores_g = scores.reshape(T, GROUPS, E // GROUPS)
            group_scores = jnp.sum(jax.lax.top_k(scores_g, 2)[0], axis=-1)
            gidx = jax.lax.top_k(group_scores, TOPK_GROUPS)[1]
            keep = jnp.zeros((T, GROUPS), bool).at[jnp.arange(T)[:, None], gidx].set(True)
            masked = jnp.where(keep[:, :, None], scores_g, -jnp.inf).reshape(T, E)
            indices = jax.lax.top_k(masked, TOPK)[1]
            weights = jnp.take_along_axis(original_scores, indices, axis=1) * ROUTE_SCALE
            return (weights.astype(xf.dtype), indices)
        key = jax.random.key(seed)
        ks = jax.random.split(key, 16)

        def xav(k, shape):
            fan_in, fan_out = (shape[-2], shape[-1])
            lim = np.sqrt(6.0 / (fan_in + fan_out))
            return jax.random.uniform(k, shape, jnp.float32, -lim, lim)
        return {'x': jax.random.normal(ks[0], (B, S, DIM), jnp.float32), 'gw': xav(ks[1], (DIM, E)), 'gb': jnp.zeros((E,), jnp.float32), 'w1': xav(ks[2], (E, DIM, INTER)), 'b1': jnp.zeros((E, INTER), jnp.float32), 'w3': xav(ks[3], (E, DIM, INTER)), 'b3': jnp.zeros((E, INTER), jnp.float32), 'w2': xav(ks[4], (E, INTER, DIM)), 'b2': jnp.zeros((E, DIM), jnp.float32), 'sw1': xav(ks[5], (DIM, SHARED_INTER)), 'sb1': jnp.zeros((SHARED_INTER,), jnp.float32), 'sw3': xav(ks[6], (DIM, SHARED_INTER)), 'sb3': jnp.zeros((SHARED_INTER,), jnp.float32), 'sw2': xav(ks[7], (SHARED_INTER, DIM)), 'sb2': jnp.zeros((DIM,), jnp.float32)}
    _L0_ffn_all = _L0_ffn_setup()
    _L0_ffn_in = {k: v for k, v in _L0_ffn_all.items() if k in ('gw', 'gb', 'w1', 'b1', 'w3', 'b3', 'w2', 'b2', 'sw1', 'sb1', 'sw3', 'sb3', 'sw2', 'sb2')}
    del _L0_ffn_all

    def _L1_xcond_setup():
        import jax, jax.numpy as jnp
        import numpy as np
        B, S, D, H = (2, 256, 128, 16)
        DK = D // H

        def _split_heads(x):
            b, s, _ = x.shape
            return x.reshape(b, s, H, DK).transpose(0, 2, 1, 3)
        key = jax.random.key(seed)
        ks = jax.random.split(key, 14)
        inp = {'query': jax.random.normal(ks[0], (B, S, D), jnp.float32), 'key': jax.random.normal(ks[1], (B, S, D), jnp.float32), 'value': jax.random.normal(ks[2], (B, S, D), jnp.float32), 'tau': jax.random.uniform(ks[3], (B, 1), jnp.float32, 0.5, 1.5), 'delta': jax.random.normal(ks[4], (B, S), jnp.float32)}
        sc = 1.0 / np.sqrt(D)
        for i, name in enumerate(['q', 'k', 'v', 'o']):
            inp[f'W{name}'] = jax.random.normal(ks[5 + 2 * i], (D, D), jnp.float32) * sc
            inp[f'b{name}'] = jax.random.normal(ks[6 + 2 * i], (D,), jnp.float32) * 0.01
        return inp
    _L1_xcond_all = _L1_xcond_setup()
    _L1_xcond_in = {k: v for k, v in _L1_xcond_all.items() if k in ('Wq', 'bq', 'Wk', 'bk', 'Wv', 'bv', 'Wo', 'bo')}
    del _L1_xcond_all

    def _L1_ffn_setup():
        import jax, jax.numpy as jnp
        import numpy as np
        HID, FFN, E, K = (128, 512, 8, 2)
        CAP_FACTOR = 1.25
        key = jax.random.key(seed)
        k1, k2, k3, k4 = jax.random.split(key, 4)
        B, T = (4, 256)
        x = jax.random.normal(k1, (B, T, HID), dtype=jnp.float32)
        router_w = jax.random.normal(k2, (E, HID), dtype=jnp.float32) * 0.02
        w1 = jax.random.normal(k3, (E, HID, FFN), dtype=jnp.float32) * 0.02
        w2 = jax.random.normal(k4, (E, FFN, HID), dtype=jnp.float32) * 0.02
        return {'x': x, 'router_w': router_w, 'w1': w1, 'w2': w2}
    _L1_ffn_all = _L1_ffn_setup()
    _L1_ffn_in = {k: v for k, v in _L1_ffn_all.items() if k in ('router_w', 'w1', 'w2')}
    del _L1_ffn_all

    def _L2_xcond_setup():
        import jax, jax.numpy as jnp
        import numpy as np
        D_MODEL = 128
        N_HEADS = 16
        key = jax.random.key(seed)
        ks = jax.random.split(key, 16)
        B, L, S, D = (4, 256, 256, D_MODEL)
        inp = {'q': jax.random.normal(ks[0], (B, L, D), jnp.float32), 'k': jax.random.normal(ks[1], (B, S, D), jnp.float32), 'v': jax.random.normal(ks[2], (B, S, D), jnp.float32), 'tau': jax.random.uniform(ks[3], (B, 1), jnp.float32, 0.5, 1.5), 'delta': jax.random.normal(ks[4], (B, S), jnp.float32)}
        s = 1.0 / np.sqrt(D)
        inp['Wq'] = jax.random.normal(ks[5], (D, D), jnp.float32) * s
        inp['bq'] = jnp.zeros((D,), jnp.float32)
        inp['Wk'] = jax.random.normal(ks[6], (D, D), jnp.float32) * s
        inp['bk'] = jnp.zeros((D,), jnp.float32)
        inp['Wv'] = jax.random.normal(ks[7], (D, D), jnp.float32) * s
        inp['bv'] = jnp.zeros((D,), jnp.float32)
        inp['Wo'] = jax.random.normal(ks[8], (D, D), jnp.float32) * s
        inp['bo'] = jnp.zeros((D,), jnp.float32)
        return inp
    _L2_xcond_all = _L2_xcond_setup()
    _L2_xcond_in = {k: v for k, v in _L2_xcond_all.items() if k in ('Wq', 'bq', 'Wk', 'bk', 'Wv', 'bv', 'Wo', 'bo')}
    del _L2_xcond_all

    def _L2_ffn_setup():
        import jax, jax.numpy as jnp
        import numpy as np
        DM, NE, ES, ESZ = (128, 16, 4, 64)
        BATCH, SEQ = (8, 256)
        key = jax.random.key(seed)
        k = jax.random.split(key, 5)
        scale = 0.02
        return {'x': jax.random.normal(k[0], (BATCH, SEQ, DM), dtype=jnp.float32), 'controller': jax.random.normal(k[1], (DM, NE, ES), dtype=jnp.float32) * scale, 'f1': jax.random.normal(k[2], (DM, NE, ES, ESZ), dtype=jnp.float32) * scale, 'f2': jax.random.normal(k[3], (NE, ES, ESZ, DM), dtype=jnp.float32) * scale, 'bias': jax.random.normal(k[4], (NE, ES, ESZ), dtype=jnp.float32) * scale}
    _L2_ffn_all = _L2_ffn_setup()
    _L2_ffn_in = {k: v for k, v in _L2_ffn_all.items() if k in ('controller', 'f1', 'f2', 'bias')}
    del _L2_ffn_all

    def _L3_xcond_setup():
        import jax, jax.numpy as jnp
        import numpy as np
        N, L, H, Q = (64, 258, 128, 32)
        WINDOW = 16.0
        DEV_POW = 128.0
        key = jax.random.key(seed)
        k1, k2, k3, k4, k5, k6 = jax.random.split(key, 6)
        encoder_outputs = jax.random.normal(k1, (N, L, H), dtype=jnp.float32)
        decoder_h_t = jax.random.normal(k2, (N, Q, H), dtype=jnp.float32)
        src_len = jax.random.randint(k3, (N,), 32, L + 1).astype(jnp.int32)
        p_t = jax.random.uniform(k4, (N,), dtype=jnp.float32) * (src_len.astype(jnp.float32) - 1.0)
        W_a = jax.random.normal(k5, (H, H), dtype=jnp.float32) * (1.0 / np.sqrt(H))
        W_c = jax.random.normal(k6, (H, 2 * H), dtype=jnp.float32) * (1.0 / np.sqrt(2 * H))
        return {'encoder_outputs': encoder_outputs, 'decoder_h_t': decoder_h_t, 'src_len': src_len, 'p_t': p_t, 'W_a': W_a, 'W_c': W_c}
    _L3_xcond_all = _L3_xcond_setup()
    _L3_xcond_in = {k: v for k, v in _L3_xcond_all.items() if k in ('W_a', 'W_c')}
    del _L3_xcond_all

    def _L3_ffn_setup():
        import jax, jax.numpy as jnp
        import numpy as np
        B, S, D, F, E = (4, 256, 128, 512, 8)
        LN_EPS = 1e-05
        key = jax.random.key(seed)
        ks = jax.random.split(key, 6)
        sc = 0.02
        return {'x': jax.random.normal(ks[0], (B, S, D), dtype=jnp.float32), 'Wr': jax.random.normal(ks[1], (D, E), dtype=jnp.float32) * sc, 'br': jnp.zeros((E,), jnp.float32), 'ln_g': jnp.ones((D,), jnp.float32), 'ln_b': jnp.zeros((D,), jnp.float32), 'W1': jax.random.normal(ks[2], (E, D, F), dtype=jnp.float32) * sc, 'b1': jnp.zeros((E, F), jnp.float32), 'W2': jax.random.normal(ks[3], (E, F, D), dtype=jnp.float32) * sc, 'b2': jnp.zeros((E, D), jnp.float32)}
    _L3_ffn_all = _L3_ffn_setup()
    _L3_ffn_in = {k: v for k, v in _L3_ffn_all.items() if k in ('Wr', 'br', 'ln_g', 'ln_b', 'W1', 'b1', 'W2', 'b2')}
    del _L3_ffn_all
    return {'x': x, 'ctx_1024': ctx_1024, 'condB_pt': condB_pt, 'condB_tau': condB_tau, 'fside_BxS2_0': fside_BxS2_0, '_lenS2': _lenS2, 'L0_xcond_W_a': _L0_xcond_in['W_a'], 'L0_xcond_W_c': _L0_xcond_in['W_c'], 'L0_ffn_gw': _L0_ffn_in['gw'], 'L0_ffn_gb': _L0_ffn_in['gb'], 'L0_ffn_w1': _L0_ffn_in['w1'], 'L0_ffn_b1': _L0_ffn_in['b1'], 'L0_ffn_w3': _L0_ffn_in['w3'], 'L0_ffn_b3': _L0_ffn_in['b3'], 'L0_ffn_w2': _L0_ffn_in['w2'], 'L0_ffn_b2': _L0_ffn_in['b2'], 'L0_ffn_sw1': _L0_ffn_in['sw1'], 'L0_ffn_sb1': _L0_ffn_in['sb1'], 'L0_ffn_sw3': _L0_ffn_in['sw3'], 'L0_ffn_sb3': _L0_ffn_in['sb3'], 'L0_ffn_sw2': _L0_ffn_in['sw2'], 'L0_ffn_sb2': _L0_ffn_in['sb2'], 'L1_xcond_Wq': _L1_xcond_in['Wq'], 'L1_xcond_bq': _L1_xcond_in['bq'], 'L1_xcond_Wk': _L1_xcond_in['Wk'], 'L1_xcond_bk': _L1_xcond_in['bk'], 'L1_xcond_Wv': _L1_xcond_in['Wv'], 'L1_xcond_bv': _L1_xcond_in['bv'], 'L1_xcond_Wo': _L1_xcond_in['Wo'], 'L1_xcond_bo': _L1_xcond_in['bo'], 'L1_ffn_router_w': _L1_ffn_in['router_w'], 'L1_ffn_w1': _L1_ffn_in['w1'], 'L1_ffn_w2': _L1_ffn_in['w2'], 'L2_xcond_Wq': _L2_xcond_in['Wq'], 'L2_xcond_bq': _L2_xcond_in['bq'], 'L2_xcond_Wk': _L2_xcond_in['Wk'], 'L2_xcond_bk': _L2_xcond_in['bk'], 'L2_xcond_Wv': _L2_xcond_in['Wv'], 'L2_xcond_bv': _L2_xcond_in['bv'], 'L2_xcond_Wo': _L2_xcond_in['Wo'], 'L2_xcond_bo': _L2_xcond_in['bo'], 'L2_ffn_controller': _L2_ffn_in['controller'], 'L2_ffn_f1': _L2_ffn_in['f1'], 'L2_ffn_f2': _L2_ffn_in['f2'], 'L2_ffn_bias': _L2_ffn_in['bias'], 'L3_xcond_W_a': _L3_xcond_in['W_a'], 'L3_xcond_W_c': _L3_xcond_in['W_c'], 'L3_ffn_Wr': _L3_ffn_in['Wr'], 'L3_ffn_br': _L3_ffn_in['br'], 'L3_ffn_ln_g': _L3_ffn_in['ln_g'], 'L3_ffn_ln_b': _L3_ffn_in['ln_b'], 'L3_ffn_W1': _L3_ffn_in['W1'], 'L3_ffn_b1': _L3_ffn_in['b1'], 'L3_ffn_W2': _L3_ffn_in['W2'], 'L3_ffn_b2': _L3_ffn_in['b2']}

def reference(x, ctx_1024, condB_pt, condB_tau, fside_BxS2_0, _lenS2, L0_xcond_W_a, L0_xcond_W_c, L0_ffn_gw, L0_ffn_gb, L0_ffn_w1, L0_ffn_b1, L0_ffn_w3, L0_ffn_b3, L0_ffn_w2, L0_ffn_b2, L0_ffn_sw1, L0_ffn_sb1, L0_ffn_sw3, L0_ffn_sb3, L0_ffn_sw2, L0_ffn_sb2, L1_xcond_Wq, L1_xcond_bq, L1_xcond_Wk, L1_xcond_bk, L1_xcond_Wv, L1_xcond_bv, L1_xcond_Wo, L1_xcond_bo, L1_ffn_router_w, L1_ffn_w1, L1_ffn_w2, L2_xcond_Wq, L2_xcond_bq, L2_xcond_Wk, L2_xcond_bk, L2_xcond_Wv, L2_xcond_bv, L2_xcond_Wo, L2_xcond_bo, L2_ffn_controller, L2_ffn_f1, L2_ffn_f2, L2_ffn_bias, L3_xcond_W_a, L3_xcond_W_c, L3_ffn_Wr, L3_ffn_br, L3_ffn_ln_g, L3_ffn_ln_b, L3_ffn_W1, L3_ffn_b1, L3_ffn_W2, L3_ffn_b2):
    import jax
    import jax.numpy as jnp

    def _L0_xcond_ref(encoder_outputs, decoder_h_t, src_len, p_t, W_a, W_c):
        import jax, jax.numpy as jnp
        import numpy as np
        N, L, H, Q = (64, 258, 128, 32)
        WINDOW = 16.0
        DEV_POW = 128.0
        n, l, h = encoder_outputs.shape
        idx = jnp.arange(l, dtype=jnp.float32)
        src_end = src_len.astype(jnp.float32)
        attn_start = jnp.maximum(p_t - WINDOW, 0.0)
        attn_end = jnp.minimum(p_t + WINDOW, src_end)
        mask = (idx[None, :] < attn_start[:, None]) | (idx[None, :] > attn_end[:, None])
        score = jnp.einsum('nqh,hk,nlk->nql', decoder_h_t, W_a, encoder_outputs)
        score = jnp.where(mask[:, None, :], -1000000000.0, score)
        align = jax.nn.softmax(score, axis=2)
        gauss = jnp.exp(-(idx[None, :] - p_t[:, None]) ** 2 / DEV_POW)
        align = align * gauss[:, None, :]
        context = jnp.einsum('nql,nlh->nqh', align, encoder_outputs)
        cat = jnp.concatenate([context, decoder_h_t], axis=2)
        return jnp.tanh(cat @ W_c.T)

    def _L0_ffn_ref(x, gw, gb, w1, b1, w3, b3, w2, b2, sw1, sb1, sw3, sb3, sw2, sb2):
        import jax, jax.numpy as jnp
        import numpy as np
        DIM = 128
        INTER = 64
        E = 32
        TOPK = 4
        GROUPS = 8
        TOPK_GROUPS = 4
        SHARED_INTER = 2 * INTER
        ROUTE_SCALE = 1.0
        B, S = (8, 512)

        def _gate(xf, gw, gb):
            T = xf.shape[0]
            scores = jax.nn.softmax((xf @ gw + gb).astype(jnp.float32), axis=-1)
            original_scores = scores
            scores_g = scores.reshape(T, GROUPS, E // GROUPS)
            group_scores = jnp.sum(jax.lax.top_k(scores_g, 2)[0], axis=-1)
            gidx = jax.lax.top_k(group_scores, TOPK_GROUPS)[1]
            keep = jnp.zeros((T, GROUPS), bool).at[jnp.arange(T)[:, None], gidx].set(True)
            masked = jnp.where(keep[:, :, None], scores_g, -jnp.inf).reshape(T, E)
            indices = jax.lax.top_k(masked, TOPK)[1]
            weights = jnp.take_along_axis(original_scores, indices, axis=1) * ROUTE_SCALE
            return (weights.astype(xf.dtype), indices)
        shape = x.shape
        xf = x.reshape(-1, DIM)
        T = xf.shape[0]
        weights, indices = _gate(xf, gw, gb)
        cw = jnp.zeros((T, E), xf.dtype).at[jnp.arange(T)[:, None], indices].add(weights)

        def body(y, p):
            w1e, b1e, w3e, b3e, w2e, b2e, we = p
            h = jax.nn.silu(xf @ w1e + b1e) * (xf @ w3e + b3e)
            return (y + we[:, None] * (h @ w2e + b2e), None)
        y0 = jnp.zeros_like(xf)
        y, _ = jax.lax.scan(body, y0, (w1, b1, w3, b3, w2, b2, cw.T))
        z = jax.nn.silu(xf @ sw1 + sb1) * (xf @ sw3 + sb3) @ sw2 + sb2
        return (y + z).reshape(shape)

    def _L1_xcond_ref(query, key, value, tau, delta, Wq, bq, Wk, bk, Wv, bv, Wo, bo):
        import jax, jax.numpy as jnp
        import numpy as np
        B, S, D, H = (2, 256, 128, 16)
        DK = D // H

        def _split_heads(x):
            b, s, _ = x.shape
            return x.reshape(b, s, H, DK).transpose(0, 2, 1, 3)
        q = _split_heads(query @ Wq.T + bq)
        k = _split_heads(key @ Wk.T + bk)
        v = _split_heads(value @ Wv.T + bv)
        scores = jnp.einsum('bhqd,bhkd->bhqk', q, k)
        scores = scores * tau[:, :, None, None] + delta[:, None, None, :]
        scores = scores / jnp.sqrt(jnp.asarray(DK, scores.dtype))
        p_attn = jax.nn.softmax(scores, axis=-1)
        x = jnp.einsum('bhqk,bhkd->bhqd', p_attn, v)
        x = x.transpose(0, 2, 1, 3).reshape(query.shape[0], -1, H * DK)
        return x @ Wo.T + bo

    def _L1_ffn_ref(x, router_w, w1, w2):
        import jax, jax.numpy as jnp
        import numpy as np
        HID, FFN, E, K = (128, 512, 8, 2)
        CAP_FACTOR = 1.25
        B, T, H = x.shape
        N = B * T
        x_flat = x.reshape(N, H)
        C = max(1, int(CAP_FACTOR * N / E * K))
        logits = x_flat @ router_w.T
        probs = jax.nn.softmax(logits, axis=-1)
        top_v, top_i = jax.lax.top_k(probs, K)
        top_v = top_v / jnp.sum(top_v, axis=-1, keepdims=True)
        out = jnp.zeros_like(x_flat)
        for k in range(K):
            eid = top_i[:, k]
            gate = top_v[:, k]
            onehot = jax.nn.one_hot(eid, E, dtype=jnp.int32)
            pos = jnp.take_along_axis(jnp.cumsum(onehot, axis=0), eid[:, None], axis=1)[:, 0] - 1
            keep = pos < C
            slot = jnp.where(keep, eid * C + pos, E * C)
            buf = jnp.zeros((E * C + 1, H), dtype=x.dtype).at[slot].add(x_flat * keep[:, None].astype(x.dtype))
            expert_in = buf[:E * C].reshape(E, C, H)
            h = jax.nn.gelu(jnp.einsum('ech,ehf->ecf', expert_in, w1), approximate=False)
            y = jnp.einsum('ecf,efh->ech', h, w2)
            tok = y.reshape(E * C, H)[jnp.minimum(slot, E * C - 1)]
            out = out + tok * (gate * keep.astype(x.dtype))[:, None]
        return out.reshape(B, T, H)

    def _L2_xcond_ref(q, k, v, tau, delta, Wq, bq, Wk, bk, Wv, bv, Wo, bo):
        import jax, jax.numpy as jnp
        import numpy as np
        D_MODEL = 128
        N_HEADS = 16
        B, L, D = q.shape
        S = k.shape[1]
        H = N_HEADS
        E = D // H
        qh = (q @ Wq.T + bq).reshape(B, L, H, E)
        kh = (k @ Wk.T + bk).reshape(B, S, H, E)
        vh = (v @ Wv.T + bv).reshape(B, S, H, E)
        scale = 1.0 / np.sqrt(E).astype(np.float32)
        scores = jnp.einsum('blhe,bshe->bhls', qh, kh)
        scores = scores * tau[:, None, None, :] + delta[:, None, None, :]
        a = jax.nn.softmax(scale * scores, axis=-1)
        out = jnp.einsum('bhls,bshd->blhd', a, vh).reshape(B, L, D)
        return out @ Wo.T + bo

    def _L2_ffn_ref(x, controller, f1, f2, bias):
        import jax, jax.numpy as jnp
        import numpy as np
        DM, NE, ES, ESZ = (128, 16, 4, 64)
        BATCH, SEQ = (8, 256)
        ne = controller.shape[1]
        d = x.shape[-1]
        grouped = x.reshape(x.shape[:-2] + (-1, ne, d))
        logits = jnp.einsum('...btd,des->...btes', grouped, controller)
        tie = jnp.linspace(0.0, 1e-06, ne, dtype=logits.dtype).reshape(ne, 1, 1)
        logits = logits + tie
        perm = (logits == jnp.max(logits, axis=-3, keepdims=True)).astype(x.dtype)
        sel = jnp.einsum('...btd,...btes->...besd', grouped, perm)
        inner = jax.nn.relu(jnp.einsum('...besd,desf->...besf', sel, f1) + bias)
        inter = jnp.einsum('...besf,esfd->...besd', inner, f2)
        out = jnp.einsum('...besd,...btes->...btd', inter, perm)
        return out.reshape(x.shape)

    def _L3_xcond_ref(encoder_outputs, decoder_h_t, src_len, p_t, W_a, W_c):
        import jax, jax.numpy as jnp
        import numpy as np
        N, L, H, Q = (64, 258, 128, 32)
        WINDOW = 16.0
        DEV_POW = 128.0
        n, l, h = encoder_outputs.shape
        idx = jnp.arange(l, dtype=jnp.float32)
        src_end = src_len.astype(jnp.float32)
        attn_start = jnp.maximum(p_t - WINDOW, 0.0)
        attn_end = jnp.minimum(p_t + WINDOW, src_end)
        mask = (idx[None, :] < attn_start[:, None]) | (idx[None, :] > attn_end[:, None])
        score = jnp.einsum('nqh,hk,nlk->nql', decoder_h_t, W_a, encoder_outputs)
        score = jnp.where(mask[:, None, :], -1000000000.0, score)
        align = jax.nn.softmax(score, axis=2)
        gauss = jnp.exp(-(idx[None, :] - p_t[:, None]) ** 2 / DEV_POW)
        align = align * gauss[:, None, :]
        context = jnp.einsum('nql,nlh->nqh', align, encoder_outputs)
        cat = jnp.concatenate([context, decoder_h_t], axis=2)
        return jnp.tanh(cat @ W_c.T)

    def _L3_ffn_ref(x, Wr, br, ln_g, ln_b, W1, b1, W2, b2):
        import jax, jax.numpy as jnp
        import numpy as np
        B, S, D, F, E = (4, 256, 128, 512, 8)
        LN_EPS = 1e-05
        tokens_shape = x.shape[:-1]
        xt = x.reshape(-1, x.shape[-1])
        router_logits = xt @ Wr + br
        router_probs = jax.nn.softmax(router_logits, axis=-1)
        gates = jnp.max(router_probs, axis=-1, keepdims=True)
        idx = jnp.argmax(router_probs, axis=-1)
        onehot = jax.nn.one_hot(idx, E, dtype=xt.dtype)
        mu = jnp.mean(xt, axis=-1, keepdims=True)
        var = jnp.mean(jnp.square(xt - mu), axis=-1, keepdims=True)
        xn = (xt - mu) * jax.lax.rsqrt(var + LN_EPS) * ln_g + ln_b
        h = jnp.einsum('te,td,edf->tf', onehot, xn, W1) + b1[idx]
        h = jax.nn.relu(h)
        y = jnp.einsum('te,tf,efd->td', onehot, h, W2) + b2[idx]
        y = y * gates
        return y.reshape(tokens_shape + (y.shape[-1],))
    x = x + _L0_xcond_ref(ctx_1024, _layernorm(x, axis=-1), _lenS2, condB_pt, L0_xcond_W_a, L0_xcond_W_c)
    x = x + _L0_ffn_ref(_layernorm(x, axis=-1), L0_ffn_gw, L0_ffn_gb, L0_ffn_w1, L0_ffn_b1, L0_ffn_w3, L0_ffn_b3, L0_ffn_w2, L0_ffn_b2, L0_ffn_sw1, L0_ffn_sb1, L0_ffn_sw3, L0_ffn_sb3, L0_ffn_sw2, L0_ffn_sb2)
    x = x + _L1_xcond_ref(_layernorm(x, axis=-1), ctx_1024, ctx_1024, condB_tau[:, None], fside_BxS2_0, L1_xcond_Wq, L1_xcond_bq, L1_xcond_Wk, L1_xcond_bk, L1_xcond_Wv, L1_xcond_bv, L1_xcond_Wo, L1_xcond_bo)
    x = x + _L1_ffn_ref(_layernorm(x, axis=-1), L1_ffn_router_w, L1_ffn_w1, L1_ffn_w2)
    x = x + _L2_xcond_ref(_layernorm(x, axis=-1), ctx_1024, ctx_1024, condB_tau[:, None], fside_BxS2_0, L2_xcond_Wq, L2_xcond_bq, L2_xcond_Wk, L2_xcond_bk, L2_xcond_Wv, L2_xcond_bv, L2_xcond_Wo, L2_xcond_bo)
    x = x + _L2_ffn_ref(_layernorm(x, axis=-1), L2_ffn_controller, L2_ffn_f1, L2_ffn_f2, L2_ffn_bias)
    x = x + _L3_xcond_ref(ctx_1024, _layernorm(x, axis=-1), _lenS2, condB_pt, L3_xcond_W_a, L3_xcond_W_c)
    x = x + _L3_ffn_ref(_layernorm(x, axis=-1), L3_ffn_Wr, L3_ffn_br, L3_ffn_ln_g, L3_ffn_ln_b, L3_ffn_W1, L3_ffn_b1, L3_ffn_W2, L3_ffn_b2)
    return x

_drawn_inputs = setup_inputs


def setup_inputs(seed=0):
    import zlib

    import numpy as np

    out = dict(_drawn_inputs(seed))
    spreads = {'L0_ffn_gb': (0.0, 0.336),
     'L0_ffn_b1': (0.0, 0.609),
     'L0_ffn_b3': (0.0, 0.617),
     'L0_ffn_b2': (0.0, 0.381),
     'L0_ffn_sb1': (0.0, 0.1),
     'L0_ffn_sb3': (0.0, 0.1),
     'L0_ffn_sb2': (0.0, 0.1),
     'L2_xcond_bq': (0.0, 0.8),
     'L2_xcond_bk': (0.0, 0.8),
     'L2_xcond_bv': (0.0, 0.1),
     'L2_xcond_bo': (0.0, 0.1),
     'L3_ffn_br': (0.0, 0.8),
     'L3_ffn_ln_g': (1.0, 0.6),
     'L3_ffn_ln_b': (0.0, 0.8),
     'L3_ffn_b1': (0.0, 0.8),
     'L3_ffn_b2': (0.0, 0.746)}
    factors = {'L1_xcond_bq': 8.0,
     'L1_xcond_bk': 8.0,
     'L1_xcond_bv': 7.209,
     'L1_xcond_bo': 8.0,
     'L2_ffn_bias': 8.0,
     'L3_ffn_Wr': 4.425,
     'L3_ffn_W1': 8.0,
     'L3_ffn_W2': 6.536}
    for name, (base, spread) in spreads.items():
        noise = np.random.default_rng([zlib.crc32(name.encode()), seed]).standard_normal(out[name].shape)
        drawn = base * np.exp(spread * noise) if base else spread * noise
        out[name] = jnp.asarray(drawn.astype(out[name].dtype))
    for name, factor in factors.items():
        out[name] = (out[name] * factor).astype(out[name].dtype)
    return out
```

```python
import numpy as np
from contextlib import ExitStack

import concourse.bass as bass
from concourse import mybir

BATCH, SEQ, D, KEYS = 4, 512, 128, 77
P = 128
TPC = SEQ // P
NT = BATCH * TPC
E0, F0 = 32, 64
PAIRS = E0 // 2
E1, F1 = 8, 512
FC = F1 // P
HEADS, DK = 16, 8
ES, FS, GRP = 64, 64, 16
GPT = P // GRP
NG = NT * GPT
CAPACITY = max(1, int(1.25 * BATCH * SEQ / E1 * 2))
WINDOW, DEV_POW = 16.0, 128.0
BK = BATCH * KEYS

SMALL = [("ctxT", P, BK), ("pt", P, BATCH), ("tau", P, BATCH), ("delta", 1, BK)]
for _l in (0, 3):
    SMALL += [(f"waT{_l}", P, P), (f"wcT{_l}", P, 2 * P)]
for _l in (1, 2):
    SMALL += [(f"w{_n}T{_l}", P, P) for _n in "qkvo"]
    SMALL += [(f"b{_n}{_l}", P, 1) for _n in "qk"] + [(f"b{_n}{_l}", 1, P) for _n in "vo"]
SMALL += [("gw", P, E0), ("gb", 1, E0), ("b1_0", P, PAIRS), ("b3_0", P, PAIRS), ("b2_0", E0, P),
          ("sw1", P, P), ("sw3", P, P), ("sw2", P, P), ("sb1", P, 1), ("sb3", P, 1), ("sb2", P, 1),
          ("rwT", P, E1), ("ctrl", P, 2 * ES), ("bias2", P, ES // 2), ("wr", P, E1), ("br", 1, E1),
          ("b1_3", P, E1 * FC), ("b2_3", E1, P), ("lng", P, 1), ("lnb", P, 1)]
OFFSET, _at = {}, 0
for _n, _r, _c in SMALL:
    OFFSET[_n] = (_at, _r, _c)
    _at += _c
SMALL_COLS = _at

WINDOW_ATT, GATED, HEADS_ATT, TOPK, CHOICE = range(5)
LAYERS = [(WINDOW_ATT, 0), (GATED, 0), (HEADS_ATT, 1), (TOPK, 1), (HEADS_ATT, 2), (CHOICE, 2),
          (WINDOW_ATT, 3), (TOPK, 3)]
HEAD_BANKS = [(0, 6), (6, 11), (11, 16)]


def build(nc, x_in, small_in, lens_in, w13_in, w2_in, l1w1_in, l1w2_in, f1_in, f2_in, l3w1_in,
          l3w2_in, out, n_layers=len(LAYERS)):
    f32, bf16, i32 = mybir.dt.float32, mybir.dt.bfloat16, mybir.dt.int32
    ALU, ACT, AX = mybir.AluOpType, mybir.ActivationFunctionType, mybir.AxisListType.X
    layers = LAYERS[:n_layers]
    ctx = ExitStack()
    with ctx:
        def sb(name, shape, dt=f32):
            return ctx.enter_context(nc.sbuf_tensor(name, shape, dt))

        sems = {}

        def sem(name):
            if name not in sems:
                sems[name] = ctx.enter_context(nc.semaphore(name))
            return sems[name]

        X = sb("X", [P, NT, D])
        XN = sb("XN", [P, 2, TPC, D])
        XNT = sb("XNT", [P, NT * P])
        SM = sb("SM", [P, SMALL_COLS])
        SLOT = [sb(f"SLOT{i}", [P, 4096]) for i in range(4)]
        ident = sb("ident", [P, P])
        lens_i = sb("lens_i", [P, BATCH], i32)

        def small(name):
            at, r, c = OFFSET[name]
            return SM[0:r, at:at + c]

        ones_row = sb("ones_row", [1, P])
        idx_i = sb("idx_i", [P, KEYS], i32)
        idx_f = sb("idx_f", [P, KEYS])
        pidx_i = sb("pidx_i", [P, 1], i32)
        pidx_f = sb("pidx_f", [P, 1])
        lens_f = sb("lens_f", [P, BATCH])
        lo_hi = sb("lo_hi", [P, 2, BATCH])
        keep = sb("keep", [P, BATCH, KEYS])
        neg = sb("neg", [P, BATCH, KEYS])
        gauss = sb("gauss", [P, BATCH])
        tau_s = sb("tau_s", [P, BATCH])
        headmask = sb("headmask", [P, HEADS])
        pairsel = sb("pairsel", [96, PAIRS, P], bf16)
        ones96 = sb("ones96", [96, P], bf16)
        delta3 = sb("delta3", [96, BK], bf16)
        dtmp = sb("dtmp", [1, 2, BK])
        dtb = sb("dtb", [1, BK], bf16)
        tri = sb("tri", [P, P], bf16)
        ones_b = sb("ones_b", [P, P], bf16)
        desc = sb("desc", [P, E1])
        desc_i = sb("desc_i", [P, E1], i32)
        tie_i = sb("tie_i", [P, GRP], i32)
        tie = sb("tie", [P, GRP])
        gmask = sb("gmask", [P, GPT])
        parity = sb("parity", [P, 2, GRP])
        neghalf = sb("neghalf", [P, TPC])

        stats = sb("stats", [P, TPC, 6])
        mv = sb("mv", [P, TPC, 2])
        veps = sb("veps", [P, 2, TPC])
        rstd = sb("rstd", [P, 2, TPC])
        mx = sb("mx", [P, HEADS])
        red = sb("red", [P, HEADS])

        Mk = {l: sb(f"Mk{l}", [P, BK]) for l in (0, 3)}
        Vw = {l: sb(f"Vw{l}", [KEYS, BATCH, P]) for l in (0, 3)}
        KT = {l: sb(f"KT{l}", [P, BK]) for l in (1, 2)}
        Vc = {l: sb(f"Vc{l}", [KEYS, BATCH, P]) for l in (1, 2)}

        sc = sb("sc", [P, 2, TPC, KEYS])
        eT = sb("eT", [KEYS, 2, SEQ])
        th = sb("th", [P, SEQ])
        red32 = sb("red32", [P, SEQ // GRP])
        SHARE = sb("SHARE", [P, 4352])
        S1 = SHARE[:, 0:1024].rearrange("p (a n) -> p a n", a=2)
        H1 = SHARE[:, 1024:2048].rearrange("p (a n) -> p a n", a=2)
        T1 = SHARE[:, 2048:2560]
        outT = SHARE[:, 2560:3072]
        cwT = SHARE[0:E0, 3072:4096].rearrange("p (a n) -> p a n", a=2)
        HT = SHARE[:, 0:4096].rearrange("p (a f n) -> p a f n", a=2, f=FC)
        cw3 = sb("cw3", [96, 2, SEQ], bf16)
        cwm = sb("cwm", [E0, SEQ], bf16)
        s0 = sb("s0", [P, TPC, E0])
        pr = sb("pr", [P, TPC, 8, 6])
        gs = sb("gs", [P, TPC, 12])
        gk = sb("gk", [P, TPC, 12])
        pen = sb("pen", [P, TPC, 8])
        me = sb("me", [P, TPC, 36])
        mk = sb("mk", [P, TPC, 36])
        v8 = sb("v8", [P, TPC, 8])
        r8 = sb("r8", [P, TPC, 8])
        cw = sb("cw", [P, 2, TPC, E0])
        pb8 = sb("pb8", [P, TPC, E1])
        t8 = sb("t8", [P, TPC, E1])
        oh = sb("oh", [P, 2, TPC, E1])
        ohb = sb("ohb", [P, TPC, 2, E1], bf16)
        tv = sb("tv", [P, 3, TPC])
        gk8 = sb("gk8", [P, TPC, 2, E1])
        pos = sb("pos", [P, TPC, 2 * E1])
        carry = sb("carry", [P, 2 * E1])
        cwd = sb("cwd", [P, 2, TPC, E1])
        U = sb("U", [P, 11840])
        cwr = U[0:E0, 11328:11840]
        kbd = U[:, 0:2464].rearrange("p (a h k) -> p a h k", a=2, h=HEADS)
        vpad = U[0:KEYS, 2464:3488].rearrange("p (a h k) -> p a h k", a=2, h=HEADS)
        PR = U[:, 3488:5952].rearrange("p (a h k) -> p a h k", a=2, h=HEADS)
        PT = U[0:KEYS, 5952:10048].rearrange("p (a h k) -> p a h k", a=2, h=HEADS)
        OTt = U[:, 10048:10560].rearrange("p (g q) -> p g q", g=4)
        On = U[:, 10560:10688]
        OT = U[:, 10688:10816]
        qT = U[:, 10816:11840].rearrange("p (a q) -> p a q", a=2)
        SELT = U[:, 0:8192].rearrange("p (g e) -> p g e", e=ES)
        LGT = U[:, 8192:8704]
        PERM = U[:, 8704:9216]
        BD = U[:, 9216:10240].rearrange("p (a g e) -> p a g e", a=2, e=ES)
        INN = U[:, 10240:11264].rearrange("p (a i g) -> p a i g", a=2, i=4)
        INTER = HT
        xn2 = U[:, 0:512].rearrange("p (t n) -> p t n", t=TPC)
        XNT2 = U[:, 512:1536].rearrange("p (a n) -> p a n", a=2)
        cwdT = U[0:E1, 1536:2560].rearrange("p (a n) -> p a n", a=2)

        PS = [ctx.enter_context(nc.psum_tensor(f"bank{i}", [P, 512], f32)) for i in range(8)]
        bank_full = [sem(f"bank_full{i}") for i in range(8)]
        bank_free = [sem(f"bank_free{i}") for i in range(8)]
        turn = {}
        fillings = [0] * 8

        def claim(pe, bank, key):
            if fillings[bank]:
                pe.wait_ge(bank_free[bank], fillings[bank])
            fillings[bank] += 1
            turn[key] = (bank, fillings[bank])
            return PS[bank]

        def full(eng, key):
            b, n = turn[key]
            eng.wait_ge(bank_full[b], n)
            return PS[b]

        def drained(eng, key):
            b, n = turn[key]
            eng.wait_ge(bank_free[b], n)

        def chunk(c):
            return slice(c * SEQ, (c + 1) * SEQ)

        def tile_(t):
            return slice(t * P, (t + 1) * P)

        block = ctx.enter_context(nc.Block())

        @block.tensor
        def _(pe):
            def mm(out_, lhsT, rhs, start=True, stop=True, **kw):
                return nc.tensor.matmul(out_, lhsT, rhs, start=start, stop=stop, **kw)

            def prep_xt(n):
                bank = claim(pe, 7, ("xt", n))
                pe.wait_ge(sem("xn_ready"), n + 1)
                for t in range(TPC):
                    last = nc.tensor.transpose(bank[:, tile_(t)], XN[:, n % 2, t, :], ident[:])
                last.then_inc(bank_full[7], 1)

            pe.wait_ge(sem("ident_ready"), 2)
            pe.wait_ge(sem("small_loaded"), 16)
            pe.wait_ge(sem("ones_ready"), 1)
            order = 0
            for l in (0, 3):
                b = order % 6
                bank = claim(pe, b, ("Mk", l))
                mm(bank[:, 0:BK], small(f"waT{l}"), small("ctxT")).then_inc(bank_full[b], 1)
                order += 1
                b = order % 6
                bank = claim(pe, b, ("Vw", l))
                for i in range(BATCH):
                    last = mm(bank[0:KEYS, tile_(i)], small("ctxT")[:, i * KEYS:(i + 1) * KEYS],
                              small(f"wcT{l}")[:, 0:P])
                last.then_inc(bank_full[b], 1)
                order += 1
            for l in (1, 2):
                b = order % 6
                bank = claim(pe, b, ("KT", l))
                mm(bank[:, 0:BK], small(f"wkT{l}"), small("ctxT")).then_inc(bank_full[b], 1)
                order += 1
                b = order % 6
                bank = claim(pe, b, ("Vc", l))
                for i in range(BATCH):
                    mm(bank[0:KEYS, tile_(i)], small("ctxT")[:, i * KEYS:(i + 1) * KEYS],
                       small(f"wvT{l}"), stop=False)
                    last = mm(bank[0:KEYS, tile_(i)], ones_row[:, 0:KEYS], small(f"bv{l}"), start=False)
                last.then_inc(bank_full[b], 1)
                order += 1

            def window_layer(s, l):
                def front(c):
                    n = 4 * s + c
                    prep_xt(n)
                    b = c % 2
                    bank = claim(pe, b, ("sc", s, c))
                    if c == 0:
                        drained(pe, ("Mk", l))
                    drained(pe, ("xt", n))
                    for t in range(TPC):
                        last = mm(bank[:, t * KEYS:(t + 1) * KEYS], XNT[:, tile_(4 * c + t)],
                                  Mk[l][:, c * KEYS:(c + 1) * KEYS])
                    last.then_inc(bank_full[b], 1)

                def back(c):
                    b = 2 + c % 2
                    bank = claim(pe, b, ("eT", s, c))
                    pe.wait_ge(sem(f"probs_ready{s}"), c + 1)
                    for t in range(TPC):
                        last = nc.tensor.transpose(bank[0:KEYS, tile_(t)], sc[:, c % 2, t, :], ident[:])
                    last.then_inc(bank_full[b], 1)
                    b = 4 + c % 2
                    bank = claim(pe, b, ("pre", s, c))
                    if c == 0:
                        drained(pe, ("Vw", l))
                    drained(pe, ("eT", s, c))
                    for t in range(TPC):
                        mm(bank[:, tile_(t)], eT[:, c % 2, tile_(t)], Vw[l][:, c, :], stop=False)
                        last = mm(bank[:, tile_(t)], XNT[:, tile_(4 * c + t)], small(f"wcT{l}")[:, P:2 * P],
                                  start=False)
                    last.then_inc(bank_full[b], 1)

                for c in range(BATCH):
                    front(c)
                    if c:
                        back(c - 1)
                back(BATCH - 1)

            def gated_layer(s):
                def logits(c):
                    bank = claim(pe, 7, ("lg", s, c))
                    drained(pe, ("xt", 4 * s + c))
                    for t in range(TPC):
                        mm(bank[:, t * E0:(t + 1) * E0], XNT[:, tile_(4 * c + t)], small("gw"), stop=False)
                        last = mm(bank[:, t * E0:(t + 1) * E0], ones_row[:], small("gb"), start=False)
                    last.then_inc(bank_full[7], 1)

                def gatesT(c):
                    bank = claim(pe, 7, ("cwT", s, c))
                    pe.wait_ge(sem("cw_ready"), c + 1)
                    for t in range(TPC):
                        last = nc.tensor.transpose(bank[0:E0, tile_(t)], cw[:, c % 2, t, :], ident[:])
                    last.then_inc(bank_full[7], 1)

                def up(c, i):
                    xc = XNT[:, chunk(c)]
                    w1 = SLOT[0][:, i * P:(i + 1) * P] if i < PAIRS else small("sw1")
                    w3 = SLOT[0][:, 2048 + i * P:2048 + (i + 1) * P] if i < PAIRS else small("sw3")
                    b = i % 2
                    mm(claim(pe, b, ("A", c, i))[:], w1, xc).then_inc(bank_full[b], 1)
                    mm(claim(pe, 2 + b, ("C", c, i))[:], w3, xc).then_inc(bank_full[2 + b], 1)
                    if i < PAIRS:
                        mm(claim(pe, 4 + b, ("G", c, i))[:], pairsel[:, i, :], cw3[:, c % 2, :])\
                            .then_inc(bank_full[4 + b], 1)

                def down(c, i):
                    if i == 0:
                        bank = claim(pe, 6, ("oT", c))
                        if c == 0:
                            pe.wait_ge(sem("w2_loaded"), 16)
                        mm(bank[:], small("b2_0"), cwT[:, c % 2, :], stop=False)
                    drained(pe, ("G" if i < PAIRS else "C", c, i))
                    w2 = SLOT[1][:, i * P:(i + 1) * P] if i < PAIRS else small("sw2")
                    last = mm(PS[6][:], w2, H1[:, i % 2, :], start=False, stop=i == PAIRS)
                    last.then_inc(sem("h_used"), 1) if i < PAIRS else last.then_inc(bank_full[6], 1)

                def back(c):
                    bank = claim(pe, 7, ("ob", c))
                    drained(pe, ("oT", c))
                    for t in range(TPC):
                        last = nc.tensor.transpose(bank[:, tile_(t)], outT[:, tile_(t)], ident[:])
                    last.then_inc(bank_full[7], 1)

                prep_xt(4 * s)
                logits(0)
                gatesT(0)
                pe.wait_ge(sem("w13_loaded"), 16)
                for c in range(BATCH):
                    drained(pe, ("cwT", s, c))
                    pe.wait_ge(sem("cw3_ready"), c + 1)
                    for i in range(PAIRS + 1):
                        up(c, i)
                        if i == 2 and c:
                            back(c - 1)
                        if c + 1 < BATCH:
                            if i == 5:
                                prep_xt(4 * s + c + 1)
                            if i == 6:
                                logits(c + 1)
                            if i == 14:
                                gatesT(c + 1)
                        if i:
                            down(c, i - 1)
                    down(c, PAIRS)
                back(BATCH - 1)

            def heads_layer(s, l):
                def query(c):
                    bank = claim(pe, 7, ("q", s, c))
                    drained(pe, ("xt", 4 * s + c))
                    mm(bank[:], small(f"wqT{l}"), XNT[:, chunk(c)]).then_inc(bank_full[7], 1)

                def scores(u):
                    c, t = divmod(u, TPC)
                    if t == 0:
                        drained(pe, ("q", s, c))
                        pe.wait_ge(sem("kbd_ready"), BATCH * (l - 1) + c + 1)
                    if u == 0:
                        pe.wait_ge(sem("delta_ready"), 1)
                    for b, (h0, h1) in enumerate(HEAD_BANKS):
                        bank = claim(pe, b, ("S", s, u, b))
                        n = (h1 - h0) * KEYS
                        mm(bank[:, 0:n], ones96[:],
                           delta3[:, c * KEYS:(c + 1) * KEYS].unsqueeze(1).to_broadcast([96, h1 - h0, KEYS]),
                           stop=False)
                        mm(bank[:, 0:n], qT[:, c % 2, tile_(t)],
                           kbd[:, c % 2, h0:h1, :].rearrange("p h k -> p (h k)"), start=False)\
                            .then_inc(bank_full[b], 1)

                def probsT(u):
                    pe.wait_ge(sem(f"exp_ready{s}"), u + 1)
                    for g in range(4):
                        b = 3 + g % 2
                        bank = claim(pe, b, ("T", s, u, g))
                        for j in range(4):
                            last = nc.tensor.transpose(bank[0:KEYS, tile_(j)], PR[:, u % 2, 4 * g + j, :], ident[:])
                        last.then_inc(bank_full[b], 1)

                def values(u):
                    c = u // TPC
                    bank = claim(pe, 5, ("O", s, u))
                    for g in range(4):
                        drained(pe, ("T", s, u, g))
                        for j in range(4):
                            last = mm(bank[32 * j:32 * j + 32, tile_(g)], vpad[:, c % 2, 4 * g + j, :],
                                      PT[:, u % 2, 4 * g + j, :])
                    last.then_inc(bank_full[5], 1)

                def back_to_tokens(u):
                    bank = claim(pe, 6, ("Ot", s, u))
                    drained(pe, ("O", s, u))
                    for g in range(4):
                        last = nc.tensor.transpose(bank[:, tile_(g)], OTt[:, g, :], ident[:])
                    last.then_inc(bank_full[6], 1)

                def headsT(u):
                    bank = claim(pe, 7, ("OT", s, u))
                    drained(pe, ("Ot", s, u))
                    nc.tensor.transpose(bank[:, 0:P], On, ident[:]).then_inc(bank_full[7], 1)

                def project(u):
                    bank = claim(pe, 7, ("Y", s, u))
                    drained(pe, ("OT", s, u))
                    mm(bank[:, 0:P], OT, small(f"woT{l}"), stop=False)
                    mm(bank[:, 0:P], ones_row[:], small(f"bo{l}"), start=False).then_inc(bank_full[7], 1)

                prep_xt(4 * s)
                query(0)
                for u in range(NT + 4):
                    if u < NT:
                        scores(u)
                    if 2 <= u < NT + 2:
                        values(u - 2)
                    if u >= 4:
                        project(u - 4)
                    if u < NT and u % TPC == 2 and u // TPC + 1 < BATCH:
                        prep_xt(4 * s + u // TPC + 1)
                        query(u // TPC + 1)
                    if 1 <= u < NT + 1:
                        probsT(u - 1)
                    if 3 <= u < NT + 3:
                        headsT(u - 3)
                    if 2 <= u < NT + 2:
                        back_to_tokens(u - 2)

            def topk_layer(s, l):
                rhs_of = (lambda c: XNT[:, chunk(c)]) if l == 1 else (lambda c: XNT2[:, c % 2, :])

                def route(c):
                    n = 4 * s + c
                    prep_xt(n)
                    bank = claim(pe, 6, ("rl", s, c))
                    drained(pe, ("xt", n))
                    for t in range(TPC):
                        last = mm(bank[:, t * E1:(t + 1) * E1], XNT[:, tile_(4 * c + t)],
                                  small("rwT" if l == 1 else "wr"), stop=l == 1)
                        if l == 3:
                            last = mm(bank[:, t * E1:(t + 1) * E1], ones_row[:], small("br"), start=False)
                    last.then_inc(bank_full[6], 1)
                    if l == 3:
                        bank = claim(pe, 7, ("xt2", c))
                        pe.wait_ge(sem("xn2_ready"), c + 1)
                        for t in range(TPC):
                            last = nc.tensor.transpose(bank[:, tile_(t)], xn2[:, t, :], ident[:])
                        last.then_inc(bank_full[7], 1)

                def finish_route(c):
                    if l == 1:
                        bank = claim(pe, 6, ("cum", c))
                        pe.wait_ge(sem("onehot_ready"), c + 1)
                        w = 2 * E1
                        mm(bank[:, 0:TPC * w], tri[:], ohb[:].rearrange("p t k e -> p (t k e)"),
                           stop=False, skip_group_check=True)
                        for t in range(TPC):
                            one = ohb[:, t, :, :].rearrange("p k e -> p (k e)")
                            if t + 1 < TPC:
                                mm(bank[:, (t + 1) * w:TPC * w], ones_b[:],
                                   one.unsqueeze(1).to_broadcast([P, TPC - 1 - t, w]),
                                   start=False, stop=False, skip_group_check=True)
                            last = mm(bank[:, TPC * w:(TPC + 1) * w], ones_b[:], one, start=False,
                                      stop=t == TPC - 1, skip_group_check=True)
                        last.then_inc(bank_full[6], 1)
                    else:
                        bank = claim(pe, 6, ("gT", c))
                        pe.wait_ge(sem("gates_ready"), c + 1)
                        for t in range(TPC):
                            last = nc.tensor.transpose(bank[0:E1, tile_(t)], cwd[:, c % 2, t, :], ident[:])
                        last.then_inc(bank_full[6], 1)
                        bank = claim(pe, 6, ("b2", c))
                        drained(pe, ("gT", c))
                        for t in range(TPC):
                            last = mm(bank[:, tile_(t)], cwdT[:, c % 2, tile_(t)], small("b2_3"))
                        last.then_inc(bank_full[6], 1)

                def up(c, e):
                    for f in range(FC):
                        b = (4 * (c * E1 + e) + f) % 3
                        mm(claim(pe, b, ("U", s, c, e, f))[:], SLOT[2][:, e * F1 + f * P:e * F1 + (f + 1) * P],
                           rhs_of(c)).then_inc(bank_full[b], 1)

                def down(c, e):
                    k = c * E1 + e
                    b = 3 + k % 2
                    bank = claim(pe, b, ("Yd", s, c, e))
                    for f in range(FC):
                        drained(pe, ("U", s, c, e, f))
                    for t in range(TPC):
                        for f in range(FC):
                            last = mm(bank[:, tile_(t)], HT[:, k % 2, f, tile_(t)],
                                      SLOT[3][:, (e * FC + f) * P:(e * FC + f + 1) * P],
                                      start=f == 0, stop=f == FC - 1)
                    last.then_inc(bank_full[b], 1)

                route(0)
                finish_route(0)
                pe.wait_ge(sem(f"up_loaded{l}"), 16)
                pe.wait_ge(sem(f"down_loaded{l}"), 16)
                for c in range(BATCH):
                    if l == 3:
                        drained(pe, ("xt2", c))
                    for e in range(E1):
                        up(c, e)
                        if c + 1 < BATCH:
                            if e == 3:
                                route(c + 1)
                            if e == 6:
                                finish_route(c + 1)
                        if c or e:
                            down(*divmod(c * E1 + e - 1, E1))
                down(BATCH - 1, E1 - 1)

            def choice_layer(s):
                def front(c):
                    n = 4 * s + c
                    prep_xt(n)
                    b = c % 2
                    bank = claim(pe, b, ("cl", c))
                    drained(pe, ("xt", n))
                    mm(bank[:], small("ctrl"), XNT[:, chunk(c)]).then_inc(bank_full[b], 1)

                def select(c):
                    bank = claim(pe, 2, ("pt", c))
                    pe.wait_ge(sem("perm_ready"), c + 1)
                    for t in range(TPC):
                        last = nc.tensor.transpose(bank[:, t * ES:(t + 1) * ES], PERM[0:ES, tile_(t)],
                                                   ident[0:ES, 0:ES])
                    last.then_inc(bank_full[2], 1)
                    for t in range(TPC):
                        b = 3 + t % 2
                        bank = claim(pe, b, ("sel", c, t))
                        if t < TPC - 1:
                            pe.wait_ge(sem("bd_ready"), c * (TPC - 1) + t + 1)
                        else:
                            drained(pe, ("pt", c))
                        mm(bank[:], XN[:, c % 2, t, :], BD[:, t % 2, :, :].rearrange("p g e -> p (g e)"))\
                            .then_inc(bank_full[b], 1)

                front(0)
                for c in range(BATCH):
                    if c + 1 < BATCH:
                        front(c + 1)
                    select(c)

                pe.wait_ge(sem("f1_loaded"), 16)
                pe.wait_ge(sem("f2_loaded"), 16)
                drained(pe, ("sel", BATCH - 1, 2))
                drained(pe, ("sel", BATCH - 1, 3))

                def up(q):
                    b = q % 2
                    bank = claim(pe, b, ("cu", q))
                    for i in range(4):
                        for h in range(2):
                            e = 8 * q + 2 * i + h
                            last = mm(bank[h * FS:(h + 1) * FS, tile_(i)], SLOT[0][:, e * FS:(e + 1) * FS],
                                      SELT[:, :, e])
                    last.then_inc(bank_full[b], 1)

                def down(q):
                    drained(pe, ("cu", q))
                    for h in range(2):
                        b = 2 + 2 * (q % 2) + h
                        bank = claim(pe, b, ("cd", q, h))
                        for i in range(4):
                            last = mm(bank[:, tile_(i)],
                                      SLOT[1][h * FS:(h + 1) * FS, (4 * q + i) * P:(4 * q + i + 1) * P],
                                      INN[h * FS:(h + 1) * FS, q % 2, i, :])
                        last.then_inc(bank_full[b], 1)

                for q in range(ES // 8):
                    up(q)
                    if q:
                        down(q - 1)
                down(ES // 8 - 1)
                for q in (ES // 8 - 2, ES // 8 - 1):
                    for h in range(2):
                        drained(pe, ("cd", q, h))

                def rows(c, k):
                    b = (4 * c + k) % 2
                    bank = claim(pe, b, ("in", c, k))
                    for j in range(4):
                        g = 32 * c + 8 * k + 2 * j
                        last = nc.tensor.transpose(bank[:, tile_(j)],
                                                   SELT[:, g:g + 2, :].rearrange("p g e -> p (g e)"), ident[:])
                    last.then_inc(bank_full[b], 1)

                def combine(c):
                    b = 2 + c % 2
                    bank = claim(pe, b, ("co", c))
                    pe.wait_ge(sem("pb_ready"), c + 1)
                    for k in range(4):
                        drained(pe, ("in", c, k))
                        for j in range(4):
                            last = mm(bank[32 * j:32 * j + 32, tile_(k)],
                                      XNT[:, c * SEQ + k * P + 32 * j:c * SEQ + k * P + 32 * j + 32],
                                      INTER[:, c % 2, k, tile_(j)])
                    last.then_inc(bank_full[b], 1)

                for c in range(BATCH):
                    for k in range(4):
                        rows(c, k)
                    if c:
                        combine(c - 1)
                combine(BATCH - 1)

            for s, (kind, l) in enumerate(layers):
                if kind == WINDOW_ATT:
                    window_layer(s, l)
                elif kind == GATED:
                    gated_layer(s)
                elif kind == HEADS_ATT:
                    heads_layer(s, l)
                elif kind == TOPK:
                    topk_layer(s, l)
                else:
                    choice_layer(s)

        @block.vector
        def _(dve):
            v = nc.vector
            counted = {}

            def mark(ins, name="dve_step"):
                ins.then_inc(sem(name), 1)
                counted[name] = counted.get(name, 0) + 1
                dve.wait_ge(sem(name), counted[name])

            def free(ins, key):
                b, n = turn[key]
                ins.then_inc(bank_free[b], 1)
                dve.wait_ge(bank_free[b], n)

            mark(v.memset(ones_row[:], 1.0), "ones_ready")
            mark(v.memset(neghalf[:], -0.5), "neghalf_ready")
            mark(v.memset(gs[:], -9.0))
            mark(v.memset(me[:], -9.0))
            mark(v.memset(r8[:], -9.0))
            mark(v.memset(carry[:], 0.0))
            mark(v.memset(ones_b[:], 1.0))
            mark(v.memset(ones96[:], 1.0))
            mark(v.memset(delta3[:], 0.0))
            dve.wait_ge(sem("iota_done"), 4)
            mark(v.tensor_copy(idx_f[:], idx_i[:]))
            mark(v.tensor_copy(pidx_f[:], pidx_i[:]))
            mark(v.tensor_copy(desc[:], desc_i[:]))
            mark(v.tensor_scalar(tie[:], tie_i[:], 1e-6 / (GRP - 1), None, ALU.mult))

            def layernorm(src, dst, last_name):
                for t in range(TPC):
                    ins = v.bn_stats(stats[:, t, :], src(t))
                    ins.then_inc(sem("bn_done"), 1)
                counted["bn"] = counted.get("bn", 0) + TPC
                dve.wait_ge(sem("bn_done"), counted["bn"])
                for t in range(TPC):
                    v.bn_aggr(mv[:, t, :], stats[:, t, :]).then_inc(sem("bn_done"), 1)
                counted["bn"] += TPC
                dve.wait_ge(sem("bn_done"), counted["bn"])
                k = counted.get("var_ready", 0)
                mark(v.tensor_scalar(veps[:, k % 2, :], mv[:, :, 1], 1e-5, None, ALU.add), "var_ready")
                dve.wait_ge(sem("rstd_ready"), k + 1)
                for t in range(TPC):
                    ins = v.tensor_scalar(dst(t), src(t), mv[:, t, 0:1], rstd[:, k % 2, t:t + 1],
                                          ALU.subtract, ALU.mult)
                    if t < TPC - 1:
                        ins.then_inc(sem("ln_part"), 1)
                counted["ln_part"] = counted.get("ln_part", 0) + TPC - 1
                mark(ins, last_name)
                dve.wait_ge(sem("ln_part"), counted["ln_part"])

            def prep_ln(n):
                s, c = divmod(n, BATCH)
                if n < 4:
                    dve.wait_ge(sem(f"x_loaded{n}"), 16)
                if n >= 2:
                    full(dve, ("xt", n - 2))
                    kind = layers[(n - 2) // BATCH][0]
                    if kind == CHOICE:
                        full(dve, ("sel", (n - 2) % BATCH, TPC - 1))
                layernorm(lambda t: X[:, 4 * c + t, :], lambda t: XN[:, n % 2, t, :], "xn_ready")

            prep_ln(0)
            dve.wait_ge(sem("small_loaded"), 16)
            dve.wait_ge(sem("lens_loaded"), 16)
            mark(v.tensor_copy(lens_f[:], lens_i[:]))
            mark(v.tensor_scalar(lo_hi[:, 0, :], small("pt"), -WINDOW, 0.0, ALU.add, ALU.max))
            mark(v.tensor_scalar(lo_hi[:, 1, :], small("pt"), WINDOW, None, ALU.add))
            mark(v.tensor_tensor(lo_hi[:, 1, :], lo_hi[:, 1, :], lens_f[:], ALU.min))
            idx_b = idx_f[:].unsqueeze(1).to_broadcast([P, BATCH, KEYS])
            mark(v.tensor_tensor(keep[:], idx_b, lo_hi[:, 0, :].unsqueeze(2).to_broadcast([P, BATCH, KEYS]), ALU.is_ge))
            mark(v.tensor_tensor(neg[:], idx_b, lo_hi[:, 1, :].unsqueeze(2).to_broadcast([P, BATCH, KEYS]), ALU.is_le))
            mark(v.tensor_tensor(keep[:], keep[:], neg[:], ALU.mult))
            mark(v.tensor_scalar(neg[:], keep[:], 1e9, -1e9, ALU.mult, ALU.add))
            mark(v.tensor_scalar(gauss[:], small("pt"), pidx_f[:], None, ALU.subtract))
            mark(v.tensor_tensor(gauss[:], gauss[:], gauss[:], ALU.mult), "dist_ready")
            mark(v.tensor_scalar(tau_s[:], small("tau"), float(DK) ** -0.5, None, ALU.mult))
            mark(v.tensor_scalar(dtmp[:, 0, :], small("delta"), float(DK) ** -0.5, None, ALU.mult))
            mark(v.tensor_copy(delta3[0:1, :], dtmp[:, 0, :]))
            mark(v.tensor_tensor(dtmp[:, 1, :], dtmp[:, 0, :], delta3[0:1, :], ALU.subtract))
            mark(v.tensor_copy(dtb[:], dtmp[:, 1, :]))
            mark(v.tensor_copy(delta3[32:33, :], dtb[:]))
            mark(v.tensor_tensor(dtmp[:, 1, :], dtmp[:, 1, :], dtb[:], ALU.subtract))
            mark(v.tensor_copy(delta3[64:65, :], dtmp[:, 1, :]), "delta_ready")
            dve.wait_ge(sem("gauss_ready"), 1)
            for l in (0, 3):
                bank = full(dve, ("Mk", l))
                free(v.tensor_copy(Mk[l][:], bank[:, 0:BK]), ("Mk", l))
                bank = full(dve, ("Vw", l))
                free(v.tensor_tensor(Vw[l][:], bank[0:KEYS, :].rearrange("p (b n) -> p b n", b=BATCH),
                                     gauss[0:KEYS, :].unsqueeze(2).to_broadcast([KEYS, BATCH, P]), ALU.mult),
                     ("Vw", l))
            for l in (1, 2):
                bank = full(dve, ("KT", l))
                view = bank[:, 0:BK].rearrange("p (b k) -> p b k", b=BATCH)
                tau_b = tau_s[:].unsqueeze(2).to_broadcast([P, BATCH, KEYS])
                free(v.scalar_tensor_tensor(KT[l][:].rearrange("p (b k) -> p b k", b=BATCH), view,
                                            small(f"bk{l}"), tau_b, ALU.add, ALU.mult), ("KT", l))
                bank = full(dve, ("Vc", l))
                free(v.tensor_copy(Vc[l][:], bank[0:KEYS, :].rearrange("p (b n) -> p b n", b=BATCH)), ("Vc", l))

            def window_layer(s, l):
                def masked(c):
                    bank = full(dve, ("sc", s, c))
                    S = sc[:, c % 2]
                    if c >= 2:
                        full(dve, ("eT", s, c - 2))
                    kb = keep[:, c, :].unsqueeze(1).to_broadcast([P, TPC, KEYS])
                    nb = neg[:, c, :].unsqueeze(1).to_broadcast([P, TPC, KEYS])
                    free(v.tensor_tensor(S, bank[:, 0:TPC * KEYS].rearrange("p (t k) -> p t k", t=TPC), kb,
                                         ALU.mult), ("sc", s, c))
                    mark(v.tensor_tensor(S, S, nb, ALU.add))
                    mark(v.tensor_reduce(mx[:, 0:TPC], S, AX, ALU.max))
                    mark(v.tensor_tensor(S, S, mx[:, 0:TPC].unsqueeze(2).to_broadcast([P, TPC, KEYS]),
                                         ALU.subtract), f"masked_ready{s}")

                def normed(c):
                    S = sc[:, c % 2]
                    dve.wait_ge(sem(f"wexp_ready{s}"), c + 1)
                    mark(v.tensor_reduce(red[:, 0:TPC], S, AX, ALU.add))
                    mark(v.reciprocal(red[:, 0:TPC], red[:, 0:TPC]))
                    mark(v.tensor_tensor(S, S, red[:, 0:TPC].unsqueeze(2).to_broadcast([P, TPC, KEYS]), ALU.mult),
                         f"probs_ready{s}")

                def add(c):
                    bank = full(dve, ("pre", s, c))
                    drained(dve, ("pre", s, c))
                    mark(v.tensor_tensor(X[:, 4 * c:4 * c + 4, :], X[:, 4 * c:4 * c + 4, :],
                                         th[:].rearrange("p (t n) -> p t n", t=TPC), ALU.add), f"x_done{s}")

                if s:
                    prep_ln(4 * s)
                for c in range(BATCH):
                    masked(c)
                    if c + 1 < BATCH:
                        prep_ln(4 * s + c + 1)
                    normed(c)
                    if c:
                        add(c - 1)
                add(BATCH - 1)

            def gated_layer(s):
                def top4(src, dst, w):
                    for t in range(TPC):
                        mark(v.max(v8[:, t, :], src[:, t, 0:w]))
                    mark(v.tensor_copy(r8[:, :, 0:4], v8[:, :, 0:4]))
                    for t in range(TPC):
                        mark(v.match_replace(dst[:, t, :], r8[:, t, :], src[:, t, :], 8.0))

                def route(c):
                    bank = full(dve, ("lg", s, c))
                    view = bank[:, 0:TPC * E0].rearrange("p (t e) -> p t e", t=TPC)
                    mark(v.tensor_reduce(mx[:, 0:TPC], view, AX, ALU.max))
                    free(v.tensor_tensor(s0[:], view, mx[:, 0:TPC].unsqueeze(2).to_broadcast([P, TPC, E0]),
                                         ALU.subtract), ("lg", s, c))

                def choose(c):
                    dve.wait_ge(sem("rexp_ready"), c + 1)
                    mark(v.tensor_reduce(red[:, 0:TPC], s0[:], AX, ALU.add))
                    mark(v.reciprocal(red[:, 0:TPC], red[:, 0:TPC]))
                    mark(v.tensor_tensor(s0[:], s0[:], red[:, 0:TPC].unsqueeze(2).to_broadcast([P, TPC, E0]),
                                         ALU.mult))
                    s4 = s0[:].rearrange("p t (g m) -> p (t g) m", m=4)
                    p6 = pr[:].rearrange("p t g m -> p (t g) m")
                    for a, j, w in ((0, 1, 3), (3, 2, 2), (5, 3, 1)):
                        mark(v.tensor_tensor(p6[:, :, a:a + w], s4[:, :, 0:w], s4[:, :, j:j + w], ALU.add))
                    mark(v.tensor_reduce(gs[:, :, 0:8], pr[:], AX, ALU.max))
                    top4(gs, gk, 8)
                    mark(v.tensor_scalar(pen[:], gk[:, :, 0:8], 8.0, -4.0, ALU.is_lt, ALU.mult))
                    for t in range(TPC):
                        mark(v.tensor_tensor(me[:, t, 0:E0].rearrange("p (g m) -> p g m", m=4),
                                             s0[:, t, :].rearrange("p (g m) -> p g m", m=4),
                                             pen[:, t, :].unsqueeze(2).to_broadcast([P, 8, 4]), ALU.add))
                    top4(me, mk, E0)
                    if c >= 2:
                        full(dve, ("cwT", s, c - 2))
                    mark(v.scalar_tensor_tensor(cw[:, c % 2], mk[:, :, 0:E0], 8.0, s0[:], ALU.is_equal, ALU.mult),
                         "cw_ready")

                def split(c):
                    a = c % 2
                    bank = full(dve, ("cwT", s, c))
                    if c >= 2:
                        full(dve, ("oT", c - 2))
                    free(v.tensor_copy(cwT[:, a, :], bank[0:E0, :]), ("cwT", s, c))
                    mark(v.tensor_copy(cw3[0:32, a, :], cwT[:, a, :]))
                    mark(v.tensor_tensor(cwr, cwT[:, a, :], cw3[0:32, a, :], ALU.subtract))
                    mark(v.tensor_copy(cwm[:], cwr))
                    mark(v.tensor_copy(cw3[32:64, a, :], cwm[:]))
                    mark(v.tensor_tensor(cwr, cwr, cwm[:], ALU.subtract))
                    mark(v.tensor_copy(cw3[64:96, a, :], cwr), "cw3_ready")

                def gate(c, i):
                    k = c * (PAIRS + 1) + i
                    bank = full(dve, ("C", c, i))
                    drained(dve, ("A", c, i))
                    if i >= 2:
                        dve.wait_ge(sem("h_used"), c * PAIRS + i - 1)
                    elif c:
                        full(dve, ("oT", c - 1))
                    b3 = small("b3_0")[:, i:i + 1] if i < PAIRS else small("sb3")
                    h = H1[:, i % 2, :]
                    free(v.scalar_tensor_tensor(T1 if i < PAIRS else h, bank[:], b3, S1[:, k % 2, :],
                                                ALU.add, ALU.mult), ("C", c, i))
                    if i < PAIRS:
                        bank = full(dve, ("G", c, i))
                        free(v.tensor_tensor(h, T1, bank[:], ALU.mult), ("G", c, i))

                def add(c):
                    bank = full(dve, ("ob", c))
                    free(v.tensor_tensor(X[:, 4 * c:4 * c + 4, :], X[:, 4 * c:4 * c + 4, :],
                                         bank[:].rearrange("p (t n) -> p t n", t=TPC), ALU.add), ("ob", c))

                prep_ln(4 * s)
                route(0)
                choose(0)
                split(0)
                for c in range(BATCH):
                    for i in range(PAIRS + 1):
                        if i == 3 and c:
                            add(c - 1)
                        if c + 1 < BATCH:
                            if i == 3:
                                prep_ln(4 * s + c + 1)
                            if i == 7:
                                route(c + 1)
                            if i == 8:
                                choose(c + 1)
                            if i == 15:
                                split(c + 1)
                        gate(c, i)
                add(BATCH - 1)

            def heads_layer(s, l):
                def shifted(u):
                    if u >= 2:
                        full(dve, ("T", s, u - 2, 3))
                    for b, (h0, h1) in enumerate(HEAD_BANKS):
                        bank = full(dve, ("S", s, u, b))
                        view = bank[:, 0:(h1 - h0) * KEYS].rearrange("p (h k) -> p h k", k=KEYS)
                        mark(v.tensor_reduce(mx[:, h0:h1], view, AX, ALU.max))
                        free(v.tensor_tensor(PR[:, u % 2, h0:h1, :], view,
                                             mx[:, h0:h1].unsqueeze(2).to_broadcast([P, h1 - h0, KEYS]),
                                             ALU.subtract), ("S", s, u, b))

                def probsT(u):
                    if u >= 2:
                        full(dve, ("O", s, u - 2))
                    for g in (1, 3):
                        bank = full(dve, ("T", s, u, g))
                        free(v.tensor_copy(PT[:, u % 2, 4 * g:4 * g + 4, :],
                                           bank[0:KEYS, :].rearrange("p (h q) -> p h q", h=4)), ("T", s, u, g))

                def normed(u):
                    bank = full(dve, ("Ot", s, u))
                    view = bank[:].rearrange("p (h r) -> p h r", r=32)
                    mark(v.reciprocal(red[:], view[:, :, DK]))
                    if u:
                        full(dve, ("OT", s, u - 1))
                    free(v.tensor_tensor(On.rearrange("p (h d) -> p h d", h=HEADS), view[:, :, 0:DK],
                                         red[:].unsqueeze(2).to_broadcast([P, HEADS, DK]), ALU.mult),
                         ("Ot", s, u))

                def add(u):
                    bank = full(dve, ("Y", s, u))
                    free(v.tensor_tensor(X[:, u, :], X[:, u, :], bank[:, 0:P], ALU.add), ("Y", s, u))

                prep_ln(4 * s)
                for u in range(NT + 4):
                    if u < NT:
                        shifted(u)
                    if u >= 4:
                        add(u - 4)
                    if u < NT and u % TPC == 1 and u // TPC + 1 < BATCH:
                        prep_ln(4 * s + u // TPC + 1)
                    if 1 <= u < NT + 1:
                        probsT(u - 1)
                    if 2 <= u < NT + 2:
                        normed(u - 2)

            def topk_layer(s, l):
                def route(c):
                    bank = full(dve, ("rl", s, c))
                    view = bank[:, 0:TPC * E1].rearrange("p (t e) -> p t e", t=TPC)
                    mark(v.tensor_reduce(mx[:, 0:TPC], view, AX, ALU.max))
                    free(v.tensor_tensor(pb8[:], view, mx[:, 0:TPC].unsqueeze(2).to_broadcast([P, TPC, E1]),
                                         ALU.subtract), ("rl", s, c))

                def spread(ap):
                    return ap.unsqueeze(2).to_broadcast([P, TPC, E1])

                def largest(src, k):
                    mark(v.tensor_reduce(tv[:, k, :], src, AX, ALU.max))
                    mark(v.tensor_tensor(t8[:], src, spread(tv[:, k, :]), ALU.is_equal))
                    mark(v.tensor_tensor(t8[:], t8[:], desc[:].unsqueeze(1).to_broadcast([P, TPC, E1]), ALU.mult))
                    mark(v.tensor_reduce(red[:, 0:TPC], t8[:], AX, ALU.max))
                    mark(v.tensor_tensor(oh[:, k], t8[:], spread(red[:, 0:TPC]), ALU.is_equal))

                def choose(c):
                    dve.wait_ge(sem(f"rexp_ready{s}"), c + 1)
                    mark(v.tensor_reduce(red[:, 0:TPC], pb8[:], AX, ALU.add))
                    mark(v.reciprocal(red[:, 0:TPC], red[:, 0:TPC]))
                    mark(v.tensor_tensor(pb8[:], pb8[:], spread(red[:, 0:TPC]), ALU.mult))
                    largest(pb8[:], 0)
                    if l == 3:
                        mark(v.tensor_tensor(cwd[:, c % 2], oh[:, 0], spread(tv[:, 0, :]), ALU.mult), "gates_ready")
                        return
                    mark(v.scalar_tensor_tensor(pb8[:], oh[:, 0], -2.0, pb8[:], ALU.mult, ALU.add))
                    largest(pb8[:], 1)
                    mark(v.tensor_copy(ohb[:, :, 0, :], oh[:, 0]))
                    mark(v.tensor_copy(ohb[:, :, 1, :], oh[:, 1]), "onehot_ready")
                    mark(v.tensor_tensor(tv[:, 2, :], tv[:, 0, :], tv[:, 1, :], ALU.add))
                    mark(v.reciprocal(tv[:, 2, :], tv[:, 2, :]))
                    for k in range(2):
                        mark(v.tensor_tensor(tv[:, k, :], tv[:, k, :], tv[:, 2, :], ALU.mult))
                        mark(v.tensor_tensor(gk8[:, :, k, :], oh[:, k], spread(tv[:, k, :]), ALU.mult))

                def finish(c):
                    if l == 1:
                        w = 2 * E1
                        bank = full(dve, ("cum", c))
                        mark(v.tensor_tensor(pos[:], bank[:, 0:TPC * w].rearrange("p (t n) -> p t n", t=TPC),
                                             carry[:].unsqueeze(1).to_broadcast([P, TPC, w]), ALU.add))
                        free(v.tensor_tensor(carry[:], carry[:], bank[:, TPC * w:(TPC + 1) * w], ALU.add), ("cum", c))
                        mark(v.scalar_tensor_tensor(pos[:], pos[:], float(CAPACITY),
                                                    gk8[:].rearrange("p t k e -> p t (k e)"), ALU.is_le, ALU.mult))
                        mark(v.tensor_tensor(cwd[:, c % 2], pos[:, :, 0:E1], pos[:, :, E1:w], ALU.add))
                    else:
                        bank = full(dve, ("gT", c))
                        free(v.tensor_copy(cwdT[:, c % 2, :], bank[0:E1, :]), ("gT", c))
                        bank = full(dve, ("b2", c))
                        free(v.tensor_tensor(X[:, 4 * c:4 * c + 4, :], X[:, 4 * c:4 * c + 4, :],
                                             bank[:].rearrange("p (t n) -> p t n", t=TPC), ALU.add), ("b2", c))

                def norms(c):
                    prep_ln(4 * s + c)
                    if l == 3:
                        if c:
                            full(dve, ("xt2", c - 1))
                        layernorm(lambda t: XN[:, (4 * s + c) % 2, t, :], lambda t: xn2[:, t, :], "xn2_ready")

                def add(c, e):
                    bank = full(dve, ("Yd", s, c, e))
                    for t in range(TPC):
                        ins = v.scalar_tensor_tensor(X[:, 4 * c + t, :], bank[:, tile_(t)], cwd[:, c % 2, t, e:e + 1],
                                                     X[:, 4 * c + t, :], ALU.mult, ALU.add)
                        if t < TPC - 1:
                            mark(ins, "x_tile")
                    free(ins, ("Yd", s, c, e))

                norms(0)
                route(0)
                choose(0)
                finish(0)
                for c in range(BATCH):
                    for e in range(E1):
                        if c + 1 < BATCH:
                            if e == 2:
                                norms(c + 1)
                            if e == 3:
                                route(c + 1)
                            if e == 4:
                                choose(c + 1)
                            if e == 6:
                                finish(c + 1)
                        if c or e:
                            add(*divmod(c * E1 + e - 1, E1))
                add(BATCH - 1, E1 - 1)

            def choice_layer(s):
                def choose(c):
                    bank = full(dve, ("cl", c))
                    G = SEQ // GRP
                    lg = LGT.rearrange("p (g t) -> p g t", t=GRP)
                    free(v.tensor_tensor(lg, bank[:].rearrange("p (g t) -> p g t", t=GRP),
                                         tie[:].unsqueeze(1).to_broadcast([P, G, GRP]), ALU.add), ("cl", c))
                    mark(v.tensor_reduce(red32[:], lg, AX, ALU.max))
                    if c:
                        full(dve, ("pt", c - 1))
                    mark(v.tensor_tensor(PERM.rearrange("p (g t) -> p g t", t=GRP), lg,
                                         red32[:].unsqueeze(2).to_broadcast([P, G, GRP]), ALU.is_equal),
                         "perm_ready")
                    mark(v.tensor_tensor(XNT[:, chunk(c)].rearrange("p (j m) -> p j m", m=2 * GRP),
                                         PERM.rearrange("p (j m) -> p j m", m=2 * GRP),
                                         parity[:].rearrange("p a t -> p (a t)").unsqueeze(1)
                                         .to_broadcast([P, G // 2, 2 * GRP]), ALU.mult), "pb_ready")

                def blocks(c):
                    bank = full(dve, ("pt", c))
                    for t in range(TPC):
                        k = c * TPC + t
                        if k >= 2:
                            full(dve, ("sel", *divmod(k - 2, TPC)))
                        ins = v.tensor_tensor(BD[:, t % 2], bank[:, t * ES:(t + 1) * ES].unsqueeze(1)
                                              .to_broadcast([P, GPT, ES]),
                                              gmask[:].unsqueeze(2).to_broadcast([P, GPT, ES]), ALU.mult)
                        if t < TPC - 1:
                            mark(ins, "bd_ready")
                    free(ins, ("pt", c))

                prep_ln(4 * s)
                choose(0)
                for c in range(BATCH):
                    if c + 1 < BATCH:
                        prep_ln(4 * s + c + 1)
                    blocks(c)
                    if c + 1 < BATCH:
                        choose(c + 1)
                for q in range(ES // 8):
                    bank = full(dve, ("cd", q, 0))
                    free(v.tensor_copy(SELT[:, :, 8 * q:8 * q + 8:2],
                                       bank[:].rearrange("p (i g) -> p g i", i=4)), ("cd", q, 0))

                def add(c):
                    bank = full(dve, ("co", c))
                    free(v.tensor_tensor(X[:, 4 * c:4 * c + 4, :], X[:, 4 * c:4 * c + 4, :],
                                         bank[:].rearrange("p (t n) -> p t n", t=TPC), ALU.add), ("co", c))

                for c in range(BATCH):
                    if c >= 2:
                        full(dve, ("co", c - 2))
                    for k in (1, 3):
                        bank = full(dve, ("in", c, k))
                        free(v.tensor_copy(INTER[:, c % 2, k, :], bank[:]), ("in", c, k))
                    if c:
                        add(c - 1)
                add(BATCH - 1)

            for s, (kind, l) in enumerate(layers):
                if kind == WINDOW_ATT:
                    window_layer(s, l)
                elif kind == GATED:
                    gated_layer(s)
                elif kind == HEADS_ATT:
                    heads_layer(s, l)
                elif kind == TOPK:
                    topk_layer(s, l)
                else:
                    choice_layer(s)
            dve.wait_ge(sem("dve_step"), counted["dve_step"])
            v.memset(red[:], 0.0).then_inc(sem("x_final"), 1)

        @block.scalar
        def _(act):
            a = nc.scalar

            def free(ins, key):
                ins.then_inc(bank_free[turn[key][0]], 1)

            def prep_xt(n):
                bank = full(act, ("xt", n))
                free(a.activation(XNT[:, chunk(n % BATCH)], bank[:], ACT.Copy), ("xt", n))

            act.wait_ge(sem("dist_ready"), 1)
            a.activation(gauss[:], gauss[:], ACT.Exp, scale=-1.0 / DEV_POW).then_inc(sem("gauss_ready"), 1)

            def window_layer(s, l):
                def exps(c):
                    act.wait_ge(sem(f"masked_ready{s}"), c + 1)
                    a.activation(sc[:, c % 2], sc[:, c % 2], ACT.Exp).then_inc(sem(f"wexp_ready{s}"), 1)

                def back(c):
                    bank = full(act, ("eT", s, c))
                    if c >= 2:
                        full(act, ("pre", s, c - 2))
                    free(a.activation(eT[:, c % 2, :], bank[0:KEYS, :], ACT.Copy), ("eT", s, c))
                    bank = full(act, ("pre", s, c))
                    if c:
                        act.wait_ge(sem(f"x_done{s}"), c)
                    ins = a.activation(th[:], bank[:], ACT.Tanh)
                    free(ins, ("pre", s, c))

                for c in range(BATCH):
                    prep_xt(4 * s + c)
                    exps(c)
                    if c:
                        back(c - 1)
                back(BATCH - 1)

            def gated_layer(s):
                def rexp(c):
                    drained(act, ("lg", s, c))
                    a.activation(s0[:], s0[:], ACT.Exp).then_inc(sem("rexp_ready"), 1)

                def silu(c, i):
                    k = c * (PAIRS + 1) + i
                    bank = full(act, ("A", c, i))
                    if k >= 2:
                        drained(act, ("C", *divmod(k - 2, PAIRS + 1)))
                    b1 = small("b1_0")[:, i:i + 1] if i < PAIRS else small("sb1")
                    free(a.activation(S1[:, k % 2, :], bank[:], ACT.Silu, bias=b1), ("A", c, i))

                def leave(c):
                    bank = full(act, ("oT", c))
                    if c:
                        full(act, ("ob", c - 1))
                    free(a.activation(outT, bank[:], ACT.Identity, bias=small("sb2")), ("oT", c))

                prep_xt(4 * s)
                rexp(0)
                for c in range(BATCH):
                    for i in range(PAIRS + 1):
                        if i == 1 and c:
                            leave(c - 1)
                        silu(c, i)
                        if c + 1 < BATCH:
                            if i == 5:
                                prep_xt(4 * s + c + 1)
                            if i == 6:
                                rexp(c + 1)
                leave(BATCH - 1)

            def heads_layer(s, l):
                def query(c):
                    bank = full(act, ("q", s, c))
                    free(a.activation(qT[:, c % 2, :], bank[:], ACT.Identity, bias=small(f"bq{l}")), ("q", s, c))

                def heads_out(u):
                    bank = full(act, ("O", s, u))
                    if u:
                        full(act, ("Ot", s, u - 1))
                    free(a.activation(OTt, bank[:].rearrange("p (g q) -> p g q", g=4), ACT.Copy), ("O", s, u))

                def probsT(u):
                    if u >= 2:
                        full(act, ("O", s, u - 2))
                    for g in (0, 2):
                        bank = full(act, ("T", s, u, g))
                        free(a.activation(PT[:, u % 2, 4 * g:4 * g + 4, :],
                                          bank[0:KEYS, :].rearrange("p (h q) -> p h q", h=4), ACT.Copy),
                             ("T", s, u, g))

                def exps(u):
                    for b in range(3):
                        drained(act, ("S", s, u, b))
                    a.activation(PR[:, u % 2], PR[:, u % 2], ACT.Exp).then_inc(sem(f"exp_ready{s}"), 1)

                def headsT(u):
                    bank = full(act, ("OT", s, u))
                    if u:
                        full(act, ("Y", s, u - 1))
                    free(a.activation(OT, bank[:, 0:P], ACT.Copy), ("OT", s, u))

                prep_xt(4 * s)
                query(0)
                for u in range(NT + 4):
                    if 2 <= u < NT + 2:
                        heads_out(u - 2)
                    if u < NT and u % TPC == 2 and u // TPC + 1 < BATCH:
                        prep_xt(4 * s + u // TPC + 1)
                        query(u // TPC + 1)
                    if 1 <= u < NT + 1:
                        probsT(u - 1)
                    if u < NT:
                        exps(u)
                    if 3 <= u < NT + 3:
                        headsT(u - 3)

            def topk_layer(s, l):
                def route(c):
                    prep_xt(4 * s + c)
                    drained(act, ("rl", s, c))
                    a.activation(pb8[:], pb8[:], ACT.Exp).then_inc(sem(f"rexp_ready{s}"), 1)
                    if l == 3:
                        bank = full(act, ("xt2", c))
                        free(a.activation(XNT2[:, c % 2, :], bank[:], ACT.Identity, bias=small("lnb"),
                                          scale=small("lng")), ("xt2", c))

                def hidden(c, e):
                    k = c * E1 + e
                    if k >= 2:
                        full(act, ("Yd", s, *divmod(k - 2, E1)))
                    for f in range(FC):
                        bank = full(act, ("U", s, c, e, f))
                        j = e * FC + f
                        ht = HT[:, k % 2, f, :]
                        if l == 1:
                            ins = a.activation(ht, bank[:], ACT.Gelu)
                        else:
                            ins = a.activation(ht, bank[:], ACT.Relu, bias=small("b1_3")[:, j:j + 1])
                        free(ins, ("U", s, c, e, f))

                route(0)
                for c in range(BATCH):
                    for e in range(E1):
                        hidden(c, e)
                        if e == 3 and c + 1 < BATCH:
                            route(c + 1)

            def choice_layer(s):
                def select(c):
                    for t in range(TPC):
                        bank = full(act, ("sel", c, t))
                        if c == 0 and t == 0 and s:
                            drained(act, ("Y", s - 1, NT - 1))
                        g = (TPC * c + t) * GPT
                        free(a.activation(SELT[:, g:g + GPT, :],
                                          bank[:].rearrange("p (g e) -> p g e", g=GPT), ACT.Copy), ("sel", c, t))

                prep_xt(4 * s)
                for c in range(BATCH):
                    if c + 1 < BATCH:
                        prep_xt(4 * s + c + 1)
                    select(c)

                def hidden(q):
                    bank = full(act, ("cu", q))
                    if q >= 2:
                        for h in range(2):
                            full(act, ("cd", q - 2, h))
                    for i in range(4):
                        ins = a.activation(INN[:, q % 2, i, :], bank[:, tile_(i)], ACT.Relu,
                                           bias=small("bias2")[:, 4 * q + i:4 * q + i + 1])
                        if i < 3:
                            ins.then_inc(sem("inner_part"), 1)
                    free(ins, ("cu", q))

                def leave(q):
                    bank = full(act, ("cd", q, 1))
                    free(a.activation(SELT[:, :, 8 * q + 1:8 * q + 8:2],
                                      bank[:].rearrange("p (i g) -> p g i", i=4), ACT.Copy), ("cd", q, 1))

                for q in range(ES // 8):
                    hidden(q)
                    if q:
                        leave(q - 1)
                leave(ES // 8 - 1)
                for c in range(BATCH):
                    if c >= 2:
                        full(act, ("co", c - 2))
                    for k in (0, 2):
                        bank = full(act, ("in", c, k))
                        free(a.activation(INTER[:, c % 2, k, :], bank[:], ACT.Copy), ("in", c, k))

            for s, (kind, l) in enumerate(layers):
                if kind == WINDOW_ATT:
                    window_layer(s, l)
                elif kind == GATED:
                    gated_layer(s)
                elif kind == HEADS_ATT:
                    heads_layer(s, l)
                elif kind == TOPK:
                    topk_layer(s, l)
                else:
                    choice_layer(s)

        @block.gpsimd
        def _(pool):
            g = nc.gpsimd
            counted = [0]

            def mark(ins):
                ins.then_inc(sem("pool_step"), 1)
                counted[0] += 1
                pool.wait_ge(sem("pool_step"), counted[0])

            powers = [0]

            def power():
                k = powers[0]
                powers[0] += 1
                pool.wait_ge(sem("var_ready"), k + 1)
                g.tensor_tensor(rstd[:, k % 2, :], veps[:, k % 2, :], neghalf[:], ALU.pow)\
                    .then_inc(sem("rstd_ready"), 1)

            g.iota(idx_i[:], [[1, KEYS]], base=0, channel_multiplier=0).then_inc(sem("iota_done"), 1)
            g.iota(pidx_i[:], [[0, 1]], base=0, channel_multiplier=1).then_inc(sem("iota_done"), 1)
            g.iota(desc_i[:], [[-1, E1]], base=E1, channel_multiplier=0).then_inc(sem("iota_done"), 1)
            g.iota(tie_i[:], [[1, GRP]], base=0, channel_multiplier=0).then_inc(sem("iota_done"), 1)
            g.memset(ident[:], 0.0).then_inc(sem("ident_ready"), 1)
            pool.wait_ge(sem("ident_ready"), 1)
            g.affine_select(out=ident[:], in_=ident[:], compare_op=ALU.not_equal, fill=1.0, base=0,
                            pattern=[[-1, P]], channel_multiplier=1).then_inc(sem("ident_ready"), 1)
            pool.wait_ge(sem("neghalf_ready"), 1)
            power()
            for m, w, n in ((headmask, DK, HEADS), (gmask, GRP, GPT)):
                mark(g.memset(m[:], 1.0))
                mark(g.affine_select(out=m[:], in_=m[:], compare_op=ALU.is_ge, fill=0.0, base=0,
                                     pattern=[[-w, n]], channel_multiplier=1))
                mark(g.affine_select(out=m[:], in_=m[:], compare_op=ALU.is_ge, fill=0.0, base=w - 1,
                                     pattern=[[w, n]], channel_multiplier=-1))
            mark(g.memset(tri[:], 1.0))
            mark(g.affine_select(out=tri[:], in_=tri[:], compare_op=ALU.is_ge, fill=0.0, base=0,
                                 pattern=[[1, P]], channel_multiplier=-1))
            mark(g.memset(parity[:], 1.0))
            mark(g.memset(parity[0:ES, 1, :], 0.0))
            mark(g.memset(parity[ES:P, 0, :], 0.0))
            mark(g.memset(pairsel[:], 0.0))
            for k in range(3):
                m = pairsel[32 * k:32 * k + 32, :, :].rearrange("p i (h f) -> p i h f", h=2)
                mark(g.affine_select(out=m, in_=m, compare_op=ALU.not_equal, fill=1.0, base=0,
                                     pattern=[[-2, PAIRS], [-1, 2], [0, F0]], channel_multiplier=1))
            mark(g.memset(vpad[:], 0.0))
            mark(g.memset(vpad[:, :, :, DK:DK + 1], 1.0))
            g.memset(cwm[:], 0.0).then_inc(sem("pool_consts"), 1)

            def operands(s, l, c):
                if c >= 2:
                    full(pool, ("S", s, TPC * (c - 2) + TPC - 1, 2))
                    full(pool, ("O", s, TPC * (c - 2) + TPC - 1))
                g.tensor_copy(vpad[:, c % 2, :, 0:DK], Vc[l][:, c, :].rearrange("p (h d) -> p h d", h=HEADS))\
                    .then_inc(sem("vpad_ready"), 1)
                g.tensor_tensor(kbd[:, c % 2], KT[l][:, c * KEYS:(c + 1) * KEYS].unsqueeze(1)
                                .to_broadcast([P, HEADS, KEYS]),
                                headmask[:].unsqueeze(2).to_broadcast([P, HEADS, KEYS]), ALU.mult)\
                    .then_inc(sem("kbd_ready"), 1)

            for s, (kind, l) in enumerate(layers):
                if kind == HEADS_ATT:
                    power()
                    drained(pool, ("KT", l))
                    drained(pool, ("Vc", l))
                    operands(s, l, 0)
                    operands(s, l, 1)
                    for c in range(1, BATCH):
                        power()
                        if c + 1 < BATCH:
                            operands(s, l, c + 1)
                else:
                    for _k in range(BATCH * (2 if (kind, l) == (TOPK, 3) else 1) - (s == 0)):
                        power()

        @block.sync
        def _(sp):
            sp.dma_start(X[:, 0:4, :], x_in[:, 0:4, :]).then_inc(sem("x_loaded0"), 16)
            sp.dma_start(SM[:], small_in).then_inc(sem("small_loaded"), 16)
            sp.dma_start(lens_i[:], lens_in).then_inc(sem("lens_loaded"), 16)
            for c in range(1, BATCH):
                sp.dma_start(X[:, 4 * c:4 * c + 4, :], x_in[:, 4 * c:4 * c + 4, :]).then_inc(sem(f"x_loaded{c}"), 16)
            sp.dma_start(SLOT[0][:], w13_in).then_inc(sem("w13_loaded"), 16)
            sp.dma_start(SLOT[1][:, 0:2048], w2_in).then_inc(sem("w2_loaded"), 16)
            sp.dma_start(SLOT[2][:], l1w1_in).then_inc(sem("up_loaded1"), 16)
            sp.dma_start(SLOT[3][:], l1w2_in).then_inc(sem("down_loaded1"), 16)
            if len(layers) > 5:
                full(sp, ("oT", BATCH - 1))
                sp.dma_start(SLOT[0][:], f1_in).then_inc(sem("f1_loaded"), 16)
                sp.dma_start(SLOT[1][:], f2_in).then_inc(sem("f2_loaded"), 16)
            if len(layers) > 7:
                full(sp, ("Yd", 3, BATCH - 1, E1 - 1))
                sp.dma_start(SLOT[2][:], l3w1_in).then_inc(sem("up_loaded3"), 16)
                sp.dma_start(SLOT[3][:], l3w2_in).then_inc(sem("down_loaded3"), 16)
            last = len(layers) - 1
            for c in range(BATCH):
                if layers[last] == (TOPK, 3):
                    drained(sp, ("Yd", last, c, E1 - 1))
                else:
                    sp.wait_ge(sem("x_final"), 1)
                sp.dma_start(out[:, 4 * c:4 * c + 4, :], X[:, 4 * c:4 * c + 4, :]).then_inc(sem("stored"), 16)
            sp.wait_ge(sem("stored"), 16 * BATCH)


def layout(a):
    def pack(name):
        _, r, c = OFFSET[name]
        src = small_sources[name]()
        return np.broadcast_to(src, (r, c))

    def t(n):
        return a[n].T

    small_sources = {
        "ctxT": lambda: a["ctx_1024"].transpose(2, 0, 1).reshape(P, BK),
        "pt": lambda: a["condB_pt"][None, :], "tau": lambda: a["condB_tau"][None, :],
        "delta": lambda: a["fside_BxS2_0"].reshape(1, BK),
        "gw": lambda: a["L0_ffn_gw"], "gb": lambda: a["L0_ffn_gb"][None, :],
        "b1_0": lambda: a["L0_ffn_b1"].reshape(PAIRS, P).T, "b3_0": lambda: a["L0_ffn_b3"].reshape(PAIRS, P).T,
        "b2_0": lambda: a["L0_ffn_b2"], "sw1": lambda: a["L0_ffn_sw1"], "sw3": lambda: a["L0_ffn_sw3"],
        "sw2": lambda: a["L0_ffn_sw2"], "sb1": lambda: a["L0_ffn_sb1"][:, None],
        "sb3": lambda: a["L0_ffn_sb3"][:, None], "sb2": lambda: a["L0_ffn_sb2"][:, None],
        "rwT": lambda: t("L1_ffn_router_w"),
        "ctrl": lambda: np.concatenate([a["L2_ffn_controller"].reshape(D, ES)] * 2, axis=1),
        "bias2": lambda: a["L2_ffn_bias"].reshape(ES // 2, P).T,
        "wr": lambda: a["L3_ffn_Wr"], "br": lambda: a["L3_ffn_br"][None, :],
        "b1_3": lambda: a["L3_ffn_b1"].reshape(E1 * FC, P).T, "b2_3": lambda: a["L3_ffn_b2"],
        "lng": lambda: a["L3_ffn_ln_g"][:, None], "lnb": lambda: a["L3_ffn_ln_b"][:, None],
    }
    for l in (0, 3):
        small_sources[f"waT{l}"] = lambda l=l: t(f"L{l}_xcond_W_a")
        small_sources[f"wcT{l}"] = lambda l=l: np.concatenate(
            [t(f"L{l}_xcond_W_c")[0:P], t(f"L{l}_xcond_W_c")[P:2 * P]], axis=1)
    for l in (1, 2):
        for n in "qkvo":
            small_sources[f"w{n}T{l}"] = lambda l=l, n=n: t(f"L{l}_xcond_W{n}")
        for n in "qk":
            small_sources[f"b{n}{l}"] = lambda l=l, n=n: a[f"L{l}_xcond_b{n}"][:, None]
        for n in "vo":
            small_sources[f"b{n}{l}"] = lambda l=l, n=n: a[f"L{l}_xcond_b{n}"][None, :]
    smalls = np.zeros((P, SMALL_COLS), np.float32)
    for name, r, c in SMALL:
        at = OFFSET[name][0]
        smalls[0:r, at:at + c] = pack(name)

    def up(w):
        return w.transpose(1, 0, 2).reshape(P, -1)

    def down(w):
        return w.reshape(-1, P, D).transpose(1, 0, 2).reshape(P, -1)

    return {
        "x": a["x"].reshape(NT, P, D).transpose(1, 0, 2),
        "small": smalls,
        "lens": np.broadcast_to(a["_lenS2"][None, :], (P, BATCH)),
        "w13": np.concatenate([up(a["L0_ffn_w1"]), up(a["L0_ffn_w3"])], axis=1),
        "w2": down(a["L0_ffn_w2"]),
        "l1w1": up(a["L1_ffn_w1"]), "l1w2": down(a["L1_ffn_w2"]),
        "f1": a["L2_ffn_f1"].reshape(D, ES * FS), "f2": down(a["L2_ffn_f2"]),
        "l3w1": up(a["L3_ffn_W1"]), "l3w2": down(a["L3_ffn_W2"]),
    }


def kernel(**inputs):
    import concourse.bacc as bacc
    from concourse.bass_utils import run_bass_kernel_spmd

    arrays = {n: np.ascontiguousarray(v) for n, v in layout({n: np.asarray(v) for n, v in inputs.items()}).items()}
    nc = bacc.Bacc("TRN2", target_bir_lowering=False, num_devices=1)
    args = [nc.dram_tensor(n, v.shape, mybir.dt.from_np(v.dtype), kind="ExternalInput").ap()
            for n, v in arrays.items()]
    args.append(nc.dram_tensor("y", (P, NT, D), mybir.dt.float32, kind="ExternalOutput").ap())
    build(nc, *args)
    result = run_bass_kernel_spmd(nc, [arrays], core_ids=[0])
    return result.results[0]["y"].transpose(1, 0, 2).reshape(BATCH, SEQ, D)
```

```python
import numpy as np
from contextlib import ExitStack

import concourse.bass as bass
from concourse import mybir

BATCH, SEQ, D, KEYS = 4, 512, 128, 77
P = 128
TPC = SEQ // P
NT = BATCH * TPC
E0, F0 = 32, 64
PAIRS = E0 // 2
E1, F1 = 8, 512
FC = F1 // P
HEADS, DK = 16, 8
ES, FS, GRP = 64, 64, 16
GPT = P // GRP
NG = NT * GPT
CHOICES = {1: 2, 3: 1}
BLOCKS = {l: NT * k + E1 - 1 for l, k in CHOICES.items()}
GROUPS_OF_BLOCKS = {l: -(-b // 4) for l, b in BLOCKS.items()}
MAX_ROWS = 4 * max(GROUPS_OF_BLOCKS.values()) * P
RING = 8
CAPACITY = max(1, int(1.25 * BATCH * SEQ / E1 * 2))
WINDOW, DEV_POW = 16.0, 128.0
BK = BATCH * KEYS

SMALL = [("ctxT", P, BK), ("pt", P, BATCH), ("tau", P, BATCH), ("delta", 1, BK)]
for _l in (0, 3):
    SMALL += [(f"waT{_l}", P, P), (f"wcT{_l}", P, 2 * P)]
for _l in (1, 2):
    SMALL += [(f"w{_n}T{_l}", P, P) for _n in "qkvo"]
    SMALL += [(f"b{_n}{_l}", P, 1) for _n in "qk"] + [(f"b{_n}{_l}", 1, P) for _n in "vo"]
SMALL += [("gw", P, E0), ("gb", 1, E0), ("b1_0", P, PAIRS), ("b3_0", P, PAIRS), ("b2_0", E0, P),
          ("sw1", P, P), ("sw3", P, P), ("sw2", P, P), ("sb1", P, 1), ("sb3", P, 1), ("sb2", P, 1),
          ("rwT", P, E1), ("ctrl", P, 2 * ES), ("bias2", P, ES // 2), ("wr", P, E1), ("br", 1, E1),
          ("b1_3", P, E1 * FC), ("lng", P, 1), ("lnb", P, 1)]
OFFSET, _at = {}, 0
for _n, _r, _c in SMALL:
    OFFSET[_n] = (_at, _r, _c)
    _at += _c
SMALL_COLS = _at

WINDOW_ATT, GATED, HEADS_ATT, TOPK, CHOICE = range(5)
LAYERS = [(WINDOW_ATT, 0), (GATED, 0), (HEADS_ATT, 1), (TOPK, 1), (HEADS_ATT, 2), (CHOICE, 2),
          (WINDOW_ATT, 3), (TOPK, 3)]
HEAD_BANKS = [(0, 6), (6, 11), (11, 16)]


def build(nc, x_in, small_in, lens_in, w13_in, w2_in, l1w1_in, l1w2_in, f1_in, f2_in, l3w1_in,
          l3w2_in, b2row_in, out, n_layers=len(LAYERS)):
    f32, bf16, i32, u32 = mybir.dt.float32, mybir.dt.bfloat16, mybir.dt.int32, mybir.dt.uint32
    ALU, ACT, AX = mybir.AluOpType, mybir.ActivationFunctionType, mybir.AxisListType.X
    layers = LAYERS[:n_layers]
    ctx = ExitStack()
    with ctx:
        def sb(name, shape, dt=f32):
            return ctx.enter_context(nc.sbuf_tensor(name, shape, dt))

        sems = {}

        def sem(name):
            if name not in sems:
                sems[name] = ctx.enter_context(nc.semaphore(name))
            return sems[name]

        X = sb("X", [P, NT, D])
        XN = sb("XN", [P, 2, TPC, D])
        XNT = sb("XNT", [P, NT * P])
        SM = sb("SM", [P, SMALL_COLS])
        SLOT = [sb(f"SLOT{i}", [P, 4096]) for i in range(4)]
        ident = sb("ident", [P, P])
        lens_i = sb("lens_i", [P, BATCH], i32)

        def small(name):
            at, r, c = OFFSET[name]
            return SM[0:r, at:at + c]

        ones_row = sb("ones_row", [1, P])
        idx_i = sb("idx_i", [P, KEYS], i32)
        idx_f = sb("idx_f", [P, KEYS])
        pidx_i = sb("pidx_i", [P, 1], i32)
        pidx_f = sb("pidx_f", [P, 1])
        lens_f = sb("lens_f", [P, BATCH])
        lo_hi = sb("lo_hi", [P, 2, BATCH])
        keep = sb("keep", [P, BATCH, KEYS])
        neg = sb("neg", [P, BATCH, KEYS])
        gauss = sb("gauss", [P, BATCH])
        tau_s = sb("tau_s", [P, BATCH])
        headmask = sb("headmask", [P, HEADS])
        pairsel = sb("pairsel", [96, PAIRS, P], bf16)
        ones96 = sb("ones96", [96, P], bf16)
        delta3 = sb("delta3", [96, BK], bf16)
        dtmp = sb("dtmp", [1, 2, BK])
        dtb = sb("dtb", [1, BK], bf16)
        tri = sb("tri", [P, P], bf16)
        ones_b = sb("ones_b", [P, P], bf16)
        desc = sb("desc", [P, E1])
        desc_i = sb("desc_i", [P, E1], i32)
        tie_i = sb("tie_i", [P, GRP], i32)
        tie = sb("tie", [P, GRP])
        gmask = sb("gmask", [P, GPT])
        parity = sb("parity", [P, 2, GRP])
        neghalf = sb("neghalf", [P, TPC])

        stats = sb("stats", [P, TPC, 6])
        mv = sb("mv", [P, TPC, 2])
        veps = sb("veps", [P, 2, TPC])
        rstd = sb("rstd", [P, 2, TPC])
        mx = sb("mx", [P, HEADS])
        red = sb("red", [P, HEADS])

        Mk = {l: sb(f"Mk{l}", [P, BK]) for l in (0, 3)}
        Vw = {l: sb(f"Vw{l}", [KEYS, BATCH, P]) for l in (0, 3)}
        KT = {l: sb(f"KT{l}", [P, BK]) for l in (1, 2)}
        Vc = {l: sb(f"Vc{l}", [KEYS, BATCH, P]) for l in (1, 2)}

        sc = sb("sc", [P, 2, TPC, KEYS])
        eT = sb("eT", [KEYS, 2, SEQ])
        red32 = sb("red32", [P, SEQ // GRP])
        SHARE = sb("SHARE", [P, 4352])
        S1 = SHARE[:, 0:1024].rearrange("p (a n) -> p a n", a=2)
        H1 = SHARE[:, 1024:2048].rearrange("p (a n) -> p a n", a=2)
        th = SHARE[:, 2560:3072]
        T1 = SHARE[:, 2048:2560]
        outT = SHARE[:, 2560:3072]
        cwT = SHARE[0:E0, 3072:4096].rearrange("p (a n) -> p a n", a=2)
        HS = SHARE[:, 0:1024].rearrange("p (a n) -> p a n", a=2)
        HT = SHARE[:, 1024:2048].rearrange("p (a n) -> p a n", a=2)
        YG = SHARE[:, 2048:3072].rearrange("p (r n) -> p r n", r=RING)
        YB = SHARE[:, 3072:4096].rearrange("p (a n) -> p a n", a=2)
        INTER = SHARE[:, 0:4096].rearrange("p (a f n) -> p a f n", a=2, f=4)
        cw3 = sb("cw3", [96, 2, SEQ], bf16)
        cwm = sb("cwm", [E0, SEQ], bf16)
        s0 = sb("s0", [P, TPC, E0])
        pr = sb("pr", [P, TPC, 8, 6])
        gs = sb("gs", [P, TPC, 12])
        gk = sb("gk", [P, TPC, 12])
        pen = sb("pen", [P, TPC, 8])
        me = sb("me", [P, TPC, 36])
        mk = sb("mk", [P, TPC, 36])
        v8 = sb("v8", [P, TPC, 8])
        r8 = sb("r8", [P, TPC, 8])
        cw = sb("cw", [P, 2, TPC, E0])
        pb8 = sb("pb8", [P, TPC, E1])
        t8 = sb("t8", [P, TPC, E1])
        oh = sb("oh", [P, 2, TPC, E1])
        ohb = sb("ohb", [P, TPC, 2 * E1], bf16)
        tv = sb("tv", [P, 3, TPC])
        OHA = sb("OHA", [P, NT, 2 * E1])
        POSA = sb("POSA", [P, NT, 2 * E1])
        GA = sb("GA", [P, NT, 2])
        carry = sb("carry", [P, 2 * E1])
        nblk = sb("nblk", [P, 3, E1])
        base = sb("base", [P, 2 * E1])
        step_i = sb("step_i", [P, 32], i32)
        step128 = sb("step128", [P, 32])
        lt8 = sb("lt8", [P, E1, E1])
        bidx_i = sb("bidx_i", [P, 40], i32)
        bidx = sb("bidx", [P, 40])
        bexp = sb("bexp", [P, 40])
        offs = sb("offs", [P, 2, 40], i32)
        offs4 = sb("offs4", [P, 40], i32)
        slotf = sb("slotf", [P, NT, 2])
        slots = sb("slots", [P, NT, 2], i32)
        U = sb("U", [P, 11840])
        cwr = U[0:E0, 11328:11840]
        kbd = U[:, 0:2464].rearrange("p (a h k) -> p a h k", a=2, h=HEADS)
        vpad = U[0:KEYS, 2464:3488].rearrange("p (a h k) -> p a h k", a=2, h=HEADS)
        PR = U[:, 3488:5952].rearrange("p (a h k) -> p a h k", a=2, h=HEADS)
        PT = U[0:KEYS, 5952:10048].rearrange("p (a h k) -> p a h k", a=2, h=HEADS)
        OTt = U[:, 10048:10560].rearrange("p (g q) -> p g q", g=4)
        On = U[:, 10560:10688]
        OT = U[:, 10688:10816]
        qT = U[:, 10816:11840].rearrange("p (a q) -> p a q", a=2)
        SELT = U[:, 0:8192].rearrange("p (g e) -> p g e", e=ES)
        LGT = U[:, 8192:8704]
        PERM = U[:, 8704:9216]
        BD = U[:, 9216:10240].rearrange("p (a g e) -> p a g e", a=2, e=ES)
        INN = U[:, 10240:11264].rearrange("p (a i g) -> p a i g", a=2, i=4)
        XA = U[:, 3488:5536].rearrange("p (t n) -> p t n", t=NT)
        XB = U[:, 5536:7584].rearrange("p (r b n) -> p r b n", r=4, b=4)
        XBT = U[:, 7584:9632].rearrange("p (r n) -> p r n", r=4)
        bcmp = U[:, 9632:9952].rearrange("p (b e) -> p b e", e=E1)
        cnt = U[:, 9952:10208].rearrange("p (e n) -> p e n", e=E1)
        zeros = U[:, 3488:3488 + P]
        b2row = SLOT[1][0:1, 0:E1 * D]

        xs = nc.dram_tensor("rows_in", (MAX_ROWS, D), f32).ap()
        ys = nc.dram_tensor("rows_out", (MAX_ROWS, D), f32).ap()
        xs_blocks = xs.rearrange("(b p) d -> p b d", p=P)
        ys_blocks = ys.rearrange("(b p) d -> p b d", p=P)

        PS = [ctx.enter_context(nc.psum_tensor(f"bank{i}", [P, 512], f32)) for i in range(8)]
        bank_full = [sem(f"bank_full{i}") for i in range(8)]
        bank_free = [sem(f"bank_free{i}") for i in range(8)]
        done_before = {1: 0, 3: BLOCKS[1] - GROUPS_OF_BLOCKS[1]}
        turn = {}
        fillings = [0] * 8

        def claim(pe, bank, key):
            if fillings[bank]:
                pe.wait_ge(bank_free[bank], fillings[bank])
            fillings[bank] += 1
            turn[key] = (bank, fillings[bank])
            return PS[bank]

        def full(eng, key):
            b, n = turn[key]
            eng.wait_ge(bank_full[b], n)
            return PS[b]

        def drained(eng, key):
            b, n = turn[key]
            eng.wait_ge(bank_free[b], n)

        def chunk(c):
            return slice(c * SEQ, (c + 1) * SEQ)

        def tile_(t):
            return slice(t * P, (t + 1) * P)

        block = ctx.enter_context(nc.Block())

        @block.tensor
        def _(pe):
            def mm(out_, lhsT, rhs, start=True, stop=True, **kw):
                return nc.tensor.matmul(out_, lhsT, rhs, start=start, stop=stop, **kw)

            def prep_xt(n):
                bank = claim(pe, 7, ("xt", n))
                pe.wait_ge(sem("xn_ready"), n + 1)
                s, c = divmod(n, BATCH)
                for t in range(TPC):
                    src = XA[:, 4 * c + t, :] if layers[s] == (TOPK, 1) else XN[:, n % 2, t, :]
                    last = nc.tensor.transpose(bank[:, tile_(t)], src, ident[:])
                last.then_inc(bank_full[7], 1)

            pe.wait_ge(sem("ident_ready"), 2)
            pe.wait_ge(sem("small_loaded"), 16)
            pe.wait_ge(sem("ones_ready"), 1)
            order = 0
            for l in (0, 3):
                b = order % 6
                bank = claim(pe, b, ("Mk", l))
                mm(bank[:, 0:BK], small(f"waT{l}"), small("ctxT")).then_inc(bank_full[b], 1)
                order += 1
                b = order % 6
                bank = claim(pe, b, ("Vw", l))
                for i in range(BATCH):
                    last = mm(bank[0:KEYS, tile_(i)], small("ctxT")[:, i * KEYS:(i + 1) * KEYS],
                              small(f"wcT{l}")[:, 0:P])
                last.then_inc(bank_full[b], 1)
                order += 1
            for l in (1, 2):
                b = order % 6
                bank = claim(pe, b, ("KT", l))
                mm(bank[:, 0:BK], small(f"wkT{l}"), small("ctxT")).then_inc(bank_full[b], 1)
                order += 1
                b = order % 6
                bank = claim(pe, b, ("Vc", l))
                for i in range(BATCH):
                    mm(bank[0:KEYS, tile_(i)], small("ctxT")[:, i * KEYS:(i + 1) * KEYS],
                       small(f"wvT{l}"), stop=False)
                    last = mm(bank[0:KEYS, tile_(i)], ones_row[:, 0:KEYS], small(f"bv{l}"), start=False)
                last.then_inc(bank_full[b], 1)
                order += 1

            def window_layer(s, l):
                def front(c):
                    n = 4 * s + c
                    prep_xt(n)
                    b = c % 2
                    bank = claim(pe, b, ("sc", s, c))
                    if c == 0:
                        drained(pe, ("Mk", l))
                    drained(pe, ("xt", n))
                    for t in range(TPC):
                        last = mm(bank[:, t * KEYS:(t + 1) * KEYS], XNT[:, tile_(4 * c + t)],
                                  Mk[l][:, c * KEYS:(c + 1) * KEYS])
                    last.then_inc(bank_full[b], 1)

                def back(c):
                    b = 2 + c % 2
                    bank = claim(pe, b, ("eT", s, c))
                    pe.wait_ge(sem(f"probs_ready{s}"), c + 1)
                    for t in range(TPC):
                        last = nc.tensor.transpose(bank[0:KEYS, tile_(t)], sc[:, c % 2, t, :], ident[:])
                    last.then_inc(bank_full[b], 1)
                    b = 4 + c % 2
                    bank = claim(pe, b, ("pre", s, c))
                    if c == 0:
                        drained(pe, ("Vw", l))
                    drained(pe, ("eT", s, c))
                    for t in range(TPC):
                        mm(bank[:, tile_(t)], eT[:, c % 2, tile_(t)], Vw[l][:, c, :], stop=False)
                        last = mm(bank[:, tile_(t)], XNT[:, tile_(4 * c + t)], small(f"wcT{l}")[:, P:2 * P],
                                  start=False)
                    last.then_inc(bank_full[b], 1)

                for c in range(BATCH):
                    front(c)
                    if c:
                        back(c - 1)
                back(BATCH - 1)

            def gated_layer(s):
                def logits(c):
                    bank = claim(pe, 7, ("lg", s, c))
                    drained(pe, ("xt", 4 * s + c))
                    for t in range(TPC):
                        mm(bank[:, t * E0:(t + 1) * E0], XNT[:, tile_(4 * c + t)], small("gw"), stop=False)
                        last = mm(bank[:, t * E0:(t + 1) * E0], ones_row[:], small("gb"), start=False)
                    last.then_inc(bank_full[7], 1)

                def gatesT(c):
                    bank = claim(pe, 7, ("cwT", s, c))
                    pe.wait_ge(sem("cw_ready"), c + 1)
                    for t in range(TPC):
                        last = nc.tensor.transpose(bank[0:E0, tile_(t)], cw[:, c % 2, t, :], ident[:])
                    last.then_inc(bank_full[7], 1)

                def up(c, i):
                    xc = XNT[:, chunk(c)]
                    w1 = SLOT[0][:, i * P:(i + 1) * P] if i < PAIRS else small("sw1")
                    w3 = SLOT[0][:, 2048 + i * P:2048 + (i + 1) * P] if i < PAIRS else small("sw3")
                    b = i % 2
                    mm(claim(pe, b, ("A", c, i))[:], w1, xc).then_inc(bank_full[b], 1)
                    mm(claim(pe, 2 + b, ("C", c, i))[:], w3, xc).then_inc(bank_full[2 + b], 1)
                    if i < PAIRS:
                        mm(claim(pe, 4 + b, ("G", c, i))[:], pairsel[:, i, :], cw3[:, c % 2, :])\
                            .then_inc(bank_full[4 + b], 1)

                def down(c, i):
                    if i == 0:
                        bank = claim(pe, 6, ("oT", c))
                        if c == 0:
                            pe.wait_ge(sem("w2_loaded"), 16)
                        mm(bank[:], small("b2_0"), cwT[:, c % 2, :], stop=False)
                    drained(pe, ("G" if i < PAIRS else "C", c, i))
                    w2 = SLOT[1][:, i * P:(i + 1) * P] if i < PAIRS else small("sw2")
                    last = mm(PS[6][:], w2, H1[:, i % 2, :], start=False, stop=i == PAIRS)
                    last.then_inc(sem("h_used"), 1) if i < PAIRS else last.then_inc(bank_full[6], 1)

                def back(c):
                    bank = claim(pe, 7, ("ob", c))
                    drained(pe, ("oT", c))
                    for t in range(TPC):
                        last = nc.tensor.transpose(bank[:, tile_(t)], outT[:, tile_(t)], ident[:])
                    last.then_inc(bank_full[7], 1)

                prep_xt(4 * s)
                logits(0)
                gatesT(0)
                pe.wait_ge(sem("w13_loaded"), 16)
                for c in range(BATCH):
                    drained(pe, ("cwT", s, c))
                    pe.wait_ge(sem("cw3_ready"), c + 1)
                    for i in range(PAIRS + 1):
                        up(c, i)
                        if i == 2 and c:
                            back(c - 1)
                        if c + 1 < BATCH:
                            if i == 5:
                                prep_xt(4 * s + c + 1)
                            if i == 6:
                                logits(c + 1)
                            if i == 14:
                                gatesT(c + 1)
                        if i:
                            down(c, i - 1)
                    down(c, PAIRS)
                back(BATCH - 1)

            def heads_layer(s, l):
                def query(c):
                    bank = claim(pe, 7, ("q", s, c))
                    drained(pe, ("xt", 4 * s + c))
                    mm(bank[:], small(f"wqT{l}"), XNT[:, chunk(c)]).then_inc(bank_full[7], 1)

                def scores(u):
                    c, t = divmod(u, TPC)
                    if t == 0:
                        drained(pe, ("q", s, c))
                        pe.wait_ge(sem("kbd_ready"), BATCH * (l - 1) + c + 1)
                    if u == 0:
                        pe.wait_ge(sem("delta_ready"), 1)
                    for b, (h0, h1) in enumerate(HEAD_BANKS):
                        bank = claim(pe, b, ("S", s, u, b))
                        n = (h1 - h0) * KEYS
                        mm(bank[:, 0:n], ones96[:],
                           delta3[:, c * KEYS:(c + 1) * KEYS].unsqueeze(1).to_broadcast([96, h1 - h0, KEYS]),
                           stop=False)
                        mm(bank[:, 0:n], qT[:, c % 2, tile_(t)],
                           kbd[:, c % 2, h0:h1, :].rearrange("p h k -> p (h k)"), start=False)\
                            .then_inc(bank_full[b], 1)

                def probsT(u):
                    pe.wait_ge(sem(f"exp_ready{s}"), u + 1)
                    for g in range(4):
                        b = 3 + g % 2
                        bank = claim(pe, b, ("T", s, u, g))
                        for j in range(4):
                            last = nc.tensor.transpose(bank[0:KEYS, tile_(j)], PR[:, u % 2, 4 * g + j, :], ident[:])
                        last.then_inc(bank_full[b], 1)

                def values(u):
                    c = u // TPC
                    bank = claim(pe, 5, ("O", s, u))
                    for g in range(4):
                        drained(pe, ("T", s, u, g))
                        for j in range(4):
                            last = mm(bank[32 * j:32 * j + 32, tile_(g)], vpad[:, c % 2, 4 * g + j, :],
                                      PT[:, u % 2, 4 * g + j, :])
                    last.then_inc(bank_full[5], 1)

                def back_to_tokens(u):
                    bank = claim(pe, 6, ("Ot", s, u))
                    drained(pe, ("O", s, u))
                    for g in range(4):
                        last = nc.tensor.transpose(bank[:, tile_(g)], OTt[:, g, :], ident[:])
                    last.then_inc(bank_full[6], 1)

                def headsT(u):
                    bank = claim(pe, 7, ("OT", s, u))
                    drained(pe, ("Ot", s, u))
                    nc.tensor.transpose(bank[:, 0:P], On, ident[:]).then_inc(bank_full[7], 1)

                def project(u):
                    bank = claim(pe, 7, ("Y", s, u))
                    drained(pe, ("OT", s, u))
                    mm(bank[:, 0:P], OT, small(f"woT{l}"), stop=False)
                    mm(bank[:, 0:P], ones_row[:], small(f"bo{l}"), start=False).then_inc(bank_full[7], 1)

                prep_xt(4 * s)
                query(0)
                for u in range(NT + 4):
                    if u < NT:
                        scores(u)
                    if 2 <= u < NT + 2:
                        values(u - 2)
                    if u >= 4:
                        project(u - 4)
                    if u < NT and u % TPC == 2 and u // TPC + 1 < BATCH:
                        prep_xt(4 * s + u // TPC + 1)
                        query(u // TPC + 1)
                    if 1 <= u < NT + 1:
                        probsT(u - 1)
                    if 3 <= u < NT + 3:
                        headsT(u - 3)
                    if 2 <= u < NT + 2:
                        back_to_tokens(u - 2)

            def topk_layer(s, l):
                w = CHOICES[l] * E1

                def route(c):
                    n = 4 * s + c
                    prep_xt(n)
                    bank = claim(pe, 6, ("rl", s, c))
                    drained(pe, ("xt", n))
                    for t in range(TPC):
                        last = mm(bank[:, t * E1:(t + 1) * E1], XNT[:, tile_(4 * c + t)],
                                  small("rwT" if l == 1 else "wr"), stop=l == 1)
                        if l == 3:
                            last = mm(bank[:, t * E1:(t + 1) * E1], ones_row[:], small("br"), start=False)
                    last.then_inc(bank_full[6], 1)

                def count(c):
                    bank = claim(pe, 5, ("cum", s, c))
                    pe.wait_ge(sem(f"onehot_ready{s}"), c + 1)
                    out_ = bank[:, 0:TPC * w].rearrange("p (t n) -> p t n", t=TPC)
                    mm(out_, tri[:], ohb[:, :, 0:w], stop=False, skip_group_check=True)
                    for t in range(TPC):
                        one = ohb[:, t, 0:w]
                        if t + 1 < TPC:
                            mm(out_[:, t + 1:TPC, :], ones_b[:], one.unsqueeze(1).to_broadcast([P, TPC - 1 - t, w]),
                               start=False, stop=False, skip_group_check=True)
                        last = mm(bank[:, TPC * w:(TPC + 1) * w], ones_b[:], one, start=False,
                                  stop=t == TPC - 1, skip_group_check=True)
                    last.then_inc(bank_full[5], 1)

                def rows_in(g):
                    bank = claim(pe, 7, ("XB", s, g))
                    pe.wait_ge(sem(f"rows_loaded{s}_{g}"), 16)
                    for j in range(4):
                        last = nc.tensor.transpose(bank[:, tile_(j)], XB[:, g % 4, j, :], ident[:])
                    last.then_inc(bank_full[7], 1)

                def up(b):
                    bank = claim(pe, b % 2, ("U", s, b))
                    if b % 4 == 0:
                        drained(pe, ("XB", s, b // 4))
                    mm(bank[:], XBT[:, b // 4 % 4, tile_(b % 4)], SLOT[2][:, bass.ds(columns[b], F1)])\
                        .then_inc(bank_full[b % 2], 1)

                def hiddenT(b):
                    bank = claim(pe, 2 + b % 2, ("HT", s, b))
                    drained(pe, ("U", s, b))
                    for f in range(FC):
                        last = nc.tensor.transpose(bank[:, tile_(f)], HS[:, b % 2, tile_(f)], ident[:])
                    last.then_inc(bank_full[2 + b % 2], 1)

                def down(b):
                    k = 4 + b // 4 % 2
                    bank = claim(pe, k, ("Yd", s, b // 4)) if b % 4 == 0 else PS[k]
                    if l == 3:
                        mm(bank[:, tile_(b % 4)], ones_row[:], b2row[:, bass.ds(b2_columns[b], D)], stop=False)
                        pe.wait_ge(sem("relu_done"), FC * (b + 1))
                    else:
                        drained(pe, ("HT", s, b))
                    for f in range(FC):
                        last = mm(bank[:, tile_(b % 4)], HT[:, b % 2, tile_(f)],
                                  SLOT[3][:, bass.ds(columns[b] + f * P, P)], start=f == 0 and l == 1,
                                  stop=f == FC - 1)
                    last.then_inc(bank_full[k], 1) if b % 4 == 3 or b == BLOCKS[l] - 1 \
                        else last.then_inc(sem("down_done"), 1)

                route(0)
                for c in range(BATCH):
                    if c + 1 < BATCH:
                        route(c + 1)
                    count(c)
                pe.wait_ge(sem(f"up_loaded{l}"), 16)
                pe.wait_ge(sem(f"down_loaded{l}"), 16)
                if l == 3:
                    pe.wait_ge(sem("b2row_loaded"), 16)
                pe.wait_ge(sem(f"offsets_ready{s}"), 1)
                columns, b2_columns = {}, {}
                rows_in(0)
                for b in range(BLOCKS[l] + 2):
                    if b < BLOCKS[l]:
                        columns[b] = pe.value_load(offs[0:1, 0, b:b + 1], min_val=0, max_val=(E1 - 1) * F1)
                        if l == 3:
                            b2_columns[b] = pe.value_load(offs[0:1, 1, b:b + 1], min_val=0, max_val=(E1 - 1) * D)
                        up(b)
                    if b % 4 == 1 and b // 4 + 1 < GROUPS_OF_BLOCKS[l]:
                        rows_in(b // 4 + 1)
                    if 1 <= b <= BLOCKS[l]:
                        hiddenT(b - 1)
                    if b >= 2:
                        down(b - 2)

            def choice_layer(s):
                def front(c):
                    n = 4 * s + c
                    prep_xt(n)
                    b = c % 2
                    bank = claim(pe, b, ("cl", c))
                    drained(pe, ("xt", n))
                    mm(bank[:], small("ctrl"), XNT[:, chunk(c)]).then_inc(bank_full[b], 1)

                def select(c):
                    bank = claim(pe, 2, ("pt", c))
                    pe.wait_ge(sem("perm_ready"), c + 1)
                    for t in range(TPC):
                        last = nc.tensor.transpose(bank[:, t * ES:(t + 1) * ES], PERM[0:ES, tile_(t)],
                                                   ident[0:ES, 0:ES])
                    last.then_inc(bank_full[2], 1)
                    for t in range(TPC):
                        b = 3 + t % 2
                        bank = claim(pe, b, ("sel", c, t))
                        if t < TPC - 1:
                            pe.wait_ge(sem("bd_ready"), c * (TPC - 1) + t + 1)
                        else:
                            drained(pe, ("pt", c))
                        mm(bank[:], XN[:, c % 2, t, :], BD[:, t % 2, :, :].rearrange("p g e -> p (g e)"))\
                            .then_inc(bank_full[b], 1)

                front(0)
                for c in range(BATCH):
                    if c + 1 < BATCH:
                        front(c + 1)
                    select(c)

                pe.wait_ge(sem("f1_loaded"), 16)
                pe.wait_ge(sem("f2_loaded"), 16)
                drained(pe, ("sel", BATCH - 1, 2))
                drained(pe, ("sel", BATCH - 1, 3))

                def up(q):
                    b = q % 2
                    bank = claim(pe, b, ("cu", q))
                    for i in range(4):
                        for h in range(2):
                            e = 8 * q + 2 * i + h
                            last = mm(bank[h * FS:(h + 1) * FS, tile_(i)], SLOT[0][:, e * FS:(e + 1) * FS],
                                      SELT[:, :, e])
                    last.then_inc(bank_full[b], 1)

                def down(q):
                    drained(pe, ("cu", q))
                    for h in range(2):
                        b = 2 + 2 * (q % 2) + h
                        bank = claim(pe, b, ("cd", q, h))
                        for i in range(4):
                            last = mm(bank[:, tile_(i)],
                                      SLOT[1][h * FS:(h + 1) * FS, (4 * q + i) * P:(4 * q + i + 1) * P],
                                      INN[h * FS:(h + 1) * FS, q % 2, i, :])
                        last.then_inc(bank_full[b], 1)

                for q in range(ES // 8):
                    up(q)
                    if q:
                        down(q - 1)
                down(ES // 8 - 1)
                for q in (ES // 8 - 2, ES // 8 - 1):
                    for h in range(2):
                        drained(pe, ("cd", q, h))

                def rows(c, k):
                    b = (4 * c + k) % 2
                    bank = claim(pe, b, ("in", c, k))
                    for j in range(4):
                        g = 32 * c + 8 * k + 2 * j
                        last = nc.tensor.transpose(bank[:, tile_(j)],
                                                   SELT[:, g:g + 2, :].rearrange("p g e -> p (g e)"), ident[:])
                    last.then_inc(bank_full[b], 1)

                def combine(c):
                    b = 2 + c % 2
                    bank = claim(pe, b, ("co", c))
                    pe.wait_ge(sem("pb_ready"), c + 1)
                    for k in range(4):
                        drained(pe, ("in", c, k))
                        for j in range(4):
                            last = mm(bank[32 * j:32 * j + 32, tile_(k)],
                                      XNT[:, c * SEQ + k * P + 32 * j:c * SEQ + k * P + 32 * j + 32],
                                      INTER[:, c % 2, k, tile_(j)])
                    last.then_inc(bank_full[b], 1)

                for c in range(BATCH):
                    for k in range(4):
                        rows(c, k)
                    if c:
                        combine(c - 1)
                combine(BATCH - 1)

            for s, (kind, l) in enumerate(layers):
                if kind == WINDOW_ATT:
                    window_layer(s, l)
                elif kind == GATED:
                    gated_layer(s)
                elif kind == HEADS_ATT:
                    heads_layer(s, l)
                elif kind == TOPK:
                    topk_layer(s, l)
                else:
                    choice_layer(s)

        @block.vector
        def _(dve):
            v = nc.vector
            counted = {}

            def mark(ins, name="dve_step"):
                ins.then_inc(sem(name), 1)
                counted[name] = counted.get(name, 0) + 1
                dve.wait_ge(sem(name), counted[name])

            def free(ins, key):
                b, n = turn[key]
                ins.then_inc(bank_free[b], 1)
                dve.wait_ge(bank_free[b], n)

            mark(v.memset(ones_row[:], 1.0), "ones_ready")
            mark(v.memset(neghalf[:], -0.5), "neghalf_ready")
            mark(v.memset(gs[:], -9.0))
            mark(v.memset(me[:], -9.0))
            mark(v.memset(r8[:], -9.0))
            mark(v.memset(ones_b[:], 1.0))
            mark(v.memset(ones96[:], 1.0))
            mark(v.memset(delta3[:], 0.0))
            dve.wait_ge(sem("iota_done"), 6)
            mark(v.tensor_copy(step128[:], step_i[:]))
            mark(v.tensor_copy(bidx[:], bidx_i[:]))
            mark(v.tensor_copy(idx_f[:], idx_i[:]))
            mark(v.tensor_copy(pidx_f[:], pidx_i[:]))
            mark(v.tensor_copy(desc[:], desc_i[:]))
            mark(v.tensor_scalar(tie[:], tie_i[:], 1e-6 / (GRP - 1), None, ALU.mult))

            def layernorm(src, dst, last_name):
                for t in range(TPC):
                    ins = v.bn_stats(stats[:, t, :], src(t))
                    ins.then_inc(sem("bn_done"), 1)
                counted["bn"] = counted.get("bn", 0) + TPC
                dve.wait_ge(sem("bn_done"), counted["bn"])
                for t in range(TPC):
                    v.bn_aggr(mv[:, t, :], stats[:, t, :]).then_inc(sem("bn_done"), 1)
                counted["bn"] += TPC
                dve.wait_ge(sem("bn_done"), counted["bn"])
                k = counted.get("var_ready", 0)
                mark(v.tensor_scalar(veps[:, k % 2, :], mv[:, :, 1], 1e-5, None, ALU.add), "var_ready")
                dve.wait_ge(sem("rstd_ready"), k + 1)
                for t in range(TPC):
                    ins = v.tensor_scalar(dst(t), src(t), mv[:, t, 0:1], rstd[:, k % 2, t:t + 1],
                                          ALU.subtract, ALU.mult)
                    if t < TPC - 1:
                        ins.then_inc(sem("ln_part"), 1)
                counted["ln_part"] = counted.get("ln_part", 0) + TPC - 1
                mark(ins, last_name)
                dve.wait_ge(sem("ln_part"), counted["ln_part"])

            def kind_of(s):
                return layers[s]

            def combine(s, l, c):
                nk = CHOICES[l]
                for j in range(TPC * nk * c, TPC * nk * (c + 1)):
                    t, k = divmod(j, nk)
                    dve.wait_ge(sem(f"gathered{s}_{j % RING}"), 16 * (j // RING + 1))
                    mark(v.scalar_tensor_tensor(X[:, t, :], YG[:, j % RING, :], GA[:, t, k:k + 1], X[:, t, :],
                                                ALU.mult, ALU.add), f"combined{s}")

            def prep_ln(n):
                s, c = divmod(n, BATCH)
                if s and layers[s - 1][0] == TOPK:
                    combine(s - 1, layers[s - 1][1], c)
                if n < 4:
                    dve.wait_ge(sem(f"x_loaded{n}"), 16)
                if (kind_of(s)) == (TOPK, 1):
                    layernorm(lambda t: X[:, 4 * c + t, :], lambda t: XA[:, 4 * c + t, :], "xn_ready")
                    return
                if n >= 2:
                    full(dve, ("xt", n - 2))
                    kind = layers[(n - 2) // BATCH][0]
                    if kind == CHOICE:
                        full(dve, ("sel", (n - 2) % BATCH, TPC - 1))
                layernorm(lambda t: X[:, 4 * c + t, :], lambda t: XN[:, n % 2, t, :], "xn_ready")

            prep_ln(0)
            dve.wait_ge(sem("small_loaded"), 16)
            dve.wait_ge(sem("lens_loaded"), 16)
            mark(v.tensor_copy(lens_f[:], lens_i[:]))
            mark(v.tensor_scalar(lo_hi[:, 0, :], small("pt"), -WINDOW, 0.0, ALU.add, ALU.max))
            mark(v.tensor_scalar(lo_hi[:, 1, :], small("pt"), WINDOW, None, ALU.add))
            mark(v.tensor_tensor(lo_hi[:, 1, :], lo_hi[:, 1, :], lens_f[:], ALU.min))
            idx_b = idx_f[:].unsqueeze(1).to_broadcast([P, BATCH, KEYS])
            mark(v.tensor_tensor(keep[:], idx_b, lo_hi[:, 0, :].unsqueeze(2).to_broadcast([P, BATCH, KEYS]), ALU.is_ge))
            mark(v.tensor_tensor(neg[:], idx_b, lo_hi[:, 1, :].unsqueeze(2).to_broadcast([P, BATCH, KEYS]), ALU.is_le))
            mark(v.tensor_tensor(keep[:], keep[:], neg[:], ALU.mult))
            mark(v.tensor_scalar(neg[:], keep[:], 1e9, -1e9, ALU.mult, ALU.add))
            mark(v.tensor_scalar(gauss[:], small("pt"), pidx_f[:], None, ALU.subtract))
            mark(v.tensor_tensor(gauss[:], gauss[:], gauss[:], ALU.mult), "dist_ready")
            mark(v.tensor_scalar(tau_s[:], small("tau"), float(DK) ** -0.5, None, ALU.mult))
            mark(v.tensor_scalar(dtmp[:, 0, :], small("delta"), float(DK) ** -0.5, None, ALU.mult))
            mark(v.tensor_copy(delta3[0:1, :], dtmp[:, 0, :]))
            mark(v.tensor_tensor(dtmp[:, 1, :], dtmp[:, 0, :], delta3[0:1, :], ALU.subtract))
            mark(v.tensor_copy(dtb[:], dtmp[:, 1, :]))
            mark(v.tensor_copy(delta3[32:33, :], dtb[:]))
            mark(v.tensor_tensor(dtmp[:, 1, :], dtmp[:, 1, :], dtb[:], ALU.subtract))
            mark(v.tensor_copy(delta3[64:65, :], dtmp[:, 1, :]), "delta_ready")
            dve.wait_ge(sem("gauss_ready"), 1)
            for l in (0, 3):
                bank = full(dve, ("Mk", l))
                free(v.tensor_copy(Mk[l][:], bank[:, 0:BK]), ("Mk", l))
                bank = full(dve, ("Vw", l))
                free(v.tensor_tensor(Vw[l][:], bank[0:KEYS, :].rearrange("p (b n) -> p b n", b=BATCH),
                                     gauss[0:KEYS, :].unsqueeze(2).to_broadcast([KEYS, BATCH, P]), ALU.mult),
                     ("Vw", l))
            for l in (1, 2):
                bank = full(dve, ("KT", l))
                view = bank[:, 0:BK].rearrange("p (b k) -> p b k", b=BATCH)
                tau_b = tau_s[:].unsqueeze(2).to_broadcast([P, BATCH, KEYS])
                free(v.scalar_tensor_tensor(KT[l][:].rearrange("p (b k) -> p b k", b=BATCH), view,
                                            small(f"bk{l}"), tau_b, ALU.add, ALU.mult), ("KT", l))
                bank = full(dve, ("Vc", l))
                free(v.tensor_copy(Vc[l][:], bank[0:KEYS, :].rearrange("p (b n) -> p b n", b=BATCH)), ("Vc", l))

            def window_layer(s, l):
                def masked(c):
                    bank = full(dve, ("sc", s, c))
                    S = sc[:, c % 2]
                    if c >= 2:
                        full(dve, ("eT", s, c - 2))
                    kb = keep[:, c, :].unsqueeze(1).to_broadcast([P, TPC, KEYS])
                    nb = neg[:, c, :].unsqueeze(1).to_broadcast([P, TPC, KEYS])
                    free(v.tensor_tensor(S, bank[:, 0:TPC * KEYS].rearrange("p (t k) -> p t k", t=TPC), kb,
                                         ALU.mult), ("sc", s, c))
                    mark(v.tensor_tensor(S, S, nb, ALU.add))
                    mark(v.tensor_reduce(mx[:, 0:TPC], S, AX, ALU.max))
                    mark(v.tensor_tensor(S, S, mx[:, 0:TPC].unsqueeze(2).to_broadcast([P, TPC, KEYS]),
                                         ALU.subtract), f"masked_ready{s}")

                def normed(c):
                    S = sc[:, c % 2]
                    dve.wait_ge(sem(f"wexp_ready{s}"), c + 1)
                    mark(v.tensor_reduce(red[:, 0:TPC], S, AX, ALU.add))
                    mark(v.reciprocal(red[:, 0:TPC], red[:, 0:TPC]))
                    mark(v.tensor_tensor(S, S, red[:, 0:TPC].unsqueeze(2).to_broadcast([P, TPC, KEYS]), ALU.mult),
                         f"probs_ready{s}")

                def add(c):
                    bank = full(dve, ("pre", s, c))
                    drained(dve, ("pre", s, c))
                    mark(v.tensor_tensor(X[:, 4 * c:4 * c + 4, :], X[:, 4 * c:4 * c + 4, :],
                                         th.rearrange("p (t n) -> p t n", t=TPC), ALU.add), f"x_done{s}")

                if s:
                    prep_ln(4 * s)
                for c in range(BATCH):
                    masked(c)
                    if c + 1 < BATCH:
                        prep_ln(4 * s + c + 1)
                    normed(c)
                    if c:
                        add(c - 1)
                add(BATCH - 1)

            def gated_layer(s):
                def top4(src, dst, w):
                    for t in range(TPC):
                        mark(v.max(v8[:, t, :], src[:, t, 0:w]))
                    mark(v.tensor_copy(r8[:, :, 0:4], v8[:, :, 0:4]))
                    for t in range(TPC):
                        mark(v.match_replace(dst[:, t, :], r8[:, t, :], src[:, t, :], 8.0))

                def route(c):
                    bank = full(dve, ("lg", s, c))
                    view = bank[:, 0:TPC * E0].rearrange("p (t e) -> p t e", t=TPC)
                    mark(v.tensor_reduce(mx[:, 0:TPC], view, AX, ALU.max))
                    free(v.tensor_tensor(s0[:], view, mx[:, 0:TPC].unsqueeze(2).to_broadcast([P, TPC, E0]),
                                         ALU.subtract), ("lg", s, c))

                def choose(c):
                    dve.wait_ge(sem("rexp_ready"), c + 1)
                    mark(v.tensor_reduce(red[:, 0:TPC], s0[:], AX, ALU.add))
                    mark(v.reciprocal(red[:, 0:TPC], red[:, 0:TPC]))
                    mark(v.tensor_tensor(s0[:], s0[:], red[:, 0:TPC].unsqueeze(2).to_broadcast([P, TPC, E0]),
                                         ALU.mult))
                    s4 = s0[:].rearrange("p t (g m) -> p (t g) m", m=4)
                    p6 = pr[:].rearrange("p t g m -> p (t g) m")
                    for a, j, w in ((0, 1, 3), (3, 2, 2), (5, 3, 1)):
                        mark(v.tensor_tensor(p6[:, :, a:a + w], s4[:, :, 0:w], s4[:, :, j:j + w], ALU.add))
                    mark(v.tensor_reduce(gs[:, :, 0:8], pr[:], AX, ALU.max))
                    top4(gs, gk, 8)
                    mark(v.tensor_scalar(pen[:], gk[:, :, 0:8], 8.0, -4.0, ALU.is_lt, ALU.mult))
                    for t in range(TPC):
                        mark(v.tensor_tensor(me[:, t, 0:E0].rearrange("p (g m) -> p g m", m=4),
                                             s0[:, t, :].rearrange("p (g m) -> p g m", m=4),
                                             pen[:, t, :].unsqueeze(2).to_broadcast([P, 8, 4]), ALU.add))
                    top4(me, mk, E0)
                    if c >= 2:
                        full(dve, ("cwT", s, c - 2))
                    mark(v.scalar_tensor_tensor(cw[:, c % 2], mk[:, :, 0:E0], 8.0, s0[:], ALU.is_equal, ALU.mult),
                         "cw_ready")

                def split(c):
                    a = c % 2
                    bank = full(dve, ("cwT", s, c))
                    if c >= 2:
                        full(dve, ("oT", c - 2))
                    free(v.tensor_copy(cwT[:, a, :], bank[0:E0, :]), ("cwT", s, c))
                    mark(v.tensor_copy(cw3[0:32, a, :], cwT[:, a, :]))
                    mark(v.tensor_tensor(cwr, cwT[:, a, :], cw3[0:32, a, :], ALU.subtract))
                    mark(v.tensor_copy(cwm[:], cwr))
                    mark(v.tensor_copy(cw3[32:64, a, :], cwm[:]))
                    mark(v.tensor_tensor(cwr, cwr, cwm[:], ALU.subtract))
                    mark(v.tensor_copy(cw3[64:96, a, :], cwr), "cw3_ready")

                def gate(c, i):
                    k = c * (PAIRS + 1) + i
                    bank = full(dve, ("C", c, i))
                    drained(dve, ("A", c, i))
                    if i >= 2:
                        dve.wait_ge(sem("h_used"), c * PAIRS + i - 1)
                    elif c:
                        full(dve, ("oT", c - 1))
                    b3 = small("b3_0")[:, i:i + 1] if i < PAIRS else small("sb3")
                    h = H1[:, i % 2, :]
                    free(v.scalar_tensor_tensor(T1 if i < PAIRS else h, bank[:], b3, S1[:, k % 2, :],
                                                ALU.add, ALU.mult), ("C", c, i))
                    if i < PAIRS:
                        bank = full(dve, ("G", c, i))
                        free(v.tensor_tensor(h, T1, bank[:], ALU.mult), ("G", c, i))

                def add(c):
                    bank = full(dve, ("ob", c))
                    free(v.tensor_tensor(X[:, 4 * c:4 * c + 4, :], X[:, 4 * c:4 * c + 4, :],
                                         bank[:].rearrange("p (t n) -> p t n", t=TPC), ALU.add), ("ob", c))

                prep_ln(4 * s)
                route(0)
                choose(0)
                split(0)
                for c in range(BATCH):
                    for i in range(PAIRS + 1):
                        if i == 3 and c:
                            add(c - 1)
                        if c + 1 < BATCH:
                            if i == 3:
                                prep_ln(4 * s + c + 1)
                            if i == 7:
                                route(c + 1)
                            if i == 8:
                                choose(c + 1)
                            if i == 15:
                                split(c + 1)
                        gate(c, i)
                add(BATCH - 1)

            def heads_layer(s, l):
                def shifted(u):
                    if u >= 2:
                        full(dve, ("T", s, u - 2, 3))
                    for b, (h0, h1) in enumerate(HEAD_BANKS):
                        bank = full(dve, ("S", s, u, b))
                        view = bank[:, 0:(h1 - h0) * KEYS].rearrange("p (h k) -> p h k", k=KEYS)
                        mark(v.tensor_reduce(mx[:, h0:h1], view, AX, ALU.max))
                        free(v.tensor_tensor(PR[:, u % 2, h0:h1, :], view,
                                             mx[:, h0:h1].unsqueeze(2).to_broadcast([P, h1 - h0, KEYS]),
                                             ALU.subtract), ("S", s, u, b))

                def probsT(u):
                    if u >= 2:
                        full(dve, ("O", s, u - 2))
                    for g in (1, 3):
                        bank = full(dve, ("T", s, u, g))
                        free(v.tensor_copy(PT[:, u % 2, 4 * g:4 * g + 4, :],
                                           bank[0:KEYS, :].rearrange("p (h q) -> p h q", h=4)), ("T", s, u, g))

                def normed(u):
                    bank = full(dve, ("Ot", s, u))
                    view = bank[:].rearrange("p (h r) -> p h r", r=32)
                    mark(v.reciprocal(red[:], view[:, :, DK]))
                    if u:
                        full(dve, ("OT", s, u - 1))
                    free(v.tensor_tensor(On.rearrange("p (h d) -> p h d", h=HEADS), view[:, :, 0:DK],
                                         red[:].unsqueeze(2).to_broadcast([P, HEADS, DK]), ALU.mult),
                         ("Ot", s, u))

                def add(u):
                    bank = full(dve, ("Y", s, u))
                    free(v.tensor_tensor(X[:, u, :], X[:, u, :], bank[:, 0:P], ALU.add), ("Y", s, u))

                dve.wait_ge(sem("zero_stored"), 16)
                prep_ln(4 * s)
                for u in range(NT + 4):
                    if u < NT:
                        shifted(u)
                    if u >= 4:
                        add(u - 4)
                    if u < NT and u % TPC == 1 and u // TPC + 1 < BATCH:
                        prep_ln(4 * s + u // TPC + 1)
                    if 1 <= u < NT + 1:
                        probsT(u - 1)
                    if 2 <= u < NT + 2:
                        normed(u - 2)

            def topk_layer(s, l):
                def route(c):
                    bank = full(dve, ("rl", s, c))
                    view = bank[:, 0:TPC * E1].rearrange("p (t e) -> p t e", t=TPC)
                    mark(v.tensor_reduce(mx[:, 0:TPC], view, AX, ALU.max))
                    free(v.tensor_tensor(pb8[:], view, mx[:, 0:TPC].unsqueeze(2).to_broadcast([P, TPC, E1]),
                                         ALU.subtract), ("rl", s, c))

                def spread(ap):
                    return ap.unsqueeze(2).to_broadcast([P, TPC, E1])

                def largest(src, k):
                    mark(v.tensor_reduce(tv[:, k, :], src, AX, ALU.max))
                    mark(v.tensor_tensor(t8[:], src, spread(tv[:, k, :]), ALU.is_equal))
                    mark(v.tensor_tensor(t8[:], t8[:], desc[:].unsqueeze(1).to_broadcast([P, TPC, E1]), ALU.mult))
                    mark(v.tensor_reduce(red[:, 0:TPC], t8[:], AX, ALU.max))
                    mark(v.tensor_tensor(oh[:, k], t8[:], spread(red[:, 0:TPC]), ALU.is_equal))

                def choose(c):
                    dve.wait_ge(sem(f"rexp_ready{s}"), c + 1)
                    mark(v.tensor_reduce(red[:, 0:TPC], pb8[:], AX, ALU.add))
                    mark(v.reciprocal(red[:, 0:TPC], red[:, 0:TPC]))
                    mark(v.tensor_tensor(pb8[:], pb8[:], spread(red[:, 0:TPC]), ALU.mult))
                    largest(pb8[:], 0)
                    for k in range(nk):
                        if k:
                            mark(v.scalar_tensor_tensor(pb8[:], oh[:, 0], -2.0, pb8[:], ALU.mult, ALU.add))
                            largest(pb8[:], 1)
                        mark(v.tensor_copy(OHA[:, 4 * c:4 * c + 4, k * E1:(k + 1) * E1], oh[:, k]))
                    if c:
                        full(dve, ("cum", s, c - 1))
                    mark(v.tensor_copy(ohb[:, :, 0:w], OHA[:, 4 * c:4 * c + 4, 0:w]), f"onehot_ready{s}")
                    if nk == 1:
                        mark(v.tensor_copy(GA[:, 4 * c:4 * c + 4, 0], tv[:, 0, :]))
                        return
                    mark(v.tensor_tensor(tv[:, 2, :], tv[:, 0, :], tv[:, 1, :], ALU.add))
                    mark(v.reciprocal(tv[:, 2, :], tv[:, 2, :]))
                    for k in range(nk):
                        mark(v.tensor_tensor(GA[:, 4 * c:4 * c + 4, k], tv[:, k, :], tv[:, 2, :], ALU.mult))

                def finish(c):
                    bank = full(dve, ("cum", s, c))
                    mark(v.tensor_tensor(POSA[:, 4 * c:4 * c + 4, 0:w],
                                         bank[:, 0:TPC * w].rearrange("p (t n) -> p t n", t=TPC),
                                         carry[:, 0:w].unsqueeze(1).to_broadcast([P, TPC, w]), ALU.add))
                    free(v.tensor_tensor(carry[:, 0:w], carry[:, 0:w], bank[:, TPC * w:(TPC + 1) * w], ALU.add),
                         ("cum", s, c))

                def norms(c):
                    prep_ln(4 * s + c)
                    if l == 3:
                        layernorm(lambda t: XN[:, (4 * s + c) % 2, t, :], lambda t: XA[:, 4 * c + t, :], "xn2_ready")

                def place():
                    rows_n, blocks_n, before = nblk[:, 0, :], nblk[:, 1, :], nblk[:, 2, :]
                    if nk == 2:
                        mark(v.tensor_tensor(rows_n, carry[:, 0:E1], carry[:, E1:w], ALU.add))
                    else:
                        mark(v.tensor_copy(rows_n, carry[:, 0:E1]))
                    mark(v.tensor_tensor(cnt, rows_n.unsqueeze(2).to_broadcast([P, E1, 32]),
                                         step128[:].unsqueeze(1).to_broadcast([P, E1, 32]), ALU.is_gt))
                    mark(v.tensor_reduce(blocks_n, cnt, AX, ALU.add))
                    mark(v.tensor_tensor(cnt[:, :, 0:E1], lt8[:], blocks_n.unsqueeze(1).to_broadcast([P, E1, E1]),
                                         ALU.mult))
                    mark(v.tensor_reduce(before, cnt[:, :, 0:E1], AX, ALU.add))
                    mark(v.tensor_scalar(base[:, 0:E1], before, float(P), -1.0, ALU.mult, ALU.add))
                    if nk == 2:
                        mark(v.tensor_tensor(base[:, E1:w], base[:, 0:E1], carry[:, 0:E1], ALU.add))
                        mark(v.scalar_tensor_tensor(cnt_all, POSA[:], float(CAPACITY), OHA[:], ALU.is_le, ALU.mult))
                        mark(v.tensor_reduce(slotf[:], cnt_all.rearrange("p t (k e) -> p t k e", k=2), AX, ALU.add))
                        mark(v.tensor_tensor(GA[:], GA[:], slotf[:], ALU.mult))
                    tmp = cnt_all[:, :, 0:w]
                    mark(v.tensor_tensor(tmp, POSA[:, :, 0:w], base[:, 0:w].unsqueeze(1).to_broadcast([P, NT, w]),
                                         ALU.add))
                    mark(v.tensor_tensor(tmp, tmp, OHA[:, :, 0:w], ALU.mult))
                    for k in range(nk):
                        mark(v.tensor_reduce(slotf[:, :, k], tmp[:, :, k * E1:(k + 1) * E1], AX, ALU.add))
                        mark(v.tensor_copy(slots[:, :, k], slotf[:, :, k]), f"slots_ready{s}")
                    mark(v.tensor_tensor(before, before, blocks_n, ALU.add))
                    mark(v.tensor_tensor(bcmp, before.unsqueeze(1).to_broadcast([P, 40, E1]),
                                         bidx[:].unsqueeze(2).to_broadcast([P, 40, E1]), ALU.is_le))
                    mark(v.tensor_reduce(bexp[:], bcmp, AX, ALU.add))
                    mark(v.tensor_scalar(bexp[:], bexp[:], float(E1 - 1), None, ALU.min))
                    mark(v.tensor_scalar(offs[:, 1, :], bexp[:], float(D), None, ALU.mult))
                    mark(v.tensor_scalar(offs[:, 0, :], bexp[:], float(F1), None, ALU.mult), f"offsets_ready{s}")
                    if l == 3:
                        mark(v.tensor_scalar(offs4[:], bexp[:], float(FC), None, ALU.mult))

                def hiddenT(b):
                    if l == 3:
                        column = dve.value_load(offs4[0:1, b:b + 1], min_val=0, max_val=(E1 - 1) * FC)
                    bank = full(dve, ("HT", s, b))
                    if b >= 2:
                        n = b - 2
                        if n % 4 == 3:
                            full(dve, ("Yd", s, n // 4))
                        else:
                            dve.wait_ge(sem("down_done"), done_before[l] + n + 1 - (n + 1) // 4)
                    if l == 1:
                        free(v.tensor_copy(HT[:, b % 2, :], bank[:]), ("HT", s, b))
                        return
                    for f in range(FC):
                        v.tensor_scalar(HT[:, b % 2, tile_(f)], bank[:, tile_(f)],
                                        small("b1_3")[:, bass.ds(column + f, 1)], 0.0, ALU.add, ALU.max)\
                            .then_inc(sem("relu_done"), 1)
                    dve.wait_ge(sem("relu_done"), FC * (b + 1))
                    dve.sem_inc(bank_free[turn[("HT", s, b)][0]], 1)

                nk = CHOICES[l]
                w = nk * E1
                cnt_all = cnt.rearrange("p e n -> p (e n)").rearrange("p (t n) -> p t n", t=NT)
                mark(v.memset(carry[:], 0.0))
                norms(0)
                for c in range(BATCH):
                    if c + 1 < BATCH:
                        norms(c + 1)
                    route(c)
                    choose(c)
                    finish(c)
                place()
                for b in range(BLOCKS[l]):
                    hiddenT(b)

            def choice_layer(s):
                def choose(c):
                    bank = full(dve, ("cl", c))
                    G = SEQ // GRP
                    lg = LGT.rearrange("p (g t) -> p g t", t=GRP)
                    free(v.tensor_tensor(lg, bank[:].rearrange("p (g t) -> p g t", t=GRP),
                                         tie[:].unsqueeze(1).to_broadcast([P, G, GRP]), ALU.add), ("cl", c))
                    mark(v.tensor_reduce(red32[:], lg, AX, ALU.max))
                    if c:
                        full(dve, ("pt", c - 1))
                    mark(v.tensor_tensor(PERM.rearrange("p (g t) -> p g t", t=GRP), lg,
                                         red32[:].unsqueeze(2).to_broadcast([P, G, GRP]), ALU.is_equal),
                         "perm_ready")
                    mark(v.tensor_tensor(XNT[:, chunk(c)].rearrange("p (j m) -> p j m", m=2 * GRP),
                                         PERM.rearrange("p (j m) -> p j m", m=2 * GRP),
                                         parity[:].rearrange("p a t -> p (a t)").unsqueeze(1)
                                         .to_broadcast([P, G // 2, 2 * GRP]), ALU.mult), "pb_ready")

                def blocks(c):
                    bank = full(dve, ("pt", c))
                    for t in range(TPC):
                        k = c * TPC + t
                        if k >= 2:
                            full(dve, ("sel", *divmod(k - 2, TPC)))
                        ins = v.tensor_tensor(BD[:, t % 2], bank[:, t * ES:(t + 1) * ES].unsqueeze(1)
                                              .to_broadcast([P, GPT, ES]),
                                              gmask[:].unsqueeze(2).to_broadcast([P, GPT, ES]), ALU.mult)
                        if t < TPC - 1:
                            mark(ins, "bd_ready")
                    free(ins, ("pt", c))

                prep_ln(4 * s)
                choose(0)
                for c in range(BATCH):
                    if c + 1 < BATCH:
                        prep_ln(4 * s + c + 1)
                    blocks(c)
                    if c + 1 < BATCH:
                        choose(c + 1)
                for q in range(ES // 8):
                    bank = full(dve, ("cd", q, 0))
                    free(v.tensor_copy(SELT[:, :, 8 * q:8 * q + 8:2],
                                       bank[:].rearrange("p (i g) -> p g i", i=4)), ("cd", q, 0))

                def add(c):
                    bank = full(dve, ("co", c))
                    free(v.tensor_tensor(X[:, 4 * c:4 * c + 4, :], X[:, 4 * c:4 * c + 4, :],
                                         bank[:].rearrange("p (t n) -> p t n", t=TPC), ALU.add), ("co", c))

                for c in range(BATCH):
                    if c >= 2:
                        full(dve, ("co", c - 2))
                    for k in (1, 3):
                        bank = full(dve, ("in", c, k))
                        free(v.tensor_copy(INTER[:, c % 2, k, :], bank[:]), ("in", c, k))
                    if c:
                        add(c - 1)
                add(BATCH - 1)

            for s, (kind, l) in enumerate(layers):
                if kind == WINDOW_ATT:
                    window_layer(s, l)
                elif kind == GATED:
                    gated_layer(s)
                elif kind == HEADS_ATT:
                    heads_layer(s, l)
                elif kind == TOPK:
                    topk_layer(s, l)
                else:
                    choice_layer(s)
            if layers[-1][0] == TOPK:
                for c in range(BATCH):
                    combine(len(layers) - 1, layers[-1][1], c)
            else:
                dve.wait_ge(sem("dve_step"), counted["dve_step"])
                v.memset(red[:], 0.0).then_inc(sem("x_final"), 1)

        @block.scalar
        def _(act):
            a = nc.scalar

            def free(ins, key):
                ins.then_inc(bank_free[turn[key][0]], 1)

            def prep_xt(n):
                bank = full(act, ("xt", n))
                free(a.activation(XNT[:, chunk(n % BATCH)], bank[:], ACT.Copy), ("xt", n))

            act.wait_ge(sem("dist_ready"), 1)
            a.activation(gauss[:], gauss[:], ACT.Exp, scale=-1.0 / DEV_POW).then_inc(sem("gauss_ready"), 1)

            def window_layer(s, l):
                def exps(c):
                    act.wait_ge(sem(f"masked_ready{s}"), c + 1)
                    a.activation(sc[:, c % 2], sc[:, c % 2], ACT.Exp).then_inc(sem(f"wexp_ready{s}"), 1)

                def back(c):
                    bank = full(act, ("eT", s, c))
                    if c >= 2:
                        full(act, ("pre", s, c - 2))
                    free(a.activation(eT[:, c % 2, :], bank[0:KEYS, :], ACT.Copy), ("eT", s, c))
                    bank = full(act, ("pre", s, c))
                    if c:
                        act.wait_ge(sem(f"x_done{s}"), c)
                    ins = a.activation(th, bank[:], ACT.Tanh)
                    free(ins, ("pre", s, c))

                for c in range(BATCH):
                    prep_xt(4 * s + c)
                    exps(c)
                    if c:
                        back(c - 1)
                back(BATCH - 1)

            def gated_layer(s):
                def rexp(c):
                    drained(act, ("lg", s, c))
                    a.activation(s0[:], s0[:], ACT.Exp).then_inc(sem("rexp_ready"), 1)

                def silu(c, i):
                    k = c * (PAIRS + 1) + i
                    bank = full(act, ("A", c, i))
                    if k >= 2:
                        drained(act, ("C", *divmod(k - 2, PAIRS + 1)))
                    b1 = small("b1_0")[:, i:i + 1] if i < PAIRS else small("sb1")
                    free(a.activation(S1[:, k % 2, :], bank[:], ACT.Silu, bias=b1), ("A", c, i))

                def leave(c):
                    bank = full(act, ("oT", c))
                    if c:
                        full(act, ("ob", c - 1))
                    free(a.activation(outT, bank[:], ACT.Identity, bias=small("sb2")), ("oT", c))

                prep_xt(4 * s)
                rexp(0)
                for c in range(BATCH):
                    for i in range(PAIRS + 1):
                        if i == 1 and c:
                            leave(c - 1)
                        silu(c, i)
                        if c + 1 < BATCH:
                            if i == 5:
                                prep_xt(4 * s + c + 1)
                            if i == 6:
                                rexp(c + 1)
                leave(BATCH - 1)

            def heads_layer(s, l):
                def query(c):
                    bank = full(act, ("q", s, c))
                    free(a.activation(qT[:, c % 2, :], bank[:], ACT.Identity, bias=small(f"bq{l}")), ("q", s, c))

                def heads_out(u):
                    bank = full(act, ("O", s, u))
                    if u:
                        full(act, ("Ot", s, u - 1))
                    free(a.activation(OTt, bank[:].rearrange("p (g q) -> p g q", g=4), ACT.Copy), ("O", s, u))

                def probsT(u):
                    if u >= 2:
                        full(act, ("O", s, u - 2))
                    for g in (0, 2):
                        bank = full(act, ("T", s, u, g))
                        free(a.activation(PT[:, u % 2, 4 * g:4 * g + 4, :],
                                          bank[0:KEYS, :].rearrange("p (h q) -> p h q", h=4), ACT.Copy),
                             ("T", s, u, g))

                def exps(u):
                    for b in range(3):
                        drained(act, ("S", s, u, b))
                    a.activation(PR[:, u % 2], PR[:, u % 2], ACT.Exp).then_inc(sem(f"exp_ready{s}"), 1)

                def headsT(u):
                    bank = full(act, ("OT", s, u))
                    if u:
                        full(act, ("Y", s, u - 1))
                    free(a.activation(OT, bank[:, 0:P], ACT.Copy), ("OT", s, u))

                prep_xt(4 * s)
                query(0)
                for u in range(NT + 4):
                    if 2 <= u < NT + 2:
                        heads_out(u - 2)
                    if u < NT and u % TPC == 2 and u // TPC + 1 < BATCH:
                        prep_xt(4 * s + u // TPC + 1)
                        query(u // TPC + 1)
                    if 1 <= u < NT + 1:
                        probsT(u - 1)
                    if u < NT:
                        exps(u)
                    if 3 <= u < NT + 3:
                        headsT(u - 3)

            def topk_layer(s, l):
                def exps(c):
                    drained(act, ("rl", s, c))
                    a.activation(pb8[:], pb8[:], ACT.Exp).then_inc(sem(f"rexp_ready{s}"), 1)

                def rows_in(g):
                    bank = full(act, ("XB", s, g))
                    if g >= 4:
                        full(act, ("U", s, 4 * (g - 4) + 3))
                    if l == 1:
                        ins = a.activation(XBT[:, g % 4, :], bank[:], ACT.Copy)
                    else:
                        ins = a.activation(XBT[:, g % 4, :], bank[:], ACT.Identity, bias=small("lnb"),
                                           scale=small("lng"))
                    free(ins, ("XB", s, g))

                def hidden(b):
                    bank = full(act, ("U", s, b))
                    if b >= 2:
                        full(act, ("HT", s, b - 2))
                    free(a.activation(HS[:, b % 2, :], bank[:], ACT.Gelu if l == 1 else ACT.Copy), ("U", s, b))

                def results(g):
                    bank = full(act, ("Yd", s, g))
                    if g >= 2:
                        act.wait_ge(sem(f"rows_stored{s}_{g % 2}"), 16 * (g // 2))
                    n = min(4, BLOCKS[l] - 4 * g) * P
                    free(a.activation(YB[:, g % 2, 0:n], bank[:, 0:n], ACT.Copy), ("Yd", s, g))

                prep_xt(4 * s)
                for c in range(BATCH):
                    if c + 1 < BATCH:
                        prep_xt(4 * s + c + 1)
                    exps(c)
                rows_in(0)
                for b in range(BLOCKS[l] + 3):
                    if b < BLOCKS[l]:
                        hidden(b)
                    if b % 4 == 1 and b // 4 + 1 < GROUPS_OF_BLOCKS[l]:
                        rows_in(b // 4 + 1)
                    if b >= 3 and (b - 3 == BLOCKS[l] - 1 or (b - 3) % 4 == 3):
                        results((b - 3) // 4)

            def choice_layer(s):
                def select(c):
                    for t in range(TPC):
                        bank = full(act, ("sel", c, t))
                        if c == 0 and t == 0 and s:
                            drained(act, ("Y", s - 1, NT - 1))
                        g = (TPC * c + t) * GPT
                        free(a.activation(SELT[:, g:g + GPT, :],
                                          bank[:].rearrange("p (g e) -> p g e", g=GPT), ACT.Copy), ("sel", c, t))

                prep_xt(4 * s)
                for c in range(BATCH):
                    if c + 1 < BATCH:
                        prep_xt(4 * s + c + 1)
                    select(c)

                def hidden(q):
                    bank = full(act, ("cu", q))
                    if q >= 2:
                        for h in range(2):
                            full(act, ("cd", q - 2, h))
                    for i in range(4):
                        ins = a.activation(INN[:, q % 2, i, :], bank[:, tile_(i)], ACT.Relu,
                                           bias=small("bias2")[:, 4 * q + i:4 * q + i + 1])
                        if i < 3:
                            ins.then_inc(sem("inner_part"), 1)
                    free(ins, ("cu", q))

                def leave(q):
                    bank = full(act, ("cd", q, 1))
                    free(a.activation(SELT[:, :, 8 * q + 1:8 * q + 8:2],
                                      bank[:].rearrange("p (i g) -> p g i", i=4), ACT.Copy), ("cd", q, 1))

                for q in range(ES // 8):
                    hidden(q)
                    if q:
                        leave(q - 1)
                leave(ES // 8 - 1)
                for c in range(BATCH):
                    if c >= 2:
                        full(act, ("co", c - 2))
                    for k in (0, 2):
                        bank = full(act, ("in", c, k))
                        free(a.activation(INTER[:, c % 2, k, :], bank[:], ACT.Copy), ("in", c, k))

            for s, (kind, l) in enumerate(layers):
                if kind == WINDOW_ATT:
                    window_layer(s, l)
                elif kind == GATED:
                    gated_layer(s)
                elif kind == HEADS_ATT:
                    heads_layer(s, l)
                elif kind == TOPK:
                    topk_layer(s, l)
                else:
                    choice_layer(s)

        @block.gpsimd
        def _(pool):
            g = nc.gpsimd
            counted = [0]

            def mark(ins):
                ins.then_inc(sem("pool_step"), 1)
                counted[0] += 1
                pool.wait_ge(sem("pool_step"), counted[0])

            powers = [0]

            def power():
                k = powers[0]
                powers[0] += 1
                pool.wait_ge(sem("var_ready"), k + 1)
                g.tensor_tensor(rstd[:, k % 2, :], veps[:, k % 2, :], neghalf[:], ALU.pow)\
                    .then_inc(sem("rstd_ready"), 1)

            g.iota(idx_i[:], [[1, KEYS]], base=0, channel_multiplier=0).then_inc(sem("iota_done"), 1)
            g.iota(pidx_i[:], [[0, 1]], base=0, channel_multiplier=1).then_inc(sem("iota_done"), 1)
            g.iota(desc_i[:], [[-1, E1]], base=E1, channel_multiplier=0).then_inc(sem("iota_done"), 1)
            g.iota(tie_i[:], [[1, GRP]], base=0, channel_multiplier=0).then_inc(sem("iota_done"), 1)
            g.iota(step_i[:], [[P, 32]], base=0, channel_multiplier=0).then_inc(sem("iota_done"), 1)
            g.iota(bidx_i[:], [[1, 40]], base=0, channel_multiplier=0).then_inc(sem("iota_done"), 1)
            g.memset(ident[:], 0.0).then_inc(sem("ident_ready"), 1)
            pool.wait_ge(sem("ident_ready"), 1)
            g.affine_select(out=ident[:], in_=ident[:], compare_op=ALU.not_equal, fill=1.0, base=0,
                            pattern=[[-1, P]], channel_multiplier=1).then_inc(sem("ident_ready"), 1)
            pool.wait_ge(sem("neghalf_ready"), 1)
            power()
            for m, w, n in ((headmask, DK, HEADS), (gmask, GRP, GPT)):
                mark(g.memset(m[:], 1.0))
                mark(g.affine_select(out=m[:], in_=m[:], compare_op=ALU.is_ge, fill=0.0, base=0,
                                     pattern=[[-w, n]], channel_multiplier=1))
                mark(g.affine_select(out=m[:], in_=m[:], compare_op=ALU.is_ge, fill=0.0, base=w - 1,
                                     pattern=[[w, n]], channel_multiplier=-1))
            mark(g.memset(tri[:], 1.0))
            mark(g.affine_select(out=tri[:], in_=tri[:], compare_op=ALU.is_ge, fill=0.0, base=0,
                                 pattern=[[1, P]], channel_multiplier=-1))
            mark(g.memset(lt8[:], 1.0))
            mark(g.affine_select(out=lt8[:], in_=lt8[:], compare_op=ALU.is_gt, fill=0.0, base=0,
                                 pattern=[[1, E1], [-1, E1]], channel_multiplier=0))
            g.memset(zeros, 0.0).then_inc(sem("zeros_ready"), 1)
            mark(g.memset(parity[:], 1.0))
            mark(g.memset(parity[0:ES, 1, :], 0.0))
            mark(g.memset(parity[ES:P, 0, :], 0.0))
            mark(g.memset(pairsel[:], 0.0))
            for k in range(3):
                m = pairsel[32 * k:32 * k + 32, :, :].rearrange("p i (h f) -> p i h f", h=2)
                mark(g.affine_select(out=m, in_=m, compare_op=ALU.not_equal, fill=1.0, base=0,
                                     pattern=[[-2, PAIRS], [-1, 2], [0, F0]], channel_multiplier=1))
            mark(g.memset(vpad[:], 0.0))
            mark(g.memset(vpad[:, :, :, DK:DK + 1], 1.0))
            g.memset(cwm[:], 0.0).then_inc(sem("pool_consts"), 1)

            def operands(s, l, c):
                if c >= 2:
                    full(pool, ("S", s, TPC * (c - 2) + TPC - 1, 2))
                    full(pool, ("O", s, TPC * (c - 2) + TPC - 1))
                g.tensor_copy(vpad[:, c % 2, :, 0:DK], Vc[l][:, c, :].rearrange("p (h d) -> p h d", h=HEADS))\
                    .then_inc(sem("vpad_ready"), 1)
                g.tensor_tensor(kbd[:, c % 2], KT[l][:, c * KEYS:(c + 1) * KEYS].unsqueeze(1)
                                .to_broadcast([P, HEADS, KEYS]),
                                headmask[:].unsqueeze(2).to_broadcast([P, HEADS, KEYS]), ALU.mult)\
                    .then_inc(sem("kbd_ready"), 1)

            def gather(s, l, c):
                nk = CHOICES[l]
                for j in range(TPC * nk * c, TPC * nk * (c + 1)):
                    t, k = divmod(j, nk)
                    if j >= RING:
                        pool.wait_ge(sem(f"combined{s}"), j - RING + 1)
                    g.indirect_dma_start(YG[:, j % RING, :], None, ys[0:BLOCKS[l] * P, :],
                                         bass.IndirectOffsetOnAxis(ap=slots[:, t, k:k + 1].bitcast(u32), axis=0))\
                        .then_inc(sem(f"gathered{s}_{j % RING}"), 16)

            for s, (kind, l) in enumerate(layers):
                after_topk = s > 0 and layers[s - 1][0] == TOPK
                if kind == HEADS_ATT:
                    if after_topk:
                        gather(s - 1, layers[s - 1][1], 0)
                    power()
                    drained(pool, ("KT", l))
                    drained(pool, ("Vc", l))
                    operands(s, l, 0)
                    operands(s, l, 1)
                    for c in range(1, BATCH):
                        if after_topk and c == 1:
                            gather(s - 1, layers[s - 1][1], 1)
                        power()
                        if after_topk and c + 1 < BATCH:
                            gather(s - 1, layers[s - 1][1], c + 1)
                        if c + 1 < BATCH:
                            operands(s, l, c + 1)
                elif kind != TOPK:
                    for _k in range(BATCH - (s == 0)):
                        power()
                else:
                    for _k in range(BATCH * (2 if l == 3 else 1)):
                        power()
                    nk = CHOICES[l]
                    pool.wait_ge(sem(f"slots_ready{s}"), nk)
                    pool.wait_ge(sem("zero_stored"), 16)
                    for j in range(NT * nk):
                        t, k = divmod(j, nk)
                        g.indirect_dma_start(xs[0:BLOCKS[l] * P, :], bass.IndirectOffsetOnAxis(ap=slots[:, t, k:k + 1].bitcast(u32), axis=0),
                                             XA[:, t, :], None).then_inc(sem(f"scattered{s}"), 16)
                    for h in range(2):
                        pool.wait_ge(sem(f"rows_stored{s}_{h}"), 16 * ((GROUPS_OF_BLOCKS[l] + 1 - h) // 2))
                    if s == len(layers) - 1:
                        for c in range(BATCH):
                            gather(s, l, c)

        @block.sync
        def _(sp):
            sp.dma_start(X[:, 0:4, :], x_in[:, 0:4, :]).then_inc(sem("x_loaded0"), 16)
            sp.dma_start(SM[:], small_in).then_inc(sem("small_loaded"), 16)
            sp.dma_start(lens_i[:], lens_in).then_inc(sem("lens_loaded"), 16)
            for c in range(1, BATCH):
                sp.dma_start(X[:, 4 * c:4 * c + 4, :], x_in[:, 4 * c:4 * c + 4, :]).then_inc(sem(f"x_loaded{c}"), 16)
            sp.dma_start(SLOT[0][:], w13_in).then_inc(sem("w13_loaded"), 16)
            sp.dma_start(SLOT[1][:, 0:2048], w2_in).then_inc(sem("w2_loaded"), 16)
            sp.dma_start(SLOT[2][:], l1w1_in).then_inc(sem("up_loaded1"), 16)
            sp.dma_start(SLOT[3][:], l1w2_in).then_inc(sem("down_loaded1"), 16)
            if len(layers) > 2:
                sp.wait_ge(sem("zeros_ready"), 1)
                sp.dma_start(xs_blocks, zeros.unsqueeze(1).to_broadcast([P, MAX_ROWS // P, D]))\
                    .then_inc(sem("zero_stored"), 16)

            def move_rows(s, l):
                n_groups = GROUPS_OF_BLOCKS[l]

                def load(g):
                    if g >= 4:
                        full(sp, ("XB", s, g - 4))
                    sp.dma_start(XB[:, g % 4], xs_blocks[:, 4 * g:4 * g + 4, :])\
                        .then_inc(sem(f"rows_loaded{s}_{g}"), 16)

                sp.wait_ge(sem(f"scattered{s}"), 16 * NT * CHOICES[l])
                for g in range(min(4, n_groups)):
                    load(g)
                for g in range(n_groups):
                    n = min(4, BLOCKS[l] - 4 * g)
                    drained(sp, ("Yd", s, g))
                    sp.dma_start(ys_blocks[:, 4 * g:4 * g + n, :],
                                 YB[:, g % 2, 0:n * P].rearrange("p (b d) -> p b d", d=D))\
                        .then_inc(sem(f"rows_stored{s}_{g % 2}"), 16)
                    if g + 4 < n_groups:
                        load(g + 4)

            if len(layers) > 5:
                full(sp, ("oT", BATCH - 1))
                sp.dma_start(SLOT[0][:], f1_in).then_inc(sem("f1_loaded"), 16)
                sp.dma_start(SLOT[1][:], f2_in).then_inc(sem("f2_loaded"), 16)
            if len(layers) > 3:
                move_rows(3, 1)
            if len(layers) > 7:
                sp.dma_start(SLOT[2][:], l3w1_in).then_inc(sem("up_loaded3"), 16)
                sp.dma_start(SLOT[3][:], l3w2_in).then_inc(sem("down_loaded3"), 16)
                full(sp, ("cd", ES // 8 - 1, 1))
                sp.dma_start(b2row, b2row_in).then_inc(sem("b2row_loaded"), 16)
                move_rows(7, 3)
            last = len(layers) - 1
            for c in range(BATCH):
                if layers[last][0] == TOPK:
                    sp.wait_ge(sem(f"combined{last}"), TPC * CHOICES[layers[last][1]] * (c + 1))
                else:
                    sp.wait_ge(sem("x_final"), 1)
                sp.dma_start(out[:, 4 * c:4 * c + 4, :], X[:, 4 * c:4 * c + 4, :]).then_inc(sem("stored"), 16)
            sp.wait_ge(sem("stored"), 16 * BATCH)


def layout(a):
    def pack(name):
        _, r, c = OFFSET[name]
        src = small_sources[name]()
        return np.broadcast_to(src, (r, c))

    def t(n):
        return a[n].T

    small_sources = {
        "ctxT": lambda: a["ctx_1024"].transpose(2, 0, 1).reshape(P, BK),
        "pt": lambda: a["condB_pt"][None, :], "tau": lambda: a["condB_tau"][None, :],
        "delta": lambda: a["fside_BxS2_0"].reshape(1, BK),
        "gw": lambda: a["L0_ffn_gw"], "gb": lambda: a["L0_ffn_gb"][None, :],
        "b1_0": lambda: a["L0_ffn_b1"].reshape(PAIRS, P).T, "b3_0": lambda: a["L0_ffn_b3"].reshape(PAIRS, P).T,
        "b2_0": lambda: a["L0_ffn_b2"], "sw1": lambda: a["L0_ffn_sw1"], "sw3": lambda: a["L0_ffn_sw3"],
        "sw2": lambda: a["L0_ffn_sw2"], "sb1": lambda: a["L0_ffn_sb1"][:, None],
        "sb3": lambda: a["L0_ffn_sb3"][:, None], "sb2": lambda: a["L0_ffn_sb2"][:, None],
        "rwT": lambda: t("L1_ffn_router_w"),
        "ctrl": lambda: np.concatenate([a["L2_ffn_controller"].reshape(D, ES)] * 2, axis=1),
        "bias2": lambda: a["L2_ffn_bias"].reshape(ES // 2, P).T,
        "wr": lambda: a["L3_ffn_Wr"], "br": lambda: a["L3_ffn_br"][None, :],
        "b1_3": lambda: a["L3_ffn_b1"].reshape(E1 * FC, P).T, 
        "lng": lambda: a["L3_ffn_ln_g"][:, None], "lnb": lambda: a["L3_ffn_ln_b"][:, None],
    }
    for l in (0, 3):
        small_sources[f"waT{l}"] = lambda l=l: t(f"L{l}_xcond_W_a")
        small_sources[f"wcT{l}"] = lambda l=l: np.concatenate(
            [t(f"L{l}_xcond_W_c")[0:P], t(f"L{l}_xcond_W_c")[P:2 * P]], axis=1)
    for l in (1, 2):
        for n in "qkvo":
            small_sources[f"w{n}T{l}"] = lambda l=l, n=n: t(f"L{l}_xcond_W{n}")
        for n in "qk":
            small_sources[f"b{n}{l}"] = lambda l=l, n=n: a[f"L{l}_xcond_b{n}"][:, None]
        for n in "vo":
            small_sources[f"b{n}{l}"] = lambda l=l, n=n: a[f"L{l}_xcond_b{n}"][None, :]
    smalls = np.zeros((P, SMALL_COLS), np.float32)
    for name, r, c in SMALL:
        at = OFFSET[name][0]
        smalls[0:r, at:at + c] = pack(name)

    def up(w):
        return w.transpose(1, 0, 2).reshape(P, -1)

    def down(w):
        return w.reshape(-1, P, D).transpose(1, 0, 2).reshape(P, -1)

    return {
        "x": a["x"].reshape(NT, P, D).transpose(1, 0, 2),
        "small": smalls,
        "lens": np.broadcast_to(a["_lenS2"][None, :], (P, BATCH)),
        "w13": np.concatenate([up(a["L0_ffn_w1"]), up(a["L0_ffn_w3"])], axis=1),
        "w2": down(a["L0_ffn_w2"]),
        "l1w1": up(a["L1_ffn_w1"]), "l1w2": down(a["L1_ffn_w2"]),
        "f1": a["L2_ffn_f1"].reshape(D, ES * FS), "f2": down(a["L2_ffn_f2"]),
        "l3w1": up(a["L3_ffn_W1"]), "l3w2": down(a["L3_ffn_W2"]),
        "b2row": a["L3_ffn_b2"].reshape(1, E1 * D),
    }


def kernel(**inputs):
    import concourse.bacc as bacc
    from concourse.bass_utils import run_bass_kernel_spmd

    arrays = {n: np.ascontiguousarray(v) for n, v in layout({n: np.asarray(v) for n, v in inputs.items()}).items()}
    nc = bacc.Bacc("TRN2", target_bir_lowering=False, num_devices=1)
    args = [nc.dram_tensor(n, v.shape, mybir.dt.from_np(v.dtype), kind="ExternalInput").ap()
            for n, v in arrays.items()]
    args.append(nc.dram_tensor("y", (P, NT, D), mybir.dt.float32, kind="ExternalOutput").ap())
    build(nc, *args)
    result = run_bass_kernel_spmd(nc, [arrays], core_ids=[0])
    return result.results[0]["y"].transpose(1, 0, 2).reshape(BATCH, SEQ, D)
```

```python
import numpy as np
from contextlib import ExitStack

import concourse.bass as bass
from concourse import mybir

BATCH, SEQ, D, KEYS = 4, 512, 128, 77
P = 128
TPC = SEQ // P
NT = BATCH * TPC
E0, F0 = 32, 64
PAIRS = E0 // 2
E1, F1 = 8, 512
FC = F1 // P
HEADS, DK = 16, 8
ES, FS, GRP = 64, 64, 16
GPT = P // GRP
NG = NT * GPT
CHOICES = {1: 2, 3: 1}
BLOCKS = {l: NT * k + E1 - 1 for l, k in CHOICES.items()}
GROUPS_OF_BLOCKS = {l: -(-b // 4) for l, b in BLOCKS.items()}
MAX_ROWS = 4 * max(GROUPS_OF_BLOCKS.values()) * P
REGION = NT * P
RING = 8
CAPACITY = max(1, int(1.25 * BATCH * SEQ / E1 * 2))
WINDOW, DEV_POW = 16.0, 128.0
BK = BATCH * KEYS

SMALL = [("ctxT", P, BK), ("pt", P, BATCH), ("tau", P, BATCH), ("delta", 1, BK)]
for _l in (0, 3):
    SMALL += [(f"waT{_l}", P, P), (f"wcT{_l}", P, 2 * P)]
for _l in (1, 2):
    SMALL += [(f"w{_n}T{_l}", P, P) for _n in "qkvo"]
    SMALL += [(f"b{_n}{_l}", P, 1) for _n in "qk"] + [(f"b{_n}{_l}", 1, P) for _n in "vo"]
SMALL += [("gw", P, E0), ("gb", 1, E0), ("b1_0", P, PAIRS), ("b3_0", P, PAIRS), ("b2_0", E0, P),
          ("sw1", P, P), ("sw3", P, P), ("sw2", P, P), ("sb1", P, 1), ("sb3", P, 1), ("sb2", P, 1),
          ("rwT", P, E1), ("ctrl", P, 2 * ES), ("bias2", P, ES // 2), ("wr", P, E1), ("br", 1, E1),
          ("b1_3", P, E1 * FC), ("lng", P, 1), ("lnb", P, 1)]
OFFSET, _at = {}, 0
for _n, _r, _c in SMALL:
    OFFSET[_n] = (_at, _r, _c)
    _at += _c
SMALL_COLS = _at

WINDOW_ATT, GATED, HEADS_ATT, TOPK, CHOICE = range(5)
LAYERS = [(WINDOW_ATT, 0), (GATED, 0), (HEADS_ATT, 1), (TOPK, 1), (HEADS_ATT, 2), (CHOICE, 2),
          (WINDOW_ATT, 3), (TOPK, 3)]
NEXT_CHUNK_AT = (1, 4, 8)
NORMS_AT = (10, 13, 16, 19)
LOGITS_AT, SHIFT_AT, CHOOSE_AT, FINISH_AT = (tuple(u + k for u in NORMS_AT) for k in (1, 2, 3, 4))
CHOICE_NORMS_AT, CHOICE_TURN_AT = (12, 16), (13, 17)
HEAD_BANKS = [(0, 6), (6, 11), (11, 16)]


def build(nc, x_in, small_in, lens_in, w13_in, w2_in, l1w1_in, l1w2_in, f1_in, f2_in, l3w1_in,
          l3w2_in, b2row_in, out, n_layers=len(LAYERS)):
    f32, bf16, i32, u32 = mybir.dt.float32, mybir.dt.bfloat16, mybir.dt.int32, mybir.dt.uint32
    ALU, ACT, AX = mybir.AluOpType, mybir.ActivationFunctionType, mybir.AxisListType.X
    layers = LAYERS[:n_layers]
    ctx = ExitStack()
    with ctx:
        def sb(name, shape, dt=f32):
            return ctx.enter_context(nc.sbuf_tensor(name, shape, dt))

        sems = {}

        def sem(name):
            if name not in sems:
                sems[name] = ctx.enter_context(nc.semaphore(name))
            return sems[name]

        X = sb("X", [P, NT, D])
        XN = sb("XN", [P, 2, TPC, D])
        XNT = sb("XNT", [P, NT * P])
        SM = sb("SM", [P, SMALL_COLS])
        SLOT = [sb(f"SLOT{i}", [P, 4096]) for i in range(4)]
        ident = sb("ident", [P, P])
        lens_i = sb("lens_i", [P, BATCH], i32)

        def small(name):
            at, r, c = OFFSET[name]
            return SM[0:r, at:at + c]

        ones_row = sb("ones_row", [1, P])
        idx_i = sb("idx_i", [P, KEYS], i32)
        idx_f = sb("idx_f", [P, KEYS])
        pidx_i = sb("pidx_i", [P, 1], i32)
        pidx_f = sb("pidx_f", [P, 1])
        lens_f = sb("lens_f", [P, BATCH])
        lo_hi = sb("lo_hi", [P, 2, BATCH])
        keep = sb("keep", [P, BATCH, KEYS])
        neg = sb("neg", [P, BATCH, KEYS])
        gauss = sb("gauss", [P, BATCH])
        tau_s = sb("tau_s", [P, BATCH])
        headmask = sb("headmask", [P, HEADS])
        pairsel = sb("pairsel", [96, PAIRS, P], bf16)
        ones96 = sb("ones96", [96, P], bf16)
        delta3 = sb("delta3", [96, BK], bf16)
        dtmp = sb("dtmp", [1, 2, BK])
        dtb = sb("dtb", [1, BK], bf16)
        tri = sb("tri", [P, P], bf16)
        ones_b = sb("ones_b", [P, P], bf16)
        desc = sb("desc", [P, E1])
        desc_i = sb("desc_i", [P, E1], i32)
        tie_i = sb("tie_i", [P, GRP], i32)
        tie = sb("tie", [P, GRP])
        gmask = sb("gmask", [P, GPT])
        parity = sb("parity", [P, 2, GRP])
        neghalf = sb("neghalf", [P, TPC])

        stats = sb("stats", [P, TPC, 6])
        mv = sb("mv", [P, TPC, 2])
        veps = sb("veps", [P, 2, TPC])
        rstd = sb("rstd", [P, 2, TPC])
        mx = sb("mx", [P, HEADS])
        red = sb("red", [P, HEADS])

        Mk = {l: sb(f"Mk{l}", [P, BK]) for l in (0, 3)}
        Vw = {l: sb(f"Vw{l}", [KEYS, BATCH, P]) for l in (0, 3)}
        KT = {l: sb(f"KT{l}", [P, BK]) for l in (1, 2)}
        Vc = {l: sb(f"Vc{l}", [KEYS, BATCH, P]) for l in (1, 2)}

        sc = sb("sc", [P, 2, TPC, KEYS])
        eT = sb("eT", [KEYS, 2, SEQ])
        red32 = sb("red32", [P, SEQ // GRP])
        SHARE = sb("SHARE", [P, 4352])
        S1 = SHARE[:, 0:1024].rearrange("p (a n) -> p a n", a=2)
        H1 = SHARE[:, 1024:2048].rearrange("p (a n) -> p a n", a=2)
        th = SHARE[:, 2560:3072]
        T1 = SHARE[:, 2048:2560]
        outT = SHARE[:, 2560:3072]
        cwT = SHARE[0:E0, 3072:4096].rearrange("p (a n) -> p a n", a=2)
        HS = SHARE[:, 0:1024].rearrange("p (a n) -> p a n", a=2)
        HT = SHARE[:, 1024:2048].rearrange("p (a n) -> p a n", a=2)
        YG = SHARE[:, 2048:3072].rearrange("p (r n) -> p r n", r=RING)
        YB = SHARE[:, 3072:4096].rearrange("p (a n) -> p a n", a=2)
        INTER = SHARE[:, 0:4096].rearrange("p (a f n) -> p a f n", a=2, f=4)
        cw3 = sb("cw3", [96, 2, SEQ], bf16)
        cwm = sb("cwm", [E0, SEQ], bf16)
        s0 = sb("s0", [P, TPC, E0])
        pr = sb("pr", [P, TPC, 8, 6])
        gs = sb("gs", [P, TPC, 12])
        gk = sb("gk", [P, TPC, 12])
        pen = sb("pen", [P, TPC, 8])
        me = sb("me", [P, TPC, 36])
        mk = sb("mk", [P, TPC, 36])
        v8 = sb("v8", [P, TPC, 8])
        r8 = sb("r8", [P, TPC, 8])
        cw = sb("cw", [P, 2, TPC, E0])
        pb8 = sb("pb8", [P, TPC, E1])
        t8 = sb("t8", [P, TPC, E1])
        oh = sb("oh", [P, 2, TPC, E1])
        ohb = sb("ohb", [P, TPC, 2 * E1], bf16)
        tv = sb("tv", [P, 3, TPC])
        OHA = sb("OHA", [P, NT, 2 * E1])
        POSA = sb("POSA", [P, NT, 2 * E1])
        GA = sb("GA", [P, NT, 2])
        carry = sb("carry", [P, 2 * E1])
        nblk = sb("nblk", [P, 3, E1])
        base = sb("base", [P, E1])
        region_i = sb("region_i", [P, E1], i32)
        region = sb("region", [P, E1])
        step_i = sb("step_i", [P, 32], i32)
        step128 = sb("step128", [P, 32])
        lt8 = sb("lt8", [P, E1, E1])
        bidx_i = sb("bidx_i", [P, 40], i32)
        bidx = sb("bidx", [P, 40])
        bexp = sb("bexp", [P, 40])
        offs = sb("offs", [P, 2, 40], i32)
        offs4 = sb("offs4", [P, 40], i32)
        slotf = sb("slotf", [P, NT, 2])
        slots = sb("slots", [P, NT, 2], i32)
        slots_in = sb("slots_in", [P, NT, 2], i32)
        block_row_f = sb("block_row_f", [P, 40])
        block_row = sb("block_row", [P, 40], i32)
        U = sb("U", [P, 11840])
        cwr = U[0:E0, 11328:11840]
        kbd = U[:, 0:2464].rearrange("p (a h k) -> p a h k", a=2, h=HEADS)
        vpad = U[0:KEYS, 2464:3488].rearrange("p (a h k) -> p a h k", a=2, h=HEADS)
        PR = U[:, 3488:5952].rearrange("p (a h k) -> p a h k", a=2, h=HEADS)
        PT = U[0:KEYS, 5952:10048].rearrange("p (a h k) -> p a h k", a=2, h=HEADS)
        OTt = U[:, 10048:10560].rearrange("p (g q) -> p g q", g=4)
        On = U[:, 10560:10688]
        OT = U[:, 10688:10816]
        qT = U[:, 10816:11840].rearrange("p (a q) -> p a q", a=2)
        SELT = U[:, 0:8192].rearrange("p (g e) -> p g e", e=ES)
        LGT = U[:, 8192:8704]
        PERM = U[:, 8704:9216]
        BD = U[:, 9216:10240].rearrange("p (a g e) -> p a g e", a=2, e=ES)
        INN = U[:, 10240:11264].rearrange("p (a i g) -> p a i g", a=2, i=4)
        XA = U[:, 3488:5536].rearrange("p (t n) -> p t n", t=NT)
        XB = U[:, 5536:7584].rearrange("p (r b n) -> p r b n", r=4, b=4)
        XBT = U[:, 7584:9632].rearrange("p (r n) -> p r n", r=4)
        bcmp = U[:, 9632:9952].rearrange("p (b e) -> p b e", e=E1)
        cnt = U[:, 9952:10208].rearrange("p (e n) -> p e n", e=E1)
        zeros = U[:, 3488:3488 + 8 * P]
        b2row = SLOT[1][0:1, 0:E1 * D]

        xs = nc.dram_tensor("rows_in", (E1 * REGION, D), f32).ap()
        ys = nc.dram_tensor("rows_out", (MAX_ROWS, D), f32).ap()
        xs_wide = xs.rearrange("(p a r) d -> p a (r d)", p=P, r=8)
        ys_blocks = ys.rearrange("(b p) d -> p b d", p=P)

        PS = [ctx.enter_context(nc.psum_tensor(f"bank{i}", [P, 512], f32)) for i in range(8)]
        bank_full = [sem(f"bank_full{i}") for i in range(8)]
        bank_free = [sem(f"bank_free{i}") for i in range(8)]
        done_before = {1: 0, 3: BLOCKS[1] - GROUPS_OF_BLOCKS[1]}
        turn = {}
        fillings = [0] * 8

        def claim(pe, bank, key):
            if fillings[bank]:
                pe.wait_ge(bank_free[bank], fillings[bank])
            fillings[bank] += 1
            turn[key] = (bank, fillings[bank])
            return PS[bank]

        def full(eng, key):
            b, n = turn[key]
            eng.wait_ge(bank_full[b], n)
            return PS[b]

        def drained(eng, key):
            b, n = turn[key]
            eng.wait_ge(bank_free[b], n)

        def chunk(c):
            return slice(c * SEQ, (c + 1) * SEQ)

        def tile_(t):
            return slice(t * P, (t + 1) * P)

        block = ctx.enter_context(nc.Block())

        @block.tensor
        def _(pe):
            def mm(out_, lhsT, rhs, start=True, stop=True, **kw):
                return nc.tensor.matmul(out_, lhsT, rhs, start=start, stop=stop, **kw)

            def prep_xt(n):
                bank = claim(pe, 7, ("xt", n))
                pe.wait_ge(sem("xn_ready"), n + 1)
                s, c = divmod(n, BATCH)
                for t in range(TPC):
                    src = XN[:, n % 2, t, :]
                    last = nc.tensor.transpose(bank[:, tile_(t)], src, ident[:])
                last.then_inc(bank_full[7], 1)

            pe.wait_ge(sem("ident_ready"), 2)
            pe.wait_ge(sem("small_loaded"), 16)
            pe.wait_ge(sem("ones_ready"), 1)
            order = 0
            for l in (0, 3):
                b = order % 6
                bank = claim(pe, b, ("Mk", l))
                mm(bank[:, 0:BK], small(f"waT{l}"), small("ctxT")).then_inc(bank_full[b], 1)
                order += 1
                b = order % 6
                bank = claim(pe, b, ("Vw", l))
                for i in range(BATCH):
                    last = mm(bank[0:KEYS, tile_(i)], small("ctxT")[:, i * KEYS:(i + 1) * KEYS],
                              small(f"wcT{l}")[:, 0:P])
                last.then_inc(bank_full[b], 1)
                order += 1
            for l in (1, 2):
                b = order % 6
                bank = claim(pe, b, ("KT", l))
                mm(bank[:, 0:BK], small(f"wkT{l}"), small("ctxT")).then_inc(bank_full[b], 1)
                order += 1
                b = order % 6
                bank = claim(pe, b, ("Vc", l))
                for i in range(BATCH):
                    mm(bank[0:KEYS, tile_(i)], small("ctxT")[:, i * KEYS:(i + 1) * KEYS],
                       small(f"wvT{l}"), stop=False)
                    last = mm(bank[0:KEYS, tile_(i)], ones_row[:, 0:KEYS], small(f"bv{l}"), start=False)
                last.then_inc(bank_full[b], 1)
                order += 1

            def window_layer(s, l):
                def front(c):
                    n = 4 * s + c
                    if c or not s:
                        prep_xt(n)
                    b = c % 2
                    bank = claim(pe, b, ("sc", s, c))
                    if c == 0:
                        drained(pe, ("Mk", l))
                    drained(pe, ("xt", n))
                    for t in range(TPC):
                        last = mm(bank[:, t * KEYS:(t + 1) * KEYS], XNT[:, tile_(4 * c + t)],
                                  Mk[l][:, c * KEYS:(c + 1) * KEYS])
                    last.then_inc(bank_full[b], 1)

                def back(c):
                    b = 2 + c % 2
                    bank = claim(pe, b, ("eT", s, c))
                    pe.wait_ge(sem(f"probs_ready{s}"), c + 1)
                    for t in range(TPC):
                        last = nc.tensor.transpose(bank[0:KEYS, tile_(t)], sc[:, c % 2, t, :], ident[:])
                    last.then_inc(bank_full[b], 1)
                    b = 4 + c % 2
                    bank = claim(pe, b, ("pre", s, c))
                    if c == 0:
                        drained(pe, ("Vw", l))
                    drained(pe, ("eT", s, c))
                    for t in range(TPC):
                        mm(bank[:, tile_(t)], eT[:, c % 2, tile_(t)], Vw[l][:, c, :], stop=False)
                        last = mm(bank[:, tile_(t)], XNT[:, tile_(4 * c + t)], small(f"wcT{l}")[:, P:2 * P],
                                  start=False)
                    last.then_inc(bank_full[b], 1)

                ahead = layers[s + 1:s + 2] == [(TOPK, 3)]
                logits, count = routing(s + 1, 3)
                gated_next = layers[s + 1:s + 2] == [(GATED, 0)]
                gate_logits, gatesT = gates(s + 1)
                for i in range(BATCH + (3 if ahead else 1)):
                    c = i - 3
                    if ahead and c >= 0:
                        logits(c)
                    if i < BATCH:
                        front(i)
                    if gated_next and i == BATCH - 1:
                        prep_xt(4 * (s + 1))
                        gate_logits(0)
                    if 1 <= i < BATCH + 1:
                        back(i - 1)
                    if ahead and c >= 0:
                        count(c)
                if gated_next:
                    gatesT(0)

            def gates(s):
                def logits(c):
                    bank = claim(pe, 7, ("lg", s, c))
                    drained(pe, ("xt", 4 * s + c))
                    for t in range(TPC):
                        mm(bank[:, t * E0:(t + 1) * E0], XNT[:, tile_(4 * c + t)], small("gw"), stop=False)
                        last = mm(bank[:, t * E0:(t + 1) * E0], ones_row[:], small("gb"), start=False)
                    last.then_inc(bank_full[7], 1)

                def gatesT(c):
                    bank = claim(pe, 7, ("cwT", s, c))
                    pe.wait_ge(sem("cw_ready"), c + 1)
                    for t in range(TPC):
                        last = nc.tensor.transpose(bank[0:E0, tile_(t)], cw[:, c % 2, t, :], ident[:])
                    last.then_inc(bank_full[7], 1)

                return logits, gatesT

            def gated_layer(s):
                logits, gatesT = gates(s)

                def up(c, i):
                    xc = XNT[:, chunk(c)]
                    w1 = SLOT[0][:, i * P:(i + 1) * P] if i < PAIRS else small("sw1")
                    w3 = SLOT[0][:, 2048 + i * P:2048 + (i + 1) * P] if i < PAIRS else small("sw3")
                    b = i % 2
                    mm(claim(pe, b, ("A", c, i))[:], w1, xc).then_inc(bank_full[b], 1)
                    mm(claim(pe, 2 + b, ("C", c, i))[:], w3, xc).then_inc(bank_full[2 + b], 1)
                    if i < PAIRS:
                        mm(claim(pe, 4 + b, ("G", c, i))[:], pairsel[:, i, :], cw3[:, c % 2, :])\
                            .then_inc(bank_full[4 + b], 1)

                def down(c, i):
                    if i == 0:
                        bank = claim(pe, 6, ("oT", c))
                        if c == 0:
                            pe.wait_ge(sem("w2_loaded"), 16)
                        mm(bank[:], small("b2_0"), cwT[:, c % 2, :], stop=False)
                    drained(pe, ("G" if i < PAIRS else "C", c, i))
                    w2 = SLOT[1][:, i * P:(i + 1) * P] if i < PAIRS else small("sw2")
                    last = mm(PS[6][:], w2, H1[:, i % 2, :], start=False, stop=i == PAIRS)
                    last.then_inc(sem("h_used"), 1) if i < PAIRS else last.then_inc(bank_full[6], 1)

                def back(c):
                    bank = claim(pe, 7, ("ob", c))
                    drained(pe, ("oT", c))
                    for t in range(TPC):
                        last = nc.tensor.transpose(bank[:, tile_(t)], outT[:, tile_(t)], ident[:])
                    last.then_inc(bank_full[7], 1)

                pe.wait_ge(sem("w13_loaded"), 16)
                for c in range(BATCH):
                    drained(pe, ("cwT", s, c))
                    pe.wait_ge(sem("cw3_ready"), c + 1)
                    for i in range(PAIRS + 1):
                        up(c, i)
                        if i == 2 and c:
                            back(c - 1)
                        if c + 1 < BATCH:
                            if i == 5:
                                prep_xt(4 * s + c + 1)
                            if i == 6:
                                logits(c + 1)
                            if i == 14:
                                gatesT(c + 1)
                        elif i == 12:
                            prep_xt(4 * (s + 1))
                        elif i == 13:
                            query(s + 1, layers[s + 1][1], 0)
                        if i:
                            down(c, i - 1)
                    down(c, PAIRS)
                back(BATCH - 1)

            def routing(s, l):
                w = CHOICES[l] * E1

                def logits(c):
                    n = 4 * s + c
                    prep_xt(n)
                    bank = claim(pe, 6, ("rl", s, c))
                    drained(pe, ("xt", n))
                    for t in range(TPC):
                        last = mm(bank[:, t * E1:(t + 1) * E1], XNT[:, tile_(4 * c + t)],
                                  small("rwT" if l == 1 else "wr"), stop=l == 1)
                        if l == 3:
                            last = mm(bank[:, t * E1:(t + 1) * E1], ones_row[:], small("br"), start=False)
                    last.then_inc(bank_full[6], 1)

                def count(c):
                    bank = claim(pe, 5, ("cum", s, c))
                    pe.wait_ge(sem(f"onehot_ready{s}"), c + 1)
                    out_ = bank[:, 0:TPC * w].rearrange("p (t n) -> p t n", t=TPC)
                    mm(out_, tri[:], ohb[:, :, 0:w], stop=False, skip_group_check=True)
                    for t in range(TPC):
                        one = ohb[:, t, 0:w]
                        if t + 1 < TPC:
                            mm(out_[:, t + 1:TPC, :], ones_b[:], one.unsqueeze(1).to_broadcast([P, TPC - 1 - t, w]),
                               start=False, stop=False, skip_group_check=True)
                        last = mm(bank[:, TPC * w:(TPC + 1) * w], ones_b[:], one, start=False,
                                  stop=t == TPC - 1, skip_group_check=True)
                    last.then_inc(bank_full[5], 1)

                return logits, count

            def query(s, l, c):
                bank = claim(pe, 7, ("q", s, c))
                drained(pe, ("xt", 4 * s + c))
                mm(bank[:], small(f"wqT{l}"), XNT[:, chunk(c)]).then_inc(bank_full[7], 1)

            def heads_layer(s, l):
                def scores(u):
                    c, t = divmod(u, TPC)
                    if t == 0:
                        drained(pe, ("q", s, c))
                        pe.wait_ge(sem("kbd_ready"), BATCH * (l - 1) + c + 1)
                    if u == 0:
                        pe.wait_ge(sem("delta_ready"), 1)
                    for b, (h0, h1) in enumerate(HEAD_BANKS):
                        bank = claim(pe, b, ("S", s, u, b))
                        n = (h1 - h0) * KEYS
                        mm(bank[:, 0:n], ones96[:],
                           delta3[:, c * KEYS:(c + 1) * KEYS].unsqueeze(1).to_broadcast([96, h1 - h0, KEYS]),
                           stop=False)
                        mm(bank[:, 0:n], qT[:, c % 2, tile_(t)],
                           kbd[:, c % 2, h0:h1, :].rearrange("p h k -> p (h k)"), start=False)\
                            .then_inc(bank_full[b], 1)

                def probsT(u):
                    pe.wait_ge(sem(f"exp_ready{s}"), u + 1)
                    for g in range(4):
                        b = 3 + g % 2
                        bank = claim(pe, b, ("T", s, u, g))
                        for j in range(4):
                            last = nc.tensor.transpose(bank[0:KEYS, tile_(j)], PR[:, u % 2, 4 * g + j, :], ident[:])
                        last.then_inc(bank_full[b], 1)

                def values(u):
                    c = u // TPC
                    bank = claim(pe, 5, ("O", s, u))
                    for g in range(4):
                        drained(pe, ("T", s, u, g))
                        for j in range(4):
                            last = mm(bank[32 * j:32 * j + 32, tile_(g)], vpad[:, c % 2, 4 * g + j, :],
                                      PT[:, u % 2, 4 * g + j, :])
                    last.then_inc(bank_full[5], 1)

                def back_to_tokens(u):
                    bank = claim(pe, 6, ("Ot", s, u))
                    drained(pe, ("O", s, u))
                    for g in range(4):
                        last = nc.tensor.transpose(bank[:, tile_(g)], OTt[:, g, :], ident[:])
                    last.then_inc(bank_full[6], 1)

                def headsT(u):
                    bank = claim(pe, 7, ("OT", s, u))
                    drained(pe, ("Ot", s, u))
                    nc.tensor.transpose(bank[:, 0:P], On, ident[:]).then_inc(bank_full[7], 1)

                def project(u):
                    bank = claim(pe, 7, ("Y", s, u))
                    drained(pe, ("OT", s, u))
                    mm(bank[:, 0:P], OT, small(f"woT{l}"), stop=False)
                    mm(bank[:, 0:P], ones_row[:], small(f"bo{l}"), start=False).then_inc(bank_full[7], 1)

                ahead = layers[s + 1:s + 2] == [(TOPK, 1)]
                choice_next = layers[s + 1:s + 2] == [(CHOICE, 2)]
                logits, count = routing(s + 1, 1)
                if layers[s - 1][0] != GATED:
                    prep_xt(4 * s)
                    query(s, l, 0)
                for u in range(FINISH_AT[-1] + 1 if ahead else NT + 4):
                    if u < NT:
                        scores(u)
                    if 2 <= u < NT + 2:
                        values(u - 2)
                    if 4 <= u < NT + 4:
                        project(u - 4)
                    if u < NT and u % TPC == 2 and u // TPC + 1 < BATCH:
                        prep_xt(4 * s + u // TPC + 1)
                        query(s, l, u // TPC + 1)
                    if 1 <= u < NT + 1:
                        probsT(u - 1)
                    if 3 <= u < NT + 3:
                        headsT(u - 3)
                    if 2 <= u < NT + 2:
                        back_to_tokens(u - 2)
                    if choice_next and u in CHOICE_TURN_AT:
                        prep_xt(4 * (s + 1) + CHOICE_TURN_AT.index(u))
                    if ahead and u in LOGITS_AT:
                        logits(LOGITS_AT.index(u))
                    if ahead and u in CHOOSE_AT:
                        count(CHOOSE_AT.index(u))

            def topk_layer(s, l):
                def rows_in(g):
                    bank = claim(pe, 7, ("XB", s, g))
                    pe.wait_ge(sem(f"rows_loaded{s}_{g}"), 16 * 4)
                    for j in range(4):
                        last = nc.tensor.transpose(bank[:, tile_(j)], XB[:, g % 4, j, :], ident[:])
                    last.then_inc(bank_full[7], 1)

                def up(b):
                    bank = claim(pe, b % 2, ("U", s, b))
                    if b % 4 == 0:
                        drained(pe, ("XB", s, b // 4))
                    mm(bank[:], XBT[:, b // 4 % 4, tile_(b % 4)], SLOT[2][:, bass.ds(columns[b], F1)])\
                        .then_inc(bank_full[b % 2], 1)

                def hiddenT(b):
                    bank = claim(pe, 2 + b % 2, ("HT", s, b))
                    drained(pe, ("U", s, b))
                    for f in range(FC):
                        last = nc.tensor.transpose(bank[:, tile_(f)], HS[:, b % 2, tile_(f)], ident[:])
                    last.then_inc(bank_full[2 + b % 2], 1)

                def down(b):
                    k = 4 + b // 4 % 2
                    bank = claim(pe, k, ("Yd", s, b // 4)) if b % 4 == 0 else PS[k]
                    if l == 3:
                        mm(bank[:, tile_(b % 4)], ones_row[:], b2row[:, bass.ds(b2_columns[b], D)], stop=False)
                        pe.wait_ge(sem("relu_done"), FC * (b + 1))
                    else:
                        drained(pe, ("HT", s, b))
                    for f in range(FC):
                        last = mm(bank[:, tile_(b % 4)], HT[:, b % 2, tile_(f)],
                                  SLOT[3][:, bass.ds(columns[b] + f * P, P)], start=f == 0 and l == 1,
                                  stop=f == FC - 1)
                    last.then_inc(bank_full[k], 1) if b % 4 == 3 or b == BLOCKS[l] - 1 \
                        else last.then_inc(sem("down_done"), 1)

                pe.wait_ge(sem(f"up_loaded{l}"), 16)
                pe.wait_ge(sem(f"down_loaded{l}"), 16)
                if l == 3:
                    pe.wait_ge(sem("b2row_loaded"), 16)
                pe.wait_ge(sem(f"offsets_ready{s}"), 1)
                columns, b2_columns = {}, {}
                rows_in(0)
                for b in range(BLOCKS[l] + 2):
                    if b < BLOCKS[l]:
                        columns[b] = pe.value_load(offs[0:1, 0, b:b + 1], min_val=0, max_val=(E1 - 1) * F1)
                        if l == 3:
                            b2_columns[b] = pe.value_load(offs[0:1, 1, b:b + 1], min_val=0, max_val=(E1 - 1) * D)
                        up(b)
                    if b % 4 == 1 and b // 4 + 1 < GROUPS_OF_BLOCKS[l]:
                        rows_in(b // 4 + 1)
                    if 1 <= b <= BLOCKS[l]:
                        hiddenT(b - 1)
                    if b >= 2:
                        down(b - 2)

            def choice_layer(s):
                def front(c):
                    n = 4 * s + c
                    if c >= len(CHOICE_TURN_AT):
                        prep_xt(n)
                    b = c % 2
                    bank = claim(pe, b, ("cl", c))
                    drained(pe, ("xt", n))
                    mm(bank[:], small("ctrl"), XNT[:, chunk(c)]).then_inc(bank_full[b], 1)

                def select(c):
                    bank = claim(pe, 2, ("pt", c))
                    pe.wait_ge(sem("perm_ready"), c + 1)
                    for t in range(TPC):
                        last = nc.tensor.transpose(bank[:, t * ES:(t + 1) * ES], PERM[0:ES, tile_(t)],
                                                   ident[0:ES, 0:ES])
                    last.then_inc(bank_full[2], 1)
                    for t in range(TPC):
                        b = 3 + t % 2
                        bank = claim(pe, b, ("sel", c, t))
                        if t < TPC - 1:
                            pe.wait_ge(sem("bd_ready"), c * (TPC - 1) + t + 1)
                        else:
                            drained(pe, ("pt", c))
                        mm(bank[:], XN[:, c % 2, t, :], BD[:, t % 2, :, :].rearrange("p g e -> p (g e)"))\
                            .then_inc(bank_full[b], 1)

                front(0)
                for c in range(BATCH):
                    if c + 1 < BATCH:
                        front(c + 1)
                    select(c)

                pe.wait_ge(sem("f1_loaded"), 16)
                pe.wait_ge(sem("f2_loaded"), 16)
                drained(pe, ("sel", BATCH - 1, 2))
                drained(pe, ("sel", BATCH - 1, 3))

                def up(q):
                    b = q % 2
                    bank = claim(pe, b, ("cu", q))
                    for i in range(4):
                        for h in range(2):
                            e = 8 * q + 2 * i + h
                            last = mm(bank[h * FS:(h + 1) * FS, tile_(i)], SLOT[0][:, e * FS:(e + 1) * FS],
                                      SELT[:, :, e])
                    last.then_inc(bank_full[b], 1)

                def down(q):
                    drained(pe, ("cu", q))
                    for h in range(2):
                        b = 2 + 2 * (q % 2) + h
                        bank = claim(pe, b, ("cd", q, h))
                        for i in range(4):
                            last = mm(bank[:, tile_(i)],
                                      SLOT[1][h * FS:(h + 1) * FS, (4 * q + i) * P:(4 * q + i + 1) * P],
                                      INN[h * FS:(h + 1) * FS, q % 2, i, :])
                        last.then_inc(bank_full[b], 1)

                for q in range(ES // 8):
                    up(q)
                    if q:
                        down(q - 1)
                down(ES // 8 - 1)
                for q in (ES // 8 - 2, ES // 8 - 1):
                    for h in range(2):
                        drained(pe, ("cd", q, h))

                def rows(c, k):
                    b = (4 * c + k) % 2
                    bank = claim(pe, b, ("in", c, k))
                    for j in range(4):
                        g = 32 * c + 8 * k + 2 * j
                        last = nc.tensor.transpose(bank[:, tile_(j)],
                                                   SELT[:, g:g + 2, :].rearrange("p g e -> p (g e)"), ident[:])
                    last.then_inc(bank_full[b], 1)

                def combine(c):
                    b = 2 + c % 2
                    bank = claim(pe, b, ("co", c))
                    pe.wait_ge(sem("pb_ready"), c + 1)
                    for k in range(4):
                        drained(pe, ("in", c, k))
                        for j in range(4):
                            last = mm(bank[32 * j:32 * j + 32, tile_(k)],
                                      XNT[:, c * SEQ + k * P + 32 * j:c * SEQ + k * P + 32 * j + 32],
                                      INTER[:, c % 2, k, tile_(j)])
                    last.then_inc(bank_full[b], 1)

                for c in range(BATCH):
                    for k in range(4):
                        rows(c, k)
                    if c:
                        combine(c - 1)
                if s + 1 < len(layers):
                    prep_xt(4 * (s + 1))
                combine(BATCH - 1)

            for s, (kind, l) in enumerate(layers):
                if kind == WINDOW_ATT:
                    window_layer(s, l)
                elif kind == GATED:
                    gated_layer(s)
                elif kind == HEADS_ATT:
                    heads_layer(s, l)
                elif kind == TOPK:
                    topk_layer(s, l)
                else:
                    choice_layer(s)

        @block.vector
        def _(dve):
            v = nc.vector
            counted = {}

            def mark(ins, name="dve_step"):
                ins.then_inc(sem(name), 1)
                counted[name] = counted.get(name, 0) + 1
                dve.wait_ge(sem(name), counted[name])

            def free(ins, key):
                b, n = turn[key]
                ins.then_inc(bank_free[b], 1)
                dve.wait_ge(bank_free[b], n)

            mark(v.memset(ones_row[:], 1.0), "ones_ready")
            mark(v.memset(neghalf[:], -0.5), "neghalf_ready")
            mark(v.memset(gs[:], -9.0))
            mark(v.memset(me[:], -9.0))
            mark(v.memset(r8[:], -9.0))
            mark(v.memset(ones_b[:], 1.0))
            mark(v.memset(ones96[:], 1.0))
            mark(v.memset(delta3[:], 0.0))
            dve.wait_ge(sem("iota_done"), 7)
            mark(v.tensor_copy(region[:], region_i[:]))
            mark(v.tensor_copy(step128[:], step_i[:]))
            mark(v.tensor_copy(bidx[:], bidx_i[:]))
            mark(v.tensor_copy(idx_f[:], idx_i[:]))
            mark(v.tensor_copy(pidx_f[:], pidx_i[:]))
            mark(v.tensor_copy(desc[:], desc_i[:]))
            mark(v.tensor_scalar(tie[:], tie_i[:], 1e-6 / (GRP - 1), None, ALU.mult))

            def layernorm(src, dst, last_name):
                for t in range(TPC):
                    ins = v.bn_stats(stats[:, t, :], src(t))
                    ins.then_inc(sem("bn_done"), 1)
                counted["bn"] = counted.get("bn", 0) + TPC
                dve.wait_ge(sem("bn_done"), counted["bn"])
                for t in range(TPC):
                    v.bn_aggr(mv[:, t, :], stats[:, t, :]).then_inc(sem("bn_done"), 1)
                counted["bn"] += TPC
                dve.wait_ge(sem("bn_done"), counted["bn"])
                k = counted.get("var_ready", 0)
                mark(v.tensor_scalar(veps[:, k % 2, :], mv[:, :, 1], 1e-5, None, ALU.add), "var_ready")
                dve.wait_ge(sem("rstd_ready"), k + 1)
                for t in range(TPC):
                    ins = v.tensor_scalar(dst(t), src(t), mv[:, t, 0:1], rstd[:, k % 2, t:t + 1],
                                          ALU.subtract, ALU.mult)
                    if t < TPC - 1:
                        ins.then_inc(sem("ln_part"), 1)
                counted["ln_part"] = counted.get("ln_part", 0) + TPC - 1
                mark(ins, last_name)
                dve.wait_ge(sem("ln_part"), counted["ln_part"])

            def combine(s, l, c):
                nk = CHOICES[l]
                for j in range(TPC * nk * c, TPC * nk * (c + 1)):
                    t, k = divmod(j, nk)
                    dve.wait_ge(sem(f"gathered{s}_{j % RING}"), 16 * (j // RING + 1))
                    mark(v.scalar_tensor_tensor(X[:, t, :], YG[:, j % RING, :], GA[:, t, k:k + 1], X[:, t, :],
                                                ALU.mult, ALU.add), f"combined{s}")

            def prep_ln(n):
                s, c = divmod(n, BATCH)
                if s and layers[s - 1][0] == TOPK:
                    combine(s - 1, layers[s - 1][1], c)
                if n < 4:
                    dve.wait_ge(sem(f"x_loaded{n}"), 16)
                if n >= 2:
                    full(dve, ("xt", n - 2))
                    kind = layers[(n - 2) // BATCH][0]
                    if kind == CHOICE:
                        full(dve, ("sel", (n - 2) % BATCH, TPC - 1))
                    elif layers[(n - 2) // BATCH] == (TOPK, 1):
                        k = (n - 2) // BATCH
                        dve.wait_ge(sem(f"scattered{k}_{(n - 2) % BATCH}"), 16 * TPC * CHOICES[1])
                layernorm(lambda t: X[:, 4 * c + t, :], lambda t: XN[:, n % 2, t, :], "xn_ready")

            prep_ln(0)
            dve.wait_ge(sem("small_loaded"), 16)
            dve.wait_ge(sem("lens_loaded"), 16)
            mark(v.tensor_copy(lens_f[:], lens_i[:]))
            mark(v.tensor_scalar(lo_hi[:, 0, :], small("pt"), -WINDOW, 0.0, ALU.add, ALU.max))
            mark(v.tensor_scalar(lo_hi[:, 1, :], small("pt"), WINDOW, None, ALU.add))
            mark(v.tensor_tensor(lo_hi[:, 1, :], lo_hi[:, 1, :], lens_f[:], ALU.min))
            idx_b = idx_f[:].unsqueeze(1).to_broadcast([P, BATCH, KEYS])
            mark(v.tensor_tensor(keep[:], idx_b, lo_hi[:, 0, :].unsqueeze(2).to_broadcast([P, BATCH, KEYS]), ALU.is_ge))
            mark(v.tensor_tensor(neg[:], idx_b, lo_hi[:, 1, :].unsqueeze(2).to_broadcast([P, BATCH, KEYS]), ALU.is_le))
            mark(v.tensor_tensor(keep[:], keep[:], neg[:], ALU.mult))
            mark(v.tensor_scalar(neg[:], keep[:], 1e9, -1e9, ALU.mult, ALU.add))
            mark(v.tensor_scalar(gauss[:], small("pt"), pidx_f[:], None, ALU.subtract))
            mark(v.tensor_tensor(gauss[:], gauss[:], gauss[:], ALU.mult), "dist_ready")
            mark(v.tensor_scalar(tau_s[:], small("tau"), float(DK) ** -0.5, None, ALU.mult))
            mark(v.tensor_scalar(dtmp[:, 0, :], small("delta"), float(DK) ** -0.5, None, ALU.mult))
            mark(v.tensor_copy(delta3[0:1, :], dtmp[:, 0, :]))
            mark(v.tensor_tensor(dtmp[:, 1, :], dtmp[:, 0, :], delta3[0:1, :], ALU.subtract))
            mark(v.tensor_copy(dtb[:], dtmp[:, 1, :]))
            mark(v.tensor_copy(delta3[32:33, :], dtb[:]))
            mark(v.tensor_tensor(dtmp[:, 1, :], dtmp[:, 1, :], dtb[:], ALU.subtract))
            mark(v.tensor_copy(delta3[64:65, :], dtmp[:, 1, :]), "delta_ready")
            dve.wait_ge(sem("gauss_ready"), 1)
            for l in (0, 3):
                bank = full(dve, ("Mk", l))
                free(v.tensor_copy(Mk[l][:], bank[:, 0:BK]), ("Mk", l))
                bank = full(dve, ("Vw", l))
                free(v.tensor_tensor(Vw[l][:], bank[0:KEYS, :].rearrange("p (b n) -> p b n", b=BATCH),
                                     gauss[0:KEYS, :].unsqueeze(2).to_broadcast([KEYS, BATCH, P]), ALU.mult),
                     ("Vw", l))
            for l in (1, 2):
                bank = full(dve, ("KT", l))
                view = bank[:, 0:BK].rearrange("p (b k) -> p b k", b=BATCH)
                tau_b = tau_s[:].unsqueeze(2).to_broadcast([P, BATCH, KEYS])
                free(v.scalar_tensor_tensor(KT[l][:].rearrange("p (b k) -> p b k", b=BATCH), view,
                                            small(f"bk{l}"), tau_b, ALU.add, ALU.mult), ("KT", l))
                bank = full(dve, ("Vc", l))
                free(v.tensor_copy(Vc[l][:], bank[0:KEYS, :].rearrange("p (b n) -> p b n", b=BATCH)), ("Vc", l))

            def window_layer(s, l):
                def masked(c):
                    bank = full(dve, ("sc", s, c))
                    S = sc[:, c % 2]
                    if c >= 2:
                        full(dve, ("eT", s, c - 2))
                    kb = keep[:, c, :].unsqueeze(1).to_broadcast([P, TPC, KEYS])
                    nb = neg[:, c, :].unsqueeze(1).to_broadcast([P, TPC, KEYS])
                    free(v.tensor_tensor(S, bank[:, 0:TPC * KEYS].rearrange("p (t k) -> p t k", t=TPC), kb,
                                         ALU.mult), ("sc", s, c))
                    mark(v.tensor_tensor(S, S, nb, ALU.add))
                    mark(v.tensor_reduce(mx[:, 0:TPC], S, AX, ALU.max))
                    mark(v.tensor_tensor(S, S, mx[:, 0:TPC].unsqueeze(2).to_broadcast([P, TPC, KEYS]),
                                         ALU.subtract), f"masked_ready{s}")

                def normed(c):
                    S = sc[:, c % 2]
                    dve.wait_ge(sem(f"wexp_ready{s}"), c + 1)
                    mark(v.tensor_reduce(red[:, 0:TPC], S, AX, ALU.add))
                    mark(v.reciprocal(red[:, 0:TPC], red[:, 0:TPC]))
                    mark(v.tensor_tensor(S, S, red[:, 0:TPC].unsqueeze(2).to_broadcast([P, TPC, KEYS]), ALU.mult),
                         f"probs_ready{s}")

                def add(c):
                    bank = full(dve, ("pre", s, c))
                    drained(dve, ("pre", s, c))
                    mark(v.tensor_tensor(X[:, 4 * c:4 * c + 4, :], X[:, 4 * c:4 * c + 4, :],
                                         th.rearrange("p (t n) -> p t n", t=TPC), ALU.add), f"x_done{s}")

                ahead = layers[s + 1:s + 2] == [(TOPK, 3)]
                norms, route, choose, finish = routing(s + 1, 3)
                gated_next = layers[s + 1:s + 2] == [(GATED, 0)]
                gate_route, gate_choose, split = gates(s + 1)
                if ahead:
                    mark(v.memset(carry[:], 0.0))
                for i in range(BATCH + (3 if ahead else 1)):
                    c = i - 3
                    if ahead and c >= 0:
                        route(c)
                    if i < BATCH:
                        masked(i)
                    if i + 1 < BATCH:
                        prep_ln(4 * s + i + 1)
                    if ahead and c >= 0:
                        choose(c)
                    if gated_next and i == BATCH - 1:
                        gate_route(0)
                    if i < BATCH:
                        normed(i)
                    if 1 <= i < BATCH + 1:
                        add(i - 1)
                    if ahead and c >= 0:
                        finish(c)
                    if ahead and c == -1:
                        norms(0)
                    if ahead and -1 <= c < BATCH - 2:
                        norms(c + 2)
                    if gated_next and i == BATCH - 2:
                        prep_ln(4 * (s + 1))
                    if gated_next and i == BATCH - 1:
                        gate_choose(0)
                if gated_next:
                    split(0)

            def gates(s):
                def top4(src, dst, w):
                    for t in range(TPC):
                        mark(v.max(v8[:, t, :], src[:, t, 0:w]))
                    mark(v.tensor_copy(r8[:, :, 0:4], v8[:, :, 0:4]))
                    for t in range(TPC):
                        mark(v.match_replace(dst[:, t, :], r8[:, t, :], src[:, t, :], 8.0))

                def route(c):
                    bank = full(dve, ("lg", s, c))
                    view = bank[:, 0:TPC * E0].rearrange("p (t e) -> p t e", t=TPC)
                    mark(v.tensor_reduce(mx[:, 0:TPC], view, AX, ALU.max))
                    free(v.tensor_tensor(s0[:], view, mx[:, 0:TPC].unsqueeze(2).to_broadcast([P, TPC, E0]),
                                         ALU.subtract), ("lg", s, c))

                def choose(c):
                    dve.wait_ge(sem("rexp_ready"), c + 1)
                    mark(v.tensor_reduce(red[:, 0:TPC], s0[:], AX, ALU.add))
                    mark(v.reciprocal(red[:, 0:TPC], red[:, 0:TPC]))
                    mark(v.tensor_tensor(s0[:], s0[:], red[:, 0:TPC].unsqueeze(2).to_broadcast([P, TPC, E0]),
                                         ALU.mult))
                    s4 = s0[:].rearrange("p t (g m) -> p (t g) m", m=4)
                    p6 = pr[:].rearrange("p t g m -> p (t g) m")
                    for a, j, w in ((0, 1, 3), (3, 2, 2), (5, 3, 1)):
                        mark(v.tensor_tensor(p6[:, :, a:a + w], s4[:, :, 0:w], s4[:, :, j:j + w], ALU.add))
                    mark(v.tensor_reduce(gs[:, :, 0:8], pr[:], AX, ALU.max))
                    top4(gs, gk, 8)
                    mark(v.tensor_scalar(pen[:], gk[:, :, 0:8], 8.0, -4.0, ALU.is_lt, ALU.mult))
                    for t in range(TPC):
                        mark(v.tensor_tensor(me[:, t, 0:E0].rearrange("p (g m) -> p g m", m=4),
                                             s0[:, t, :].rearrange("p (g m) -> p g m", m=4),
                                             pen[:, t, :].unsqueeze(2).to_broadcast([P, 8, 4]), ALU.add))
                    top4(me, mk, E0)
                    if c >= 2:
                        full(dve, ("cwT", s, c - 2))
                    mark(v.scalar_tensor_tensor(cw[:, c % 2], mk[:, :, 0:E0], 8.0, s0[:], ALU.is_equal, ALU.mult),
                         "cw_ready")

                def split(c):
                    a = c % 2
                    bank = full(dve, ("cwT", s, c))
                    if c >= 2:
                        full(dve, ("oT", c - 2))
                    free(v.tensor_copy(cwT[:, a, :], bank[0:E0, :]), ("cwT", s, c))
                    mark(v.tensor_copy(cw3[0:32, a, :], cwT[:, a, :]))
                    mark(v.tensor_tensor(cwr, cwT[:, a, :], cw3[0:32, a, :], ALU.subtract))
                    mark(v.tensor_copy(cwm[:], cwr))
                    mark(v.tensor_copy(cw3[32:64, a, :], cwm[:]))
                    mark(v.tensor_tensor(cwr, cwr, cwm[:], ALU.subtract))
                    mark(v.tensor_copy(cw3[64:96, a, :], cwr), "cw3_ready")

                return route, choose, split

            def gated_layer(s):
                route, choose, split = gates(s)

                def gate(c, i):
                    k = c * (PAIRS + 1) + i
                    bank = full(dve, ("C", c, i))
                    drained(dve, ("A", c, i))
                    if i >= 2:
                        dve.wait_ge(sem("h_used"), c * PAIRS + i - 1)
                    elif c:
                        full(dve, ("oT", c - 1))
                    b3 = small("b3_0")[:, i:i + 1] if i < PAIRS else small("sb3")
                    h = H1[:, i % 2, :]
                    free(v.scalar_tensor_tensor(T1 if i < PAIRS else h, bank[:], b3, S1[:, k % 2, :],
                                                ALU.add, ALU.mult), ("C", c, i))
                    if i < PAIRS:
                        bank = full(dve, ("G", c, i))
                        free(v.tensor_tensor(h, T1, bank[:], ALU.mult), ("G", c, i))

                def add(c):
                    bank = full(dve, ("ob", c))
                    free(v.tensor_tensor(X[:, 4 * c:4 * c + 4, :], X[:, 4 * c:4 * c + 4, :],
                                         bank[:].rearrange("p (t n) -> p t n", t=TPC), ALU.add), ("ob", c))

                for c in range(BATCH):
                    for i in range(PAIRS + 1):
                        if i == 3 and c:
                            add(c - 1)
                        if c + 1 < BATCH:
                            if i == 3:
                                prep_ln(4 * s + c + 1)
                            if i == 7:
                                route(c + 1)
                            if i == 8:
                                choose(c + 1)
                            if i == 15:
                                split(c + 1)
                        elif i == 10:
                            prep_ln(4 * (s + 1))
                        gate(c, i)
                add(BATCH - 1)

            def routing(s, l):
                nk = CHOICES[l]
                w = nk * E1

                def route(c):
                    bank = full(dve, ("rl", s, c))
                    view = bank[:, 0:TPC * E1].rearrange("p (t e) -> p t e", t=TPC)
                    mark(v.tensor_reduce(mx[:, 0:TPC], view, AX, ALU.max))
                    free(v.tensor_tensor(pb8[:], view, mx[:, 0:TPC].unsqueeze(2).to_broadcast([P, TPC, E1]),
                                         ALU.subtract), ("rl", s, c))

                def spread(ap):
                    return ap.unsqueeze(2).to_broadcast([P, TPC, E1])

                def largest(src, k):
                    mark(v.tensor_reduce(tv[:, k, :], src, AX, ALU.max))
                    mark(v.tensor_tensor(t8[:], src, spread(tv[:, k, :]), ALU.is_equal))
                    mark(v.tensor_tensor(t8[:], t8[:], desc[:].unsqueeze(1).to_broadcast([P, TPC, E1]), ALU.mult))
                    mark(v.tensor_reduce(red[:, 0:TPC], t8[:], AX, ALU.max))
                    mark(v.tensor_tensor(oh[:, k], t8[:], spread(red[:, 0:TPC]), ALU.is_equal))

                def choose(c):
                    dve.wait_ge(sem(f"rexp_ready{s}"), c + 1)
                    mark(v.tensor_reduce(red[:, 0:TPC], pb8[:], AX, ALU.add))
                    mark(v.reciprocal(red[:, 0:TPC], red[:, 0:TPC]))
                    mark(v.tensor_tensor(pb8[:], pb8[:], spread(red[:, 0:TPC]), ALU.mult))
                    largest(pb8[:], 0)
                    for k in range(nk):
                        if k:
                            mark(v.scalar_tensor_tensor(pb8[:], oh[:, 0], -2.0, pb8[:], ALU.mult, ALU.add))
                            largest(pb8[:], 1)
                        mark(v.tensor_copy(OHA[:, 4 * c:4 * c + 4, k * E1:(k + 1) * E1], oh[:, k]))
                    if c:
                        full(dve, ("cum", s, c - 1))
                    mark(v.tensor_copy(ohb[:, :, 0:w], OHA[:, 4 * c:4 * c + 4, 0:w]), f"onehot_ready{s}")
                    if nk == 1:
                        mark(v.tensor_copy(GA[:, 4 * c:4 * c + 4, 0], tv[:, 0, :]))
                        return
                    mark(v.tensor_tensor(tv[:, 2, :], tv[:, 0, :], tv[:, 1, :], ALU.add))
                    mark(v.reciprocal(tv[:, 2, :], tv[:, 2, :]))
                    for k in range(nk):
                        mark(v.tensor_tensor(GA[:, 4 * c:4 * c + 4, k], tv[:, k, :], tv[:, 2, :], ALU.mult))

                def finish(c):
                    bank = full(dve, ("cum", s, c))
                    mark(v.tensor_tensor(POSA[:, 4 * c:4 * c + 4, 0:w],
                                         bank[:, 0:TPC * w].rearrange("p (t n) -> p t n", t=TPC),
                                         carry[:, 0:w].unsqueeze(1).to_broadcast([P, TPC, w]), ALU.add))
                    free(v.tensor_tensor(carry[:, 0:w], carry[:, 0:w], bank[:, TPC * w:(TPC + 1) * w], ALU.add),
                         ("cum", s, c))
                    chosen = OHA[:, 4 * c:4 * c + 4, 0:w]
                    rank = POSA[:, 4 * c:4 * c + 4, 0:E1]
                    rows = slotf[:, 4 * c:4 * c + 4, 0:nk]
                    tmp = s0[:, :, 0:w]
                    tmp_k = tmp.rearrange("p t (k e) -> p t k e", k=nk)
                    if nk == 2:
                        mark(v.scalar_tensor_tensor(tmp, POSA[:, 4 * c:4 * c + 4, :], float(CAPACITY), chosen,
                                                    ALU.is_le, ALU.mult))
                        mark(v.tensor_reduce(rows, tmp_k, AX, ALU.add))
                        mark(v.tensor_tensor(GA[:, 4 * c:4 * c + 4, :], GA[:, 4 * c:4 * c + 4, :], rows, ALU.mult))
                        mark(v.tensor_tensor(rank, rank, POSA[:, 4 * c:4 * c + 4, E1:w], ALU.add))
                    for k in range(nk):
                        mark(v.tensor_tensor(tmp[:, :, k * E1:(k + 1) * E1], rank,
                                             region[:].unsqueeze(1).to_broadcast([P, TPC, E1]), ALU.add))
                    mark(v.tensor_tensor(tmp, tmp, chosen, ALU.mult))
                    mark(v.tensor_reduce(rows, tmp_k, AX, ALU.add))
                    mark(v.tensor_copy(slots_in[:, 4 * c:4 * c + 4, 0:nk], rows), f"slots_in_ready{s}")

                def norms(c):
                    prep_ln(4 * s + c)
                    if l == 3:
                        layernorm(lambda t: XN[:, (4 * s + c) % 2, t, :], lambda t: XA[:, 4 * c + t, :], "xn2_ready")

                return norms, route, choose, finish

            def heads_layer(s, l):
                def shifted(u):
                    if u >= 2:
                        full(dve, ("T", s, u - 2, 3))
                    for b, (h0, h1) in enumerate(HEAD_BANKS):
                        bank = full(dve, ("S", s, u, b))
                        view = bank[:, 0:(h1 - h0) * KEYS].rearrange("p (h k) -> p h k", k=KEYS)
                        mark(v.tensor_reduce(mx[:, h0:h1], view, AX, ALU.max))
                        free(v.tensor_tensor(PR[:, u % 2, h0:h1, :], view,
                                             mx[:, h0:h1].unsqueeze(2).to_broadcast([P, h1 - h0, KEYS]),
                                             ALU.subtract), ("S", s, u, b))

                def normed(u):
                    bank = full(dve, ("Ot", s, u))
                    view = bank[:].rearrange("p (h r) -> p h r", r=32)
                    mark(v.reciprocal(red[:], view[:, :, DK]))
                    if u:
                        full(dve, ("OT", s, u - 1))
                    free(v.tensor_tensor(On.rearrange("p (h d) -> p h d", h=HEADS), view[:, :, 0:DK],
                                         red[:].unsqueeze(2).to_broadcast([P, HEADS, DK]), ALU.mult),
                         ("Ot", s, u))

                def add(u):
                    bank = full(dve, ("Y", s, u))
                    free(v.tensor_tensor(X[:, u, :], X[:, u, :], bank[:, 0:P], ALU.add), ("Y", s, u))

                dve.wait_ge(sem("zero_stored"), 16)
                if layers[s - 1][0] != GATED:
                    prep_ln(4 * s)
                ahead = layers[s + 1:s + 2] == [(TOPK, 1)]
                choice_next = layers[s + 1:s + 2] == [(CHOICE, 2)]
                norms, route, choose, finish = routing(s + 1, 1)
                if ahead:
                    mark(v.memset(carry[:], 0.0))
                for u in range(FINISH_AT[-1] + 1 if ahead else NT + 4):
                    if ahead and u in SHIFT_AT:
                        route(SHIFT_AT.index(u))
                    if ahead and u in CHOOSE_AT:
                        choose(CHOOSE_AT.index(u))
                    if ahead and u in FINISH_AT:
                        finish(FINISH_AT.index(u))
                    if u < NT:
                        shifted(u)
                    if 4 <= u < NT + 4:
                        add(u - 4)
                    if u in NEXT_CHUNK_AT:
                        prep_ln(4 * s + 1 + NEXT_CHUNK_AT.index(u))
                    if 2 <= u < NT + 2:
                        normed(u - 2)
                    if choice_next and u in CHOICE_NORMS_AT:
                        prep_ln(4 * (s + 1) + CHOICE_NORMS_AT.index(u))
                    if ahead and u in NORMS_AT:
                        norms(NORMS_AT.index(u))

            def topk_layer(s, l):
                def place():
                    rows_n, blocks_n, before = nblk[:, 0, :], nblk[:, 1, :], nblk[:, 2, :]
                    if nk == 2:
                        mark(v.tensor_tensor(rows_n, carry[:, 0:E1], carry[:, E1:w], ALU.add))
                    else:
                        mark(v.tensor_copy(rows_n, carry[:, 0:E1]))
                    mark(v.tensor_tensor(cnt, rows_n.unsqueeze(2).to_broadcast([P, E1, 32]),
                                         step128[:].unsqueeze(1).to_broadcast([P, E1, 32]), ALU.is_gt))
                    mark(v.tensor_reduce(blocks_n, cnt, AX, ALU.add))
                    mark(v.tensor_tensor(cnt[:, :, 0:E1], lt8[:], blocks_n.unsqueeze(1).to_broadcast([P, E1, E1]),
                                         ALU.mult))
                    mark(v.tensor_reduce(before, cnt[:, :, 0:E1], AX, ALU.add))
                    mark(v.tensor_scalar(base[:], before, float(P), -1.0, ALU.mult, ALU.add))
                    mark(v.tensor_tensor(before, before, blocks_n, ALU.add))
                    mark(v.tensor_tensor(bcmp, before.unsqueeze(1).to_broadcast([P, 40, E1]),
                                         bidx[:].unsqueeze(2).to_broadcast([P, 40, E1]), ALU.is_le))
                    mark(v.tensor_reduce(bexp[:], bcmp, AX, ALU.add))
                    mark(v.tensor_scalar(blocks_n, blocks_n, -float(P), float(REGION), ALU.mult, ALU.add))
                    mark(v.tensor_tensor(bcmp, bcmp, blocks_n.unsqueeze(1).to_broadcast([P, 40, E1]), ALU.mult))
                    mark(v.tensor_reduce(block_row_f[:], bcmp, AX, ALU.add))
                    mark(v.scalar_tensor_tensor(block_row_f[:], bidx[:], float(P), block_row_f[:], ALU.mult, ALU.add))
                    mark(v.tensor_scalar(block_row[:], block_row_f[:], float(E1 * REGION - P), None, ALU.min),
                         f"block_rows_ready{s}")
                    mark(v.tensor_scalar(bexp[:], bexp[:], float(E1 - 1), None, ALU.min))
                    mark(v.tensor_scalar(offs[:, 1, :], bexp[:], float(D), None, ALU.mult))
                    if l == 3:
                        mark(v.tensor_scalar(offs4[:], bexp[:], float(FC), None, ALU.mult))
                    mark(v.tensor_scalar(offs[:, 0, :], bexp[:], float(F1), None, ALU.mult), f"offsets_ready{s}")
                    tmp = cnt_all[:, :, 0:w]
                    for k in range(nk):
                        mark(v.tensor_tensor(tmp[:, :, k * E1:(k + 1) * E1], POSA[:, :, 0:E1],
                                             base[:].unsqueeze(1).to_broadcast([P, NT, E1]), ALU.add))
                    mark(v.tensor_tensor(tmp, tmp, OHA[:, :, 0:w], ALU.mult))
                    for k in range(nk):
                        mark(v.tensor_reduce(slotf[:, :, k], tmp[:, :, k * E1:(k + 1) * E1], AX, ALU.add))
                        mark(v.tensor_copy(slots[:, :, k], slotf[:, :, k]), f"slots_ready{s}")

                def hiddenT(b):
                    if l == 3:
                        column = dve.value_load(offs4[0:1, b:b + 1], min_val=0, max_val=(E1 - 1) * FC)
                    bank = full(dve, ("HT", s, b))
                    if b >= 2:
                        n = b - 2
                        if n % 4 == 3:
                            full(dve, ("Yd", s, n // 4))
                        else:
                            dve.wait_ge(sem("down_done"), done_before[l] + n + 1 - (n + 1) // 4)
                    if l == 1:
                        free(v.tensor_copy(HT[:, b % 2, :], bank[:]), ("HT", s, b))
                        return
                    for f in range(FC):
                        v.tensor_scalar(HT[:, b % 2, tile_(f)], bank[:, tile_(f)],
                                        small("b1_3")[:, bass.ds(column + f, 1)], 0.0, ALU.add, ALU.max)\
                            .then_inc(sem("relu_done"), 1)
                    dve.wait_ge(sem("relu_done"), FC * (b + 1))
                    dve.sem_inc(bank_free[turn[("HT", s, b)][0]], 1)

                nk = CHOICES[l]
                w = nk * E1
                cnt_all = cnt.rearrange("p e n -> p (e n)").rearrange("p (t n) -> p t n", t=NT)
                place()
                for b in range(BLOCKS[l]):
                    hiddenT(b)

            def choice_layer(s):
                def choose(c):
                    bank = full(dve, ("cl", c))
                    G = SEQ // GRP
                    lg = LGT.rearrange("p (g t) -> p g t", t=GRP)
                    free(v.tensor_tensor(lg, bank[:].rearrange("p (g t) -> p g t", t=GRP),
                                         tie[:].unsqueeze(1).to_broadcast([P, G, GRP]), ALU.add), ("cl", c))
                    mark(v.tensor_reduce(red32[:], lg, AX, ALU.max))
                    if c:
                        full(dve, ("pt", c - 1))
                    mark(v.tensor_tensor(PERM.rearrange("p (g t) -> p g t", t=GRP), lg,
                                         red32[:].unsqueeze(2).to_broadcast([P, G, GRP]), ALU.is_equal),
                         "perm_ready")
                    mark(v.tensor_tensor(XNT[:, chunk(c)].rearrange("p (j m) -> p j m", m=2 * GRP),
                                         PERM.rearrange("p (j m) -> p j m", m=2 * GRP),
                                         parity[:].rearrange("p a t -> p (a t)").unsqueeze(1)
                                         .to_broadcast([P, G // 2, 2 * GRP]), ALU.mult), "pb_ready")

                def blocks(c):
                    bank = full(dve, ("pt", c))
                    for t in range(TPC):
                        k = c * TPC + t
                        if k >= 2:
                            full(dve, ("sel", *divmod(k - 2, TPC)))
                        ins = v.tensor_tensor(BD[:, t % 2], bank[:, t * ES:(t + 1) * ES].unsqueeze(1)
                                              .to_broadcast([P, GPT, ES]),
                                              gmask[:].unsqueeze(2).to_broadcast([P, GPT, ES]), ALU.mult)
                        if t < TPC - 1:
                            mark(ins, "bd_ready")
                    free(ins, ("pt", c))

                choose(0)
                for c in range(BATCH):
                    if len(CHOICE_NORMS_AT) <= c + 1 < BATCH:
                        prep_ln(4 * s + c + 1)
                    blocks(c)
                    if c + 1 < BATCH:
                        choose(c + 1)
                for q in range(ES // 8):
                    bank = full(dve, ("cd", q, 0))
                    free(v.tensor_copy(SELT[:, :, 8 * q:8 * q + 8:2],
                                       bank[:].rearrange("p (i g) -> p g i", i=4)), ("cd", q, 0))

                def add(c):
                    bank = full(dve, ("co", c))
                    free(v.tensor_tensor(X[:, 4 * c:4 * c + 4, :], X[:, 4 * c:4 * c + 4, :],
                                         bank[:].rearrange("p (t n) -> p t n", t=TPC), ALU.add), ("co", c))

                for c in range(BATCH):
                    if c >= 2:
                        full(dve, ("co", c - 2))
                    for k in (1, 3):
                        bank = full(dve, ("in", c, k))
                        free(v.tensor_copy(INTER[:, c % 2, k, :], bank[:]), ("in", c, k))
                    if c:
                        add(c - 1)
                    if c == 2 and s + 1 < len(layers):
                        prep_ln(4 * (s + 1))
                add(BATCH - 1)

            for s, (kind, l) in enumerate(layers):
                if kind == WINDOW_ATT:
                    window_layer(s, l)
                elif kind == GATED:
                    gated_layer(s)
                elif kind == HEADS_ATT:
                    heads_layer(s, l)
                elif kind == TOPK:
                    topk_layer(s, l)
                else:
                    choice_layer(s)
            if layers[-1][0] == TOPK:
                for c in range(BATCH):
                    combine(len(layers) - 1, layers[-1][1], c)
            else:
                dve.wait_ge(sem("dve_step"), counted["dve_step"])
                v.memset(red[:], 0.0).then_inc(sem("x_final"), 1)

        @block.scalar
        def _(act):
            a = nc.scalar

            def free(ins, key):
                ins.then_inc(bank_free[turn[key][0]], 1)

            def prep_xt(n):
                bank = full(act, ("xt", n))
                free(a.activation(XNT[:, chunk(n % BATCH)], bank[:], ACT.Copy), ("xt", n))

            act.wait_ge(sem("dist_ready"), 1)
            a.activation(gauss[:], gauss[:], ACT.Exp, scale=-1.0 / DEV_POW).then_inc(sem("gauss_ready"), 1)

            def window_layer(s, l):
                def exps(c):
                    act.wait_ge(sem(f"masked_ready{s}"), c + 1)
                    a.activation(sc[:, c % 2], sc[:, c % 2], ACT.Exp).then_inc(sem(f"wexp_ready{s}"), 1)

                def back(c):
                    bank = full(act, ("eT", s, c))
                    if c >= 2:
                        full(act, ("pre", s, c - 2))
                    free(a.activation(eT[:, c % 2, :], bank[0:KEYS, :], ACT.Copy), ("eT", s, c))
                    bank = full(act, ("pre", s, c))
                    if c:
                        act.wait_ge(sem(f"x_done{s}"), c)
                    ins = a.activation(th, bank[:], ACT.Tanh)
                    free(ins, ("pre", s, c))

                gated_next = layers[s + 1:s + 2] == [(GATED, 0)]
                ahead = layers[s + 1:s + 2] == [(TOPK, 3)]
                for i in range(BATCH + (3 if ahead else 1)):
                    c = i - 3
                    if ahead and c >= 0:
                        prep_xt(4 * (s + 1) + c)
                    if i < BATCH and (i or not s):
                        prep_xt(4 * s + i)
                    if gated_next and i == BATCH - 1:
                        prep_xt(4 * (s + 1))
                    if ahead and c >= 0:
                        route_exps(s + 1, c)
                    if i < BATCH:
                        exps(i)
                    if gated_next and i == BATCH - 1:
                        gate_exps(s + 1, 0)
                    if 1 <= i < BATCH + 1:
                        back(i - 1)

            def gate_exps(s, c):
                drained(act, ("lg", s, c))
                a.activation(s0[:], s0[:], ACT.Exp).then_inc(sem("rexp_ready"), 1)

            def gated_layer(s):
                def silu(c, i):
                    k = c * (PAIRS + 1) + i
                    bank = full(act, ("A", c, i))
                    if k >= 2:
                        drained(act, ("C", *divmod(k - 2, PAIRS + 1)))
                    b1 = small("b1_0")[:, i:i + 1] if i < PAIRS else small("sb1")
                    free(a.activation(S1[:, k % 2, :], bank[:], ACT.Silu, bias=b1), ("A", c, i))

                def leave(c):
                    bank = full(act, ("oT", c))
                    if c:
                        full(act, ("ob", c - 1))
                    free(a.activation(outT, bank[:], ACT.Identity, bias=small("sb2")), ("oT", c))

                for c in range(BATCH):
                    for i in range(PAIRS + 1):
                        if i == 1 and c:
                            leave(c - 1)
                        silu(c, i)
                        if c + 1 < BATCH:
                            if i == 5:
                                prep_xt(4 * s + c + 1)
                            if i == 6:
                                gate_exps(s, c + 1)
                        elif i == 12:
                            prep_xt(4 * (s + 1))
                        elif i == 13:
                            query(s + 1, layers[s + 1][1], 0)
                leave(BATCH - 1)

            def query(s, l, c):
                bank = full(act, ("q", s, c))
                free(a.activation(qT[:, c % 2, :], bank[:], ACT.Identity, bias=small(f"bq{l}")), ("q", s, c))

            def heads_layer(s, l):
                def heads_out(u):
                    bank = full(act, ("O", s, u))
                    if u:
                        full(act, ("Ot", s, u - 1))
                    free(a.activation(OTt, bank[:].rearrange("p (g q) -> p g q", g=4), ACT.Copy), ("O", s, u))

                def probsT(u):
                    if u >= 2:
                        full(act, ("O", s, u - 2))
                    for g in range(4):
                        bank = full(act, ("T", s, u, g))
                        free(a.activation(PT[:, u % 2, 4 * g:4 * g + 4, :],
                                          bank[0:KEYS, :].rearrange("p (h q) -> p h q", h=4), ACT.Copy),
                             ("T", s, u, g))

                def exps(u):
                    for b in range(3):
                        drained(act, ("S", s, u, b))
                    a.activation(PR[:, u % 2], PR[:, u % 2], ACT.Exp).then_inc(sem(f"exp_ready{s}"), 1)

                def headsT(u):
                    bank = full(act, ("OT", s, u))
                    if u:
                        full(act, ("Y", s, u - 1))
                    free(a.activation(OT, bank[:, 0:P], ACT.Copy), ("OT", s, u))

                ahead = layers[s + 1:s + 2] == [(TOPK, 1)]
                choice_next = layers[s + 1:s + 2] == [(CHOICE, 2)]
                if layers[s - 1][0] != GATED:
                    prep_xt(4 * s)
                    query(s, l, 0)
                for u in range(FINISH_AT[-1] + 1 if ahead else NT + 4):
                    if 2 <= u < NT + 2:
                        heads_out(u - 2)
                    if u < NT and u % TPC == 2 and u // TPC + 1 < BATCH:
                        prep_xt(4 * s + u // TPC + 1)
                        query(s, l, u // TPC + 1)
                    if 1 <= u < NT + 1:
                        probsT(u - 1)
                    if u < NT:
                        exps(u)
                    if 3 <= u < NT + 3:
                        headsT(u - 3)
                    if choice_next and u in CHOICE_TURN_AT:
                        prep_xt(4 * (s + 1) + CHOICE_TURN_AT.index(u))
                    if ahead and u in LOGITS_AT:
                        prep_xt(4 * (s + 1) + LOGITS_AT.index(u))
                    if ahead and u in SHIFT_AT:
                        route_exps(s + 1, SHIFT_AT.index(u))

            def route_exps(s, c):
                drained(act, ("rl", s, c))
                a.activation(pb8[:], pb8[:], ACT.Exp).then_inc(sem(f"rexp_ready{s}"), 1)

            def topk_layer(s, l):
                def rows_in(g):
                    bank = full(act, ("XB", s, g))
                    if g >= 4:
                        full(act, ("U", s, 4 * (g - 4) + 3))
                    if l == 1:
                        ins = a.activation(XBT[:, g % 4, :], bank[:], ACT.Copy)
                    else:
                        ins = a.activation(XBT[:, g % 4, :], bank[:], ACT.Identity, bias=small("lnb"),
                                           scale=small("lng"))
                    free(ins, ("XB", s, g))

                def hidden(b):
                    bank = full(act, ("U", s, b))
                    if b >= 2:
                        full(act, ("HT", s, b - 2))
                    free(a.activation(HS[:, b % 2, :], bank[:], ACT.Gelu if l == 1 else ACT.Copy), ("U", s, b))

                def results(g):
                    bank = full(act, ("Yd", s, g))
                    if g >= 2:
                        act.wait_ge(sem(f"rows_stored{s}_{g % 2}"), 16 * (g // 2))
                    n = min(4, BLOCKS[l] - 4 * g) * P
                    free(a.activation(YB[:, g % 2, 0:n], bank[:, 0:n], ACT.Copy), ("Yd", s, g))

                rows_in(0)
                for b in range(BLOCKS[l] + 3):
                    if b < BLOCKS[l]:
                        hidden(b)
                    if b % 4 == 1 and b // 4 + 1 < GROUPS_OF_BLOCKS[l]:
                        rows_in(b // 4 + 1)
                    if b >= 3 and (b - 3 == BLOCKS[l] - 1 or (b - 3) % 4 == 3):
                        results((b - 3) // 4)

            def choice_layer(s):
                def select(c):
                    for t in range(TPC):
                        bank = full(act, ("sel", c, t))
                        if c == 0 and t == 0 and s:
                            drained(act, ("Y", s - 1, NT - 1))
                        g = (TPC * c + t) * GPT
                        free(a.activation(SELT[:, g:g + GPT, :],
                                          bank[:].rearrange("p (g e) -> p g e", g=GPT), ACT.Copy), ("sel", c, t))

                for c in range(BATCH):
                    if len(CHOICE_TURN_AT) <= c + 1 < BATCH:
                        prep_xt(4 * s + c + 1)
                    select(c)

                def hidden(q):
                    bank = full(act, ("cu", q))
                    if q >= 2:
                        for h in range(2):
                            full(act, ("cd", q - 2, h))
                    for i in range(4):
                        ins = a.activation(INN[:, q % 2, i, :], bank[:, tile_(i)], ACT.Relu,
                                           bias=small("bias2")[:, 4 * q + i:4 * q + i + 1])
                        if i < 3:
                            ins.then_inc(sem("inner_part"), 1)
                    free(ins, ("cu", q))

                def leave(q):
                    bank = full(act, ("cd", q, 1))
                    free(a.activation(SELT[:, :, 8 * q + 1:8 * q + 8:2],
                                      bank[:].rearrange("p (i g) -> p g i", i=4), ACT.Copy), ("cd", q, 1))

                for q in range(ES // 8):
                    hidden(q)
                    if q:
                        leave(q - 1)
                leave(ES // 8 - 1)
                for c in range(BATCH):
                    if c >= 2:
                        full(act, ("co", c - 2))
                    for k in (0, 2):
                        bank = full(act, ("in", c, k))
                        free(a.activation(INTER[:, c % 2, k, :], bank[:], ACT.Copy), ("in", c, k))
                if s + 1 < len(layers):
                    prep_xt(4 * (s + 1))

            for s, (kind, l) in enumerate(layers):
                if kind == WINDOW_ATT:
                    window_layer(s, l)
                elif kind == GATED:
                    gated_layer(s)
                elif kind == HEADS_ATT:
                    heads_layer(s, l)
                elif kind == TOPK:
                    topk_layer(s, l)
                else:
                    choice_layer(s)

        @block.gpsimd
        def _(pool):
            g = nc.gpsimd
            counted = [0]

            def mark(ins):
                ins.then_inc(sem("pool_step"), 1)
                counted[0] += 1
                pool.wait_ge(sem("pool_step"), counted[0])

            powers = [0]

            def power():
                k = powers[0]
                powers[0] += 1
                pool.wait_ge(sem("var_ready"), k + 1)
                g.tensor_tensor(rstd[:, k % 2, :], veps[:, k % 2, :], neghalf[:], ALU.pow)\
                    .then_inc(sem("rstd_ready"), 1)

            g.iota(idx_i[:], [[1, KEYS]], base=0, channel_multiplier=0).then_inc(sem("iota_done"), 1)
            g.iota(pidx_i[:], [[0, 1]], base=0, channel_multiplier=1).then_inc(sem("iota_done"), 1)
            g.iota(desc_i[:], [[-1, E1]], base=E1, channel_multiplier=0).then_inc(sem("iota_done"), 1)
            g.iota(tie_i[:], [[1, GRP]], base=0, channel_multiplier=0).then_inc(sem("iota_done"), 1)
            g.iota(step_i[:], [[P, 32]], base=0, channel_multiplier=0).then_inc(sem("iota_done"), 1)
            g.iota(bidx_i[:], [[1, 40]], base=0, channel_multiplier=0).then_inc(sem("iota_done"), 1)
            g.iota(region_i[:], [[REGION, E1]], base=-1, channel_multiplier=0).then_inc(sem("iota_done"), 1)
            g.memset(ident[:], 0.0).then_inc(sem("ident_ready"), 1)
            pool.wait_ge(sem("ident_ready"), 1)
            g.affine_select(out=ident[:], in_=ident[:], compare_op=ALU.not_equal, fill=1.0, base=0,
                            pattern=[[-1, P]], channel_multiplier=1).then_inc(sem("ident_ready"), 1)
            pool.wait_ge(sem("neghalf_ready"), 1)
            power()
            for m, w, n in ((headmask, DK, HEADS), (gmask, GRP, GPT)):
                mark(g.memset(m[:], 1.0))
                mark(g.affine_select(out=m[:], in_=m[:], compare_op=ALU.is_ge, fill=0.0, base=0,
                                     pattern=[[-w, n]], channel_multiplier=1))
                mark(g.affine_select(out=m[:], in_=m[:], compare_op=ALU.is_ge, fill=0.0, base=w - 1,
                                     pattern=[[w, n]], channel_multiplier=-1))
            mark(g.memset(tri[:], 1.0))
            mark(g.affine_select(out=tri[:], in_=tri[:], compare_op=ALU.is_ge, fill=0.0, base=0,
                                 pattern=[[1, P]], channel_multiplier=-1))
            mark(g.memset(lt8[:], 1.0))
            mark(g.affine_select(out=lt8[:], in_=lt8[:], compare_op=ALU.is_gt, fill=0.0, base=0,
                                 pattern=[[1, E1], [-1, E1]], channel_multiplier=0))
            g.memset(zeros, 0.0).then_inc(sem("zeros_ready"), 1)
            mark(g.memset(parity[:], 1.0))
            mark(g.memset(parity[0:ES, 1, :], 0.0))
            mark(g.memset(parity[ES:P, 0, :], 0.0))
            mark(g.memset(pairsel[:], 0.0))
            for k in range(3):
                m = pairsel[32 * k:32 * k + 32, :, :].rearrange("p i (h f) -> p i h f", h=2)
                mark(g.affine_select(out=m, in_=m, compare_op=ALU.not_equal, fill=1.0, base=0,
                                     pattern=[[-2, PAIRS], [-1, 2], [0, F0]], channel_multiplier=1))
            mark(g.memset(vpad[:], 0.0))
            mark(g.memset(vpad[:, :, :, DK:DK + 1], 1.0))
            g.memset(cwm[:], 0.0).then_inc(sem("pool_consts"), 1)

            def operands(s, l, c):
                if c >= 2:
                    full(pool, ("S", s, TPC * (c - 2) + TPC - 1, 2))
                    full(pool, ("O", s, TPC * (c - 2) + TPC - 1))
                g.tensor_copy(vpad[:, c % 2, :, 0:DK], Vc[l][:, c, :].rearrange("p (h d) -> p h d", h=HEADS))\
                    .then_inc(sem("vpad_ready"), 1)
                g.tensor_tensor(kbd[:, c % 2], KT[l][:, c * KEYS:(c + 1) * KEYS].unsqueeze(1)
                                .to_broadcast([P, HEADS, KEYS]),
                                headmask[:].unsqueeze(2).to_broadcast([P, HEADS, KEYS]), ALU.mult)\
                    .then_inc(sem("kbd_ready"), 1)

            def first_operands(s, l):
                drained(pool, ("KT", l))
                drained(pool, ("Vc", l))
                operands(s, l, 0)
                operands(s, l, 1)

            def gather(s, l, c):
                nk = CHOICES[l]
                for j in range(TPC * nk * c, TPC * nk * (c + 1)):
                    t, k = divmod(j, nk)
                    if j >= RING:
                        pool.wait_ge(sem(f"combined{s}"), j - RING + 1)
                    g.indirect_dma_start(YG[:, j % RING, :], None, ys[0:BLOCKS[l] * P, :],
                                         bass.IndirectOffsetOnAxis(ap=slots[:, t, k:k + 1].bitcast(u32), axis=0))\
                        .then_inc(sem(f"gathered{s}_{j % RING}"), 16)

            def scatter(s, l, c):
                nk = CHOICES[l]
                pool.wait_ge(sem(f"slots_in_ready{s}"), c + 1)
                if c == 0:
                    pool.wait_ge(sem("zero_stored"), 16)
                for j in range(TPC * nk):
                    t, k = divmod(j, nk)
                    src = XN[:, (4 * s + c) % 2, t, :] if l == 1 else XA[:, 4 * c + t, :]
                    row = slots_in[:, 4 * c + t, k:k + 1].bitcast(u32)
                    g.indirect_dma_start(xs[0:E1 * REGION, :], bass.IndirectOffsetOnAxis(ap=row, axis=0),
                                         src, None).then_inc(sem(f"scattered{s}_{c}"), 16)

            for s, (kind, l) in enumerate(layers):
                after_topk = s > 0 and layers[s - 1][0] == TOPK
                if kind == HEADS_ATT:
                    if after_topk:
                        gather(s - 1, layers[s - 1][1], 0)
                    power()
                    if not after_topk:
                        first_operands(s, l)
                    for c in range(1, BATCH):
                        if after_topk:
                            gather(s - 1, layers[s - 1][1], c)
                        power()
                        if c >= 2:
                            operands(s, l, c)
                elif kind != TOPK:
                    for _k in range(BATCH - (s == 0)):
                        power()
                else:
                    for c in range(BATCH + 1):
                        if c < BATCH:
                            for _k in range(2 if l == 3 else 1):
                                power()
                        if c:
                            scatter(s, l, c - 1)
                    if s + 1 < len(layers):
                        first_operands(s + 1, layers[s + 1][1])
                    pool.wait_ge(sem(f"slots_ready{s}"), CHOICES[l])
                    for h in range(2):
                        pool.wait_ge(sem(f"rows_stored{s}_{h}"), 16 * ((GROUPS_OF_BLOCKS[l] + 1 - h) // 2))
                    if s == len(layers) - 1:
                        for c in range(BATCH):
                            gather(s, l, c)

        @block.sync
        def _(sp):
            sp.dma_start(X[:, 0:4, :], x_in[:, 0:4, :]).then_inc(sem("x_loaded0"), 16)
            sp.dma_start(SM[:], small_in).then_inc(sem("small_loaded"), 16)
            sp.dma_start(lens_i[:], lens_in).then_inc(sem("lens_loaded"), 16)
            for c in range(1, BATCH):
                sp.dma_start(X[:, 4 * c:4 * c + 4, :], x_in[:, 4 * c:4 * c + 4, :]).then_inc(sem(f"x_loaded{c}"), 16)
            sp.dma_start(SLOT[0][:], w13_in).then_inc(sem("w13_loaded"), 16)
            sp.dma_start(SLOT[1][:, 0:2048], w2_in).then_inc(sem("w2_loaded"), 16)
            sp.dma_start(SLOT[2][:], l1w1_in).then_inc(sem("up_loaded1"), 16)
            sp.dma_start(SLOT[3][:], l1w2_in).then_inc(sem("down_loaded1"), 16)
            if len(layers) > 2:
                sp.wait_ge(sem("zeros_ready"), 1)
                sp.dma_start(xs_wide, zeros.unsqueeze(1).to_broadcast([P, E1 * REGION // (8 * P), 8 * P]))\
                    .then_inc(sem("zero_stored"), 16)

            def move_rows(s, l):
                n_groups = GROUPS_OF_BLOCKS[l]

                def first_row(g, j):
                    return sp.value_load(block_row[0:1, 4 * g + j:4 * g + j + 1], min_val=0,
                                         max_val=E1 * REGION - P)

                def load(g):
                    if g >= 4:
                        full(sp, ("XB", s, g - 4))
                    for j in range(4):
                        row = first_row(g, j) if g else first_rows[j]
                        sp.dma_start(XB[:, g % 4, j, :], xs[bass.ds(row, P), :])\
                            .then_inc(sem(f"rows_loaded{s}_{g}"), 16)

                sp.wait_ge(sem(f"block_rows_ready{s}"), 1)
                first_rows = [first_row(0, j) for j in range(4)]
                for c in range(BATCH):
                    sp.wait_ge(sem(f"scattered{s}_{c}"), 16 * TPC * CHOICES[l])
                for g in range(min(4, n_groups)):
                    load(g)
                for g in range(n_groups):
                    n = min(4, BLOCKS[l] - 4 * g)
                    drained(sp, ("Yd", s, g))
                    sp.dma_start(ys_blocks[:, 4 * g:4 * g + n, :],
                                 YB[:, g % 2, 0:n * P].rearrange("p (b d) -> p b d", d=D))\
                        .then_inc(sem(f"rows_stored{s}_{g % 2}"), 16)
                    if g + 4 < n_groups:
                        load(g + 4)

            if len(layers) > 5:
                full(sp, ("oT", BATCH - 1))
                sp.dma_start(SLOT[0][:], f1_in).then_inc(sem("f1_loaded"), 16)
                sp.dma_start(SLOT[1][:], f2_in).then_inc(sem("f2_loaded"), 16)
            if len(layers) > 3:
                move_rows(3, 1)
            if len(layers) > 7:
                sp.dma_start(SLOT[2][:], l3w1_in).then_inc(sem("up_loaded3"), 16)
                sp.dma_start(SLOT[3][:], l3w2_in).then_inc(sem("down_loaded3"), 16)
                full(sp, ("cd", ES // 8 - 1, 1))
                sp.dma_start(b2row, b2row_in).then_inc(sem("b2row_loaded"), 16)
                move_rows(7, 3)
            last = len(layers) - 1
            for c in range(BATCH):
                if layers[last][0] == TOPK:
                    sp.wait_ge(sem(f"combined{last}"), TPC * CHOICES[layers[last][1]] * (c + 1))
                else:
                    sp.wait_ge(sem("x_final"), 1)
                sp.dma_start(out[:, 4 * c:4 * c + 4, :], X[:, 4 * c:4 * c + 4, :]).then_inc(sem("stored"), 16)
            sp.wait_ge(sem("stored"), 16 * BATCH)


def layout(a):
    def pack(name):
        _, r, c = OFFSET[name]
        src = small_sources[name]()
        return np.broadcast_to(src, (r, c))

    def t(n):
        return a[n].T

    small_sources = {
        "ctxT": lambda: a["ctx_1024"].transpose(2, 0, 1).reshape(P, BK),
        "pt": lambda: a["condB_pt"][None, :], "tau": lambda: a["condB_tau"][None, :],
        "delta": lambda: a["fside_BxS2_0"].reshape(1, BK),
        "gw": lambda: a["L0_ffn_gw"], "gb": lambda: a["L0_ffn_gb"][None, :],
        "b1_0": lambda: a["L0_ffn_b1"].reshape(PAIRS, P).T, "b3_0": lambda: a["L0_ffn_b3"].reshape(PAIRS, P).T,
        "b2_0": lambda: a["L0_ffn_b2"], "sw1": lambda: a["L0_ffn_sw1"], "sw3": lambda: a["L0_ffn_sw3"],
        "sw2": lambda: a["L0_ffn_sw2"], "sb1": lambda: a["L0_ffn_sb1"][:, None],
        "sb3": lambda: a["L0_ffn_sb3"][:, None], "sb2": lambda: a["L0_ffn_sb2"][:, None],
        "rwT": lambda: t("L1_ffn_router_w"),
        "ctrl": lambda: np.concatenate([a["L2_ffn_controller"].reshape(D, ES)] * 2, axis=1),
        "bias2": lambda: a["L2_ffn_bias"].reshape(ES // 2, P).T,
        "wr": lambda: a["L3_ffn_Wr"], "br": lambda: a["L3_ffn_br"][None, :],
        "b1_3": lambda: a["L3_ffn_b1"].reshape(E1 * FC, P).T, 
        "lng": lambda: a["L3_ffn_ln_g"][:, None], "lnb": lambda: a["L3_ffn_ln_b"][:, None],
    }
    for l in (0, 3):
        small_sources[f"waT{l}"] = lambda l=l: t(f"L{l}_xcond_W_a")
        small_sources[f"wcT{l}"] = lambda l=l: np.concatenate(
            [t(f"L{l}_xcond_W_c")[0:P], t(f"L{l}_xcond_W_c")[P:2 * P]], axis=1)
    for l in (1, 2):
        for n in "qkvo":
            small_sources[f"w{n}T{l}"] = lambda l=l, n=n: t(f"L{l}_xcond_W{n}")
        for n in "qk":
            small_sources[f"b{n}{l}"] = lambda l=l, n=n: a[f"L{l}_xcond_b{n}"][:, None]
        for n in "vo":
            small_sources[f"b{n}{l}"] = lambda l=l, n=n: a[f"L{l}_xcond_b{n}"][None, :]
    smalls = np.zeros((P, SMALL_COLS), np.float32)
    for name, r, c in SMALL:
        at = OFFSET[name][0]
        smalls[0:r, at:at + c] = pack(name)

    def up(w):
        return w.transpose(1, 0, 2).reshape(P, -1)

    def down(w):
        return w.reshape(-1, P, D).transpose(1, 0, 2).reshape(P, -1)

    return {
        "x": a["x"].reshape(NT, P, D).transpose(1, 0, 2),
        "small": smalls,
        "lens": np.broadcast_to(a["_lenS2"][None, :], (P, BATCH)),
        "w13": np.concatenate([up(a["L0_ffn_w1"]), up(a["L0_ffn_w3"])], axis=1),
        "w2": down(a["L0_ffn_w2"]),
        "l1w1": up(a["L1_ffn_w1"]), "l1w2": down(a["L1_ffn_w2"]),
        "f1": a["L2_ffn_f1"].reshape(D, ES * FS), "f2": down(a["L2_ffn_f2"]),
        "l3w1": up(a["L3_ffn_W1"]), "l3w2": down(a["L3_ffn_W2"]),
        "b2row": a["L3_ffn_b2"].reshape(1, E1 * D),
    }


def kernel(**inputs):
    import concourse.bacc as bacc
    from concourse.bass_utils import run_bass_kernel_spmd

    arrays = {n: np.ascontiguousarray(v) for n, v in layout({n: np.asarray(v) for n, v in inputs.items()}).items()}
    nc = bacc.Bacc("TRN2", target_bir_lowering=False, num_devices=1)
    args = [nc.dram_tensor(n, v.shape, mybir.dt.from_np(v.dtype), kind="ExternalInput").ap()
            for n, v in arrays.items()]
    args.append(nc.dram_tensor("y", (P, NT, D), mybir.dt.float32, kind="ExternalOutput").ap())
    build(nc, *args)
    result = run_bass_kernel_spmd(nc, [arrays], core_ids=[0])
    return result.results[0]["y"].transpose(1, 0, 2).reshape(BATCH, SEQ, D)
```
